# Optimizing a Trainium2 kernel written in Bass

```python
import numpy as np
import jax
import jax.numpy as jnp

def _softmax(x, axis=-1):
    return jax.nn.softmax(x, axis=axis)

def _gelu(x):
    return jax.nn.gelu(x, approximate=True)

def _silu(x):
    return jax.nn.silu(x)

def _sigmoid(x):
    return jax.nn.sigmoid(x)

def _layernorm(x, axis=-1, eps=1e-05):
    m = jnp.mean(x, axis=axis, keepdims=True)
    v = jnp.var(x, axis=axis, keepdims=True)
    return (x - m) / jnp.sqrt(v + eps)

def _scatter_add(tgt, idx, src, axis=0):
    return tgt.at[idx].add(src)

def _segment_sum(src, seg, n):
    return jax.ops.segment_sum(src, seg, n)
kernel_name = 'mk_gnn_resnorm_d4_gnn_r64_f63da3'

def setup_inputs(seed: int=0):
    np.random.seed(seed)
    _w = jnp.asarray

    def _rec_inputs():
        import jax
        import jax.numpy as jnp
        _gk = jax.random.key(seed)
        x = -0.0003713 + 1 * jax.random.normal(jax.random.fold_in(_gk, 1), (50000, 128), jnp.float32)
        src = jax.random.randint(jax.random.fold_in(_gk, 2), (25000,), 0, 50000, jnp.int32)
        dst = jnp.minimum((50000 * jax.random.uniform(jax.random.fold_in(_gk, 3), (25000,)) ** 2.0).astype(jnp.int32), 49999)
        _o = jnp.argsort(dst, stable=True)
        src = src[_o]
        dst = dst[_o]
        edge_attr_64 = -5.16925e-05 + 1.00005 * jax.random.normal(jax.random.fold_in(_gk, 12), (25000, 64), jnp.float32)
        edge_weight = jax.random.uniform(jax.random.fold_in(_gk, 14), (25000,), jnp.float32, 0.0, 0.999999)
        return (x, src, dst, edge_attr_64, edge_weight)
    x, src, dst, edge_attr_64, edge_weight = _rec_inputs()

    def _L0_gnn_setup():
        import jax, jax.numpy as jnp
        import numpy as np
        N_NODES = 100000
        N_EDGES = 25000
        D_NODE = 128
        D_EDGE = 64
        HID = 128
        HEADS = 4
        N_LAYERS = 3
        LN_EPS = 1e-05
        NEG_SLOPE = 0.2

        def _layer_norm(x, g, b):
            mu = x.mean(-1, keepdims=True)
            var = ((x - mu) ** 2).mean(-1, keepdims=True)
            return (x - mu) * jax.lax.rsqrt(var + LN_EPS) * g + b

        def _gat(x, src, dst, ew, Wg, att_s, att_d, bias, n):
            h = (x @ Wg).reshape(n, HEADS, HID)
            a_s = jnp.einsum('nhc,hc->nh', h, att_s)
            a_d = jnp.einsum('nhc,hc->nh', h, att_d)
            logits = jax.nn.leaky_relu(a_s[src] + a_d[dst] + ew[:, None], NEG_SLOPE)
            m = jax.ops.segment_max(logits, dst, num_segments=n)
            ex = jnp.exp(logits - m[dst])
            denom = jax.ops.segment_sum(ex, dst, num_segments=n)
            alpha = ex / denom[dst]
            outs = []
            for hd in range(HEADS):
                msg = alpha[:, hd:hd + 1] * h[src, hd, :]
                outs.append(jax.ops.segment_sum(msg, dst, num_segments=n))
            return jnp.stack(outs, 1).mean(1) + bias
        key = jax.random.key(seed)
        ks = jax.random.split(key, 16)
        s = 0.05
        inp = {'node_features': jax.random.normal(ks[0], (N_NODES, D_NODE), jnp.float32), 'edge_index': jax.random.randint(ks[1], (2, N_EDGES), 0, N_NODES, jnp.int32), 'edge_attr': jax.random.normal(ks[2], (N_EDGES, D_EDGE), jnp.float32), 'W0': jax.random.normal(ks[3], (D_NODE, HID), jnp.float32) * s, 'b0': jnp.zeros((HID,), jnp.float32), 'We': jax.random.normal(ks[4], (N_LAYERS, D_EDGE, HID), jnp.float32) * s, 'be': jnp.zeros((N_LAYERS, HID), jnp.float32), 'Wg': jax.random.normal(ks[5], (N_LAYERS, HID, HEADS * HID), jnp.float32) * s, 'att_src': jax.random.normal(ks[6], (N_LAYERS, HEADS, HID), jnp.float32) * s, 'att_dst': jax.random.normal(ks[7], (N_LAYERS, HEADS, HID), jnp.float32) * s, 'bg': jnp.zeros((N_LAYERS, HID), jnp.float32), 'gamma': jnp.ones((N_LAYERS, HID), jnp.float32), 'beta': jnp.zeros((N_LAYERS, HID), jnp.float32)}
        return inp
    _L0_gnn_all = _L0_gnn_setup()
    _L0_gnn_in = {k: v for k, v in _L0_gnn_all.items() if k in ('W0', 'b0', 'We', 'be', 'Wg', 'att_src', 'att_dst', 'bg', 'gamma', 'beta')}
    del _L0_gnn_all

    def _L1_gnn_setup():
        import jax, jax.numpy as jnp
        import numpy as np
        N_NODES = 100000
        N_EDGES = 25000
        DIM = 128

        def _gcn_norm(edge_index, edge_weight, num_nodes, dtype):
            loop = jnp.arange(num_nodes, dtype=edge_index.dtype)
            row = jnp.concatenate([edge_index[0], loop])
            col = jnp.concatenate([edge_index[1], loop])
            w = jnp.concatenate([edge_weight, jnp.ones((num_nodes,), dtype=dtype)])
            deg = jax.ops.segment_sum(w, col, num_segments=num_nodes)
            dis = jnp.where(deg > 0, jax.lax.rsqrt(jnp.where(deg > 0, deg, 1.0)), 0.0)
            norm = dis[row] * w * dis[col]
            return (row, col, norm)
        key = jax.random.key(seed)
        ks = jax.random.split(key, 6)
        x = jax.random.normal(ks[0], (N_NODES, DIM), dtype=jnp.float32)
        edge_index = jax.random.randint(ks[1], (2, N_EDGES), 0, N_NODES, dtype=jnp.int64)
        edge_weight = jax.random.uniform(ks[2], (N_EDGES,), dtype=jnp.float32)
        s = 1.0 / np.sqrt(DIM)
        W1 = jax.random.normal(ks[3], (DIM, DIM), dtype=jnp.float32) * s
        b1 = jnp.zeros((DIM,), dtype=jnp.float32)
        W2 = jax.random.normal(ks[4], (DIM, DIM), dtype=jnp.float32) * s
        b2 = jnp.zeros((DIM,), dtype=jnp.float32)
        return {'x': x, 'edge_index': edge_index, 'edge_weight': edge_weight, 'W1': W1, 'b1': b1, 'W2': W2, 'b2': b2}
    _L1_gnn_all = _L1_gnn_setup()
    _L1_gnn_in = {k: v for k, v in _L1_gnn_all.items() if k in ('W1', 'b1', 'W2', 'b2')}
    del _L1_gnn_all

    def _L2_gnn_setup():
        import jax, jax.numpy as jnp
        import numpy as np
        N_NODES = 100000
        N_EDGES = 25000
        IN_CH = 128
        OUT_CH = 128

        def gcn_conv(x, edge_index, W, b):
            n = x.shape[0]
            loops = jnp.arange(n, dtype=edge_index.dtype)
            row = jnp.concatenate([edge_index[0], loops])
            col = jnp.concatenate([edge_index[1], loops])
            deg = jax.ops.segment_sum(jnp.ones_like(col, dtype=x.dtype), col, num_segments=n)
            dis = jnp.where(deg > 0, jax.lax.rsqrt(jnp.maximum(deg, 1e-12)), 0.0)
            norm = dis[row] * dis[col]
            xw = x @ W
            msgs = xw[row] * norm[:, None]
            out = jax.ops.segment_sum(msgs, col, num_segments=n)
            return out + b
        key = jax.random.key(seed)
        k1, k2, k3 = jax.random.split(key, 3)
        x = jax.random.normal(k1, (N_NODES, IN_CH), dtype=jnp.float32)
        edge_index = jax.random.randint(k2, (2, N_EDGES), 0, N_NODES, dtype=jnp.int64)
        W = jax.random.normal(k3, (IN_CH, OUT_CH), dtype=jnp.float32) * (1.0 / np.sqrt(IN_CH))
        b = jnp.zeros((OUT_CH,), dtype=jnp.float32)
        return {'x': x, 'edge_index': edge_index, 'W': W, 'b': b}
    _L2_gnn_all = _L2_gnn_setup()
    _L2_gnn_in = {k: v for k, v in _L2_gnn_all.items() if k in ('W', 'b')}
    del _L2_gnn_all

    def _L3_gnn_setup():
        import jax, jax.numpy as jnp
        import numpy as np
        N_NODES = 50000
        N_EDGES = 12500
        ENC_DIM = 128

        def _sage_layer(h, edge_src, edge_dst, W, b):
            n = h.shape[0]
            msg_sum = jax.ops.segment_sum(h[edge_src], edge_dst, num_segments=n)
            deg = jax.ops.segment_sum(jnp.ones_like(edge_dst, dtype=h.dtype), edge_dst, num_segments=n)
            m = msg_sum / jnp.maximum(deg, 1.0)[:, None]
            hc = jnp.concatenate([h, m], axis=1)
            return jax.nn.relu(hc @ W + b)
        key = jax.random.key(seed)
        k_h, k_s, k_d, k_w1, k_w2 = jax.random.split(key, 5)
        h = jax.random.normal(k_h, (N_NODES, ENC_DIM), dtype=jnp.float32)
        edge_src = jax.random.randint(k_s, (N_EDGES,), 0, N_NODES, dtype=jnp.int32)
        edge_dst = jax.random.randint(k_d, (N_EDGES,), 0, N_NODES, dtype=jnp.int32)
        scale = 1.0 / np.sqrt(2 * ENC_DIM)
        W1 = jax.random.normal(k_w1, (2 * ENC_DIM, ENC_DIM), dtype=jnp.float32) * scale
        b1 = jnp.zeros((ENC_DIM,), dtype=jnp.float32)
        W2 = jax.random.normal(k_w2, (2 * ENC_DIM, ENC_DIM), dtype=jnp.float32) * scale
        b2 = jnp.zeros((ENC_DIM,), dtype=jnp.float32)
        return {'h': h, 'edge_src': edge_src, 'edge_dst': edge_dst, 'W1': W1, 'b1': b1, 'W2': W2, 'b2': b2}
    _L3_gnn_all = _L3_gnn_setup()
    _L3_gnn_in = {k: v for k, v in _L3_gnn_all.items() if k in ('W1', 'b1', 'W2', 'b2')}
    del _L3_gnn_all
    return {'x': x, 'src': src, 'dst': dst, 'edge_attr_64': edge_attr_64, 'edge_weight': edge_weight, 'L0_gnn_W0': _L0_gnn_in['W0'], 'L0_gnn_b0': _L0_gnn_in['b0'], 'L0_gnn_We': _L0_gnn_in['We'], 'L0_gnn_be': _L0_gnn_in['be'], 'L0_gnn_Wg': _L0_gnn_in['Wg'], 'L0_gnn_att_src': _L0_gnn_in['att_src'], 'L0_gnn_att_dst': _L0_gnn_in['att_dst'], 'L0_gnn_bg': _L0_gnn_in['bg'], 'L0_gnn_gamma': _L0_gnn_in['gamma'], 'L0_gnn_beta': _L0_gnn_in['beta'], 'L1_gnn_W1': _L1_gnn_in['W1'], 'L1_gnn_b1': _L1_gnn_in['b1'], 'L1_gnn_W2': _L1_gnn_in['W2'], 'L1_gnn_b2': _L1_gnn_in['b2'], 'L2_gnn_W': _L2_gnn_in['W'], 'L2_gnn_b': _L2_gnn_in['b'], 'L3_gnn_W1': _L3_gnn_in['W1'], 'L3_gnn_b1': _L3_gnn_in['b1'], 'L3_gnn_W2': _L3_gnn_in['W2'], 'L3_gnn_b2': _L3_gnn_in['b2']}

def reference(x, src, dst, edge_attr_64, edge_weight, L0_gnn_W0, L0_gnn_b0, L0_gnn_We, L0_gnn_be, L0_gnn_Wg, L0_gnn_att_src, L0_gnn_att_dst, L0_gnn_bg, L0_gnn_gamma, L0_gnn_beta, L1_gnn_W1, L1_gnn_b1, L1_gnn_W2, L1_gnn_b2, L2_gnn_W, L2_gnn_b, L3_gnn_W1, L3_gnn_b1, L3_gnn_W2, L3_gnn_b2):
    import jax
    import jax.numpy as jnp

    def _L0_gnn_ref(node_features, edge_index, edge_attr, W0, b0, We, be, Wg, att_src, att_dst, bg, gamma, beta):
        import jax, jax.numpy as jnp
        import numpy as np
        N_NODES = 100000
        N_EDGES = 25000
        D_NODE = 128
        D_EDGE = 64
        HID = 128
        HEADS = 4
        N_LAYERS = 3
        LN_EPS = 1e-05
        NEG_SLOPE = 0.2

        def _layer_norm(x, g, b):
            mu = x.mean(-1, keepdims=True)
            var = ((x - mu) ** 2).mean(-1, keepdims=True)
            return (x - mu) * jax.lax.rsqrt(var + LN_EPS) * g + b

        def _gat(x, src, dst, ew, Wg, att_s, att_d, bias, n):
            h = (x @ Wg).reshape(n, HEADS, HID)
            a_s = jnp.einsum('nhc,hc->nh', h, att_s)
            a_d = jnp.einsum('nhc,hc->nh', h, att_d)
            logits = jax.nn.leaky_relu(a_s[src] + a_d[dst] + ew[:, None], NEG_SLOPE)
            m = jax.ops.segment_max(logits, dst, num_segments=n)
            ex = jnp.exp(logits - m[dst])
            denom = jax.ops.segment_sum(ex, dst, num_segments=n)
            alpha = ex / denom[dst]
            outs = []
            for hd in range(HEADS):
                msg = alpha[:, hd:hd + 1] * h[src, hd, :]
                outs.append(jax.ops.segment_sum(msg, dst, num_segments=n))
            return jnp.stack(outs, 1).mean(1) + bias
        n = node_features.shape[0]
        src, dst = (edge_index[0], edge_index[1])
        loop = jnp.arange(n, dtype=src.dtype)
        src_f = jnp.concatenate([src, loop])
        dst_f = jnp.concatenate([dst, loop])
        x = jax.nn.relu(node_features @ W0 + b0)
        for l in range(N_LAYERS):
            ew = (edge_attr @ We[l] + be[l]).mean(-1)
            ew_f = jnp.concatenate([ew, jnp.full((n,), ew.mean(), ew.dtype)])
            y = _gat(x, src_f, dst_f, ew_f, Wg[l], att_src[l], att_dst[l], bg[l], n)
            y = _layer_norm(y, gamma[l], beta[l])
            x = jax.nn.relu(x + y)
        return x

    def _L1_gnn_ref(x, edge_index, edge_weight, W1, b1, W2, b2):
        import jax, jax.numpy as jnp
        import numpy as np
        N_NODES = 100000
        N_EDGES = 25000
        DIM = 128

        def _gcn_norm(edge_index, edge_weight, num_nodes, dtype):
            loop = jnp.arange(num_nodes, dtype=edge_index.dtype)
            row = jnp.concatenate([edge_index[0], loop])
            col = jnp.concatenate([edge_index[1], loop])
            w = jnp.concatenate([edge_weight, jnp.ones((num_nodes,), dtype=dtype)])
            deg = jax.ops.segment_sum(w, col, num_segments=num_nodes)
            dis = jnp.where(deg > 0, jax.lax.rsqrt(jnp.where(deg > 0, deg, 1.0)), 0.0)
            norm = dis[row] * w * dis[col]
            return (row, col, norm)
        num_nodes = x.shape[0]
        row, col, norm = _gcn_norm(edge_index, edge_weight, num_nodes, x.dtype)

        def sgconv_relu(h, W, b):
            msg = h[row] * norm[:, None]
            agg = jax.ops.segment_sum(msg, col, num_segments=num_nodes)
            return jax.nn.relu(agg @ W.T + b)
        h = sgconv_relu(x, W1, b1)
        h = sgconv_relu(h, W2, b2)
        return h

    def _L2_gnn_ref(x, edge_index, W, b):
        import jax, jax.numpy as jnp
        import numpy as np
        N_NODES = 100000
        N_EDGES = 25000
        IN_CH = 128
        OUT_CH = 128

        def gcn_conv(x, edge_index, W, b):
            n = x.shape[0]
            loops = jnp.arange(n, dtype=edge_index.dtype)
            row = jnp.concatenate([edge_index[0], loops])
            col = jnp.concatenate([edge_index[1], loops])
            deg = jax.ops.segment_sum(jnp.ones_like(col, dtype=x.dtype), col, num_segments=n)
            dis = jnp.where(deg > 0, jax.lax.rsqrt(jnp.maximum(deg, 1e-12)), 0.0)
            norm = dis[row] * dis[col]
            xw = x @ W
            msgs = xw[row] * norm[:, None]
            out = jax.ops.segment_sum(msgs, col, num_segments=n)
            return out + b
        return jax.nn.relu(gcn_conv(x, edge_index, W, b))

    def _L3_gnn_ref(h, edge_src, edge_dst, W1, b1, W2, b2):
        import jax, jax.numpy as jnp
        import numpy as np
        N_NODES = 50000
        N_EDGES = 12500
        ENC_DIM = 128

        def _sage_layer(h, edge_src, edge_dst, W, b):
            n = h.shape[0]
            msg_sum = jax.ops.segment_sum(h[edge_src], edge_dst, num_segments=n)
            deg = jax.ops.segment_sum(jnp.ones_like(edge_dst, dtype=h.dtype), edge_dst, num_segments=n)
            m = msg_sum / jnp.maximum(deg, 1.0)[:, None]
            hc = jnp.concatenate([h, m], axis=1)
            return jax.nn.relu(hc @ W + b)
        h = _sage_layer(h, edge_src, edge_dst, W1, b1)
        h = _sage_layer(h, edge_src, edge_dst, W2, b2)
        return h
    edge_index = jnp.stack([src, dst])
    x = _layernorm(x + _L0_gnn_ref(x, edge_index, edge_attr_64, L0_gnn_W0, L0_gnn_b0, L0_gnn_We, L0_gnn_be, L0_gnn_Wg, L0_gnn_att_src, L0_gnn_att_dst, L0_gnn_bg, L0_gnn_gamma, L0_gnn_beta), axis=-1)
    x = _layernorm(x + _L1_gnn_ref(x, edge_index, edge_weight, L1_gnn_W1, L1_gnn_b1, L1_gnn_W2, L1_gnn_b2), axis=-1)
    x = _layernorm(x + _L2_gnn_ref(x, edge_index, L2_gnn_W, L2_gnn_b), axis=-1)
    x = _layernorm(x + _L3_gnn_ref(x, src, dst, L3_gnn_W1, L3_gnn_b1, L3_gnn_W2, L3_gnn_b2), axis=-1)
    return x

_drawn_inputs = setup_inputs


def setup_inputs(seed=0):
    import zlib

    import numpy as np

    out = dict(_drawn_inputs(seed))
    spreads = {'L0_gnn_b0': (0.0, 0.1),
     'L0_gnn_be': (0.0, 0.8),
     'L0_gnn_bg': (0.0, 0.1),
     'L0_gnn_gamma': (1.0, 0.2),
     'L0_gnn_beta': (0.0, 0.1),
     'L1_gnn_b1': (0.0, 0.1),
     'L1_gnn_b2': (0.0, 0.1),
     'L2_gnn_b': (0.0, 0.1),
     'L3_gnn_b1': (0.0, 0.1),
     'L3_gnn_b2': (0.0, 0.1)}
    factors = {'edge_attr_64': 8.0, 'L0_gnn_We': 8.0, 'L0_gnn_att_src': 6.964, 'L0_gnn_att_dst': 8.0}
    for name, (base, spread) in spreads.items():
        noise = np.random.default_rng([zlib.crc32(name.encode()), seed]).standard_normal(out[name].shape)
        drawn = base * np.exp(spread * noise) if base else spread * noise
        out[name] = jnp.asarray(drawn.astype(out[name].dtype))
    for name, factor in factors.items():
        out[name] = (out[name] * factor).astype(out[name].dtype)
    return out
```

```python
from contextlib import ExitStack

import numpy as np
import concourse.bass as bass
from concourse import mybir

F32 = mybir.dt.float32
I32 = mybir.dt.int32
ALU = mybir.AluOpType
ACT = mybir.ActivationFunctionType
AX = mybir.AxisListType

P = 128
D = 128
DE = 64
HEADS = 4
GB = 4
BIG = 1.0e6
FAR = 1.0e30
EPS = 1e-5
SLOPE = 0.2
ROW = 256


def sizes(n_nodes, n_edges):
    nb = max(-(-n_edges // (P * GB)), -(-n_nodes // (2 * P * GB)))
    nb += nb % 2
    return nb, nb * GB * P, 2 * nb * GB * P


class Turn:

    def __init__(self, i, half, span=2):
        self.i, self.half, self.span = i, half, span

    def count(self, k, n):
        return self.i * (self.span * k) + (self.half * k + n)

    def batch(self):
        return self.i * self.span + self.half


class Chain:

    def __init__(self, eng, sem, per_turn=0):
        self.eng, self.sem, self.n, self.per_turn, self.turn = eng, sem, 0, per_turn, None

    def begin(self, turn):
        assert self.turn is None or self.n == self.per_turn, (self.n, self.per_turn)
        self.turn, self.n = turn, 0

    def step(self, ins):
        self.n += 1
        ins.then_inc(self.sem, 1)
        self.eng.wait_ge(self.sem, self.turn.count(self.per_turn, self.n) if self.turn else self.n)


class Semaphores:

    phases = 0

    def __init__(self, nc):
        self.nc, self.held = nc, []
        Semaphores.phases += 1

    def __enter__(self):
        return self

    def __call__(self, name):
        self.held.append(self.nc.alloc_semaphore(name=f"{name}_{Semaphores.phases}"))
        return self.held[-1]

    def __exit__(self, *failed):
        if failed[0] is None:
            self.nc.clear_and_free_semaphores(self.held)
            self.nc.all_engine_barrier()


def batch_rows(table, b):
    v = table.rearrange("(b p g) d -> b p (g d)", p=P, g=GB)
    return v[bass.ds(b, 1), :, :].rearrange("a p f -> (a p) f")


def program(nc, io, n_nodes, n_edges):
    nb, n_slots, n_rows_nodes = sizes(n_nodes, n_edges)
    n_tiles = nb * GB
    n_rows = n_slots + n_rows_nodes
    rq = n_tiles // 2
    ctx = ExitStack()
    with ctx:
        def sb(name, shape, dt=F32):
            return ctx.enter_context(nc.sbuf_tensor(name, shape, dt))

        tables = [nc.dram_tensor(f"table{n}", (n_rows, D), F32, kind="Internal").ap() for n in range(9)]
        raw = nc.dram_tensor("raw_rows", (n_rows, D), F32, kind="Internal").ap()
        row_map = nc.dram_tensor("row_map", (n_rows_nodes, 4), F32, kind="Internal").ap()

        ident = sb("ident", [P, P])
        iota = sb("iota", [P, P])
        eps = sb("eps", [P, 1])
        key = sb("key", [P, n_tiles])
        slot_node = sb("slot_node", [P, n_tiles], I32)
        src_row = sb("src_row", [P, n_tiles], I32)
        dst_row = sb("dst_row", [P, n_tiles], I32)
        cont = sb("cont", [P, n_tiles])
        single = sb("single", [P, n_tiles])
        coef = sb("coef", [P, 3, n_tiles])
        self_coef = sb("self_coef", [P, 2, n_tiles])
        ew = sb("ew", [P, 3, n_tiles])
        ew_mean = sb("ew_mean", [P, 3])
        keep = sb("keep", [rq, 2, ROW])
        pen = sb("pen", [rq, 2, ROW])
        keep2 = sb("keep2", [4, 2, rq])
        pen2 = sb("pen2", [4, 2, rq])
        seg_f = sb("seg_f", [rq, 4, ROW])
        seg_b = sb("seg_b", [rq, 4, ROW])
        seg_t = sb("seg_t", [rq, 4])
        seg_s = sb("seg_s", [4, rq])
        seg_c = sb("seg_c", [4, rq])
        bank = [ctx.enter_context(nc.psum_tensor(f"bank{k}", [P, 512], F32)) for k in range(8)]

        def segments(dve, ch, pe_sem, tr_sem, cnt, what, val, first):
            neutral = 0.0 if what == "sum" else -FAR
            ops = (ALU.mult, ALU.add) if what == "sum" else (ALU.add, ALU.max)
            src, src2 = (keep, keep2) if what == "sum" else (pen, pen2)
            for d, out in ((0, seg_f), (1, seg_b)):
                rev = slice(None, None, -1) if d else slice(None)
                for h in range(4):
                    ins = nc.vector.tensor_tensor_scan(out[:, h, rev], src[:, d, rev], val[:, h, rev],
                                                       neutral, *ops)
                ch.step(ins)
                edge = 0 if d else ROW - 1
                nc.vector.tensor_copy(seg_t[:, :], out[:, :, edge]).then_inc(pe_sem, 1)
                cnt[0] += 1
                dve.wait_ge(tr_sem, cnt[0])
                ch.step(nc.vector.tensor_tensor_scan(seg_s[:, rev], src2[:, d, rev],
                                                     bank[0][0:4, 0:rq][:, rev], neutral, *ops))
                ch.step(nc.vector.memset(seg_c[:, :], neutral))
                if d:
                    ins = nc.vector.tensor_copy(seg_c[:, 0:rq - 1], seg_s[:, 1:rq])
                else:
                    ins = nc.vector.tensor_copy(seg_c[:, 1:rq], seg_s[:, 0:rq - 1])
                ins.then_inc(pe_sem, 1)
                cnt[0] += 1
                dve.wait_ge(tr_sem, cnt[0])
                ch.step(nc.vector.tensor_copy(seg_t[:, :], bank[1][0:rq, 0:4]))
                for h in range(4):
                    ins = nc.vector.tensor_tensor_scan(out[:, h, rev], src[:, d, rev], val[:, h, rev],
                                                       seg_t[:, h:h + 1], *ops)
                ch.step(ins)
            if what == "sum":
                ch.step(nc.vector.tensor_tensor(seg_f[:, :, :], seg_f[:, :, :], seg_b[:, :, :], ALU.add))
                ch.step(nc.vector.tensor_tensor(seg_f[:, :, :], seg_f[:, :, :], val[:, :, :], ALU.subtract))
            else:
                ch.step(nc.vector.tensor_tensor(seg_f[:, :, :], seg_f[:, :, :], seg_b[:, :, :], ALU.max))

        def segments_pe(pe, pe_sem, tr_sem, cnt):
            for d in range(2):
                cnt[0] += 1
                pe.wait_ge(pe_sem, cnt[0])
                nc.tensor.transpose(bank[0][0:4, 0:rq], seg_t[:, :], ident[0:rq, 0:rq]).then_inc(tr_sem, 1)
                cnt[0] += 1
                pe.wait_ge(pe_sem, cnt[0])
                nc.tensor.transpose(bank[1][0:rq, 0:4], seg_c[:, :], ident[0:4, 0:4]).then_inc(tr_sem, 1)

        def edge_structure():
            with ExitStack() as c, Semaphores(nc) as sem:
                def s(name, shape, dt=F32):
                    return c.enter_context(nc.sbuf_tensor(name, shape, dt))

                di = s("di", [rq, 3, ROW], I32)
                df = s("df", [rq, 3, ROW])
                val = s("val", [rq, 4, ROW])
                pos = s("pos", [rq, ROW])
                tst = s("tst", [rq, ROW])
                isl = s("isl", [rq, ROW])
                nst = s("nst", [rq, ROW])
                kr = s("kr", [rq, ROW])
                sr = s("sr", [rq, ROW])
                fl = s("fl", [rq, 4])
                wf = s("wf", [rq, 2, 4])
                fb = s("fb", [rq, 4, P])
                ea = s("ea", [P, 8, DE])
                prod = s("prod", [P, 3, 8, DE])
                wet = s("wet", [DE, 3, D])
                wbar = s("wbar", [DE, 3])
                wb = s("wb", [DE, 3, P])
                wrow = s("wrow", [P, 3, DE])
                bem = s("bem", [P, 3, D])
                be1 = s("be1", [P, 3])
                ones = s("ones", [P, P])
                ewc = s("ewc", [P, 3, 8])
                map_new = s("map_new", [P, n_tiles, 4])
                map_def = s("map_def", [P, n_rows_nodes // P, 4])
                wp = s("wp", [P, n_tiles])
                loaded, chain, to_pe, turned, pe_done = (sem(x) for x in (
                    "loaded", "chain", "to_pe", "turned", "pe_done"))
                ea_in, ea_used, map_out, iotas, gather_go, deg_ready = (sem(x) for x in (
                    "ea_in", "ea_used", "map_out", "iotas", "gather_go", "deg_ready"))
                n_load = 10
                with nc.Block() as block:
                    @block.sync
                    def _(sp):
                        v = io["dst3"]
                        for k in range(3):
                            sp.dma_start(di[:, k, :], v[k]).then_inc(loaded, 16)
                        sp.dma_start(val[:, 0, :], io["w_rows"]).then_inc(loaded, 16)
                        sp.dma_start(wp[:, :], io["w_part"]).then_inc(loaded, 16)
                        sp.dma_start(pos[:, :], io["pos"][0:rq, :]).then_inc(loaded, 16)
                        sp.dma_start(ident[:, :], io["ident"]).then_inc(loaded, 16)
                        sp.dma_start(iota[:, :], io["iota"]).then_inc(loaded, 16)
                        sp.dma_start(wet[:, :, :], io["L0_gnn_We"].rearrange("l e h -> e l h")).then_inc(loaded, 16)
                        sp.dma_start(bem[:, :, :], io["be_all"]).then_inc(loaded, 16)
                        sp.dma_start(raw[n_slots:, :].rearrange("(p r) d -> p (r d)", p=P),
                                     io["x"].rearrange("(p r) d -> p (r d)", p=P)).then_inc(map_out, 16)
                        with sp.Fori(0, n_tiles // 8, 1) as i:
                            sp.wait_ge(ea_used, i + 1)
                            sp.dma_start(ea[:, :, :].rearrange("p a b -> p (a b)"),
                                         io["ea"][:, bass.ds(i * (8 * DE), 8 * DE)]).then_inc(ea_in, 16)
                        sp.wait_ge(iotas, 3)
                        sp.dma_start(row_map.rearrange("(p r) f -> p (r f)", p=P),
                                     map_def[:, :, :].rearrange("p r f -> p (r f)")).then_inc(map_out, 16)
                        sp.wait_ge(map_out, 32)

                    @block.gpsimd
                    def _(pool):
                        nr = n_rows_nodes // P
                        nc.gpsimd.memset(map_def[:, :, 1:4], 1.0).then_inc(iotas, 1)
                        nc.gpsimd.iota(map_def[:, :, 0], [[1, nr]], n_slots, nr,
                                       allow_small_or_imprecise_dtypes=True).then_inc(iotas, 1)
                        nc.gpsimd.iota(map_new[:, :, 0].rearrange("p (b g) -> p b g", g=GB),
                                       [[P * GB, nb], [1, GB]], 0, GB,
                                       allow_small_or_imprecise_dtypes=True).then_inc(iotas, 1)

                    @block.tensor
                    def _(pe):
                        cnt = [0]
                        pe.wait_ge(loaded, 16 * n_load)
                        for _i in range(2):
                            cnt[0] += 1
                            pe.wait_ge(to_pe, cnt[0])
                            nc.tensor.transpose(bank[2 + _i][0:4, 0:rq], wf[:, _i, :],
                                                ident[0:rq, 0:rq]).then_inc(turned, 1)
                        cnt[0] += 1
                        pe.wait_ge(to_pe, cnt[0])
                        for j in range(2):
                            nc.tensor.transpose(bank[4][:, j * rq:(j + 1) * rq], kr[:, j * P:(j + 1) * P],
                                                ident[0:rq, 0:rq])
                            nc.tensor.transpose(bank[5][:, j * rq:(j + 1) * rq], sr[:, j * P:(j + 1) * P],
                                                ident[0:rq, 0:rq])
                        for k in range(4):
                            ins = nc.tensor.matmul(bank[6][:, k * rq:(k + 1) * rq], fb[:, k, :],
                                                   ident[0:rq, 0:rq], start=True, stop=True)
                        ins.then_inc(turned, 1)
                        segments_pe(pe, to_pe, turned, cnt)
                        cnt[0] += 1
                        pe.wait_ge(to_pe, cnt[0])
                        for k in range(2):
                            for j in range(2):
                                ins = nc.tensor.transpose(bank[2][:, (2 * k + j) * rq:(2 * k + j + 1) * rq],
                                                          seg_f[:, k, j * P:(j + 1) * P], ident[0:rq, 0:rq])
                        ins.then_inc(turned, 1)
                        cnt[0] += 1
                        pe.wait_ge(to_pe, cnt[0])
                        for k in range(3):
                            ins = nc.tensor.matmul(bank[3][:, k * DE:(k + 1) * DE], wb[:, k, :],
                                                   ident[0:DE, 0:DE], start=True, stop=True)
                        ins.then_inc(turned, 1)
                        cnt[0] += 1
                        pe.wait_ge(to_pe, cnt[0])
                        nc.tensor.matmul(bank[7][:, 0:3], ones[:, :], ewc[:, :, 0], start=True,
                                         stop=True).then_inc(turned, 1)

                    @block.vector
                    def _(dve):
                        ch = Chain(dve, chain)
                        cnt = [0]
                        dve.sem_inc(ea_used, 1)
                        st = ch.step
                        dve.wait_ge(loaded, 16 * n_load)
                        st(nc.vector.tensor_copy(df[:, :, :], di[:, :, :]))
                        st(nc.vector.memset(eps[:, :], EPS))
                        st(nc.vector.memset(ones[:, :], 1.0))
                        st(nc.vector.tensor_tensor(keep[:, 0, :], df[:, 1, :], df[:, 0, :], ALU.is_equal))
                        st(nc.vector.tensor_tensor(keep[:, 1, :], df[:, 1, :], df[:, 2, :], ALU.is_equal))
                        st(nc.vector.tensor_scalar(pen[:, :, :], keep[:, :, :], 1.0, FAR, ALU.subtract, ALU.mult))
                        st(nc.vector.tensor_reduce(fl[:, 0:2], keep[:, :, :], AX.X, ALU.min))
                        for d in range(2):
                            ins = nc.vector.tensor_scalar(wf[:, d, :], ones[0:rq, 0:4], fl[:, d:d + 1], None, ALU.mult)
                            st(ins)
                        dve.sem_inc(to_pe, 1)
                        dve.sem_inc(to_pe, 1)
                        cnt[0] += 2
                        dve.wait_ge(turned, cnt[0])
                        for d in range(2):
                            st(nc.vector.tensor_copy(keep2[:, d, :], bank[2 + d][0:4, 0:rq]))
                        st(nc.vector.tensor_scalar(pen2[:, :, :], keep2[:, :, :], 1.0, FAR, ALU.subtract, ALU.mult))
                        st(nc.vector.tensor_scalar(nst[:, :], keep[:, 0, :], 1.0, None, ALU.mult))
                        st(nc.vector.memset(nst[:, :].rearrange("q (j e) -> q j e", j=2)[:, :, 0], 0.0))
                        st(nc.vector.tensor_scalar(tst[:, :], nst[:, :], -1.0, 1.0, ALU.mult, ALU.add))
                        st(nc.vector.tensor_tensor(kr[:, :], tst[:, :], pos[:, :], ALU.mult))
                        st(nc.vector.tensor_tensor_scan(sr[:, :], nst[:, :], kr[:, :], 0.0, ALU.mult, ALU.add))
                        for j in range(2):
                            a = slice(j * P, (j + 1) * P)
                            st(nc.vector.tensor_scalar(isl[:, a], df[:, 1, a], df[:, 1, (j + 1) * P - 1:(j + 1) * P],
                                                       None, ALU.is_equal))
                        st(nc.vector.tensor_scalar(kr[:, :], sr[:, :], -1.0, P - 1.0, ALU.mult, ALU.add))
                        st(nc.vector.tensor_tensor(kr[:, :], kr[:, :], isl[:, :], ALU.mult))
                        st(nc.vector.tensor_tensor(kr[:, :], kr[:, :], sr[:, :], ALU.add))
                        for j in range(2):
                            st(nc.vector.tensor_copy(fl[:, j:j + 1], keep[:, 0, j * P:j * P + 1]))
                            st(nc.vector.tensor_tensor(fl[:, 2 + j:3 + j], fl[:, j:j + 1], isl[:, j * P:j * P + 1], ALU.mult))
                        for k in range(4):
                            st(nc.vector.tensor_scalar(fb[:, k, :], ones[0:rq, :], fl[:, k:k + 1], None, ALU.mult))
                        st(nc.vector.tensor_scalar(isl[:, :], isl[:, :], -1.0, 1.0, ALU.mult, ALU.add))
                        st(nc.vector.tensor_tensor(tst[:, :], tst[:, :], isl[:, :], ALU.mult))
                        last = tst[:, :].rearrange("q (j e) -> q j e", j=2)[:, :, P - 1]
                        st(nc.vector.tensor_scalar(last, keep[:, 1, :].rearrange("q (j e) -> q j e", j=2)[:, :, P - 1],
                                                   -1.0, 1.0, ALU.mult, ALU.add))
                        st(nc.vector.tensor_scalar(sr[:, :], df[:, 1, :], BIG, None, ALU.subtract))
                        st(nc.vector.tensor_tensor(sr[:, :], sr[:, :], tst[:, :], ALU.mult))
                        st(nc.vector.tensor_scalar(sr[:, :], sr[:, :], BIG, None, ALU.add))
                        dve.sem_inc(to_pe, 1)
                        cnt[0] += 1
                        dve.wait_ge(turned, cnt[0])

                        def parts(t):
                            return t.rearrange("p (q j) -> p j q", j=2)
                        st(nc.vector.tensor_copy(parts(key[:, :]), bank[4][:, 0:2 * rq].rearrange("p (j q) -> p j q", j=2)))
                        st(nc.vector.tensor_copy(parts(slot_node[:, :]), bank[5][:, 0:2 * rq].rearrange("p (j q) -> p j q", j=2)))
                        st(nc.vector.tensor_copy(parts(cont[:, :]), bank[6][:, 0:2 * rq].rearrange("p (j q) -> p j q", j=2)))
                        st(nc.vector.tensor_copy(parts(single[:, :]), bank[6][:, 2 * rq:4 * rq].rearrange("p (j q) -> p j q", j=2)))
                        st(nc.vector.memset(val[:, 1, :], 1.0))
                        st(nc.vector.memset(val[:, 2:4, :], 0.0))
                        segments(dve, ch, to_pe, turned, cnt, "sum", val, True)
                        dve.sem_inc(to_pe, 1)
                        cnt[0] += 1
                        dve.wait_ge(turned, cnt[0])
                        dve.wait_ge(iotas, 3)
                        for k in range(2):
                            st(nc.vector.tensor_scalar(parts(map_new[:, :, 1 + k]),
                                                       bank[2][:, 2 * k * rq:(2 * k + 2) * rq].rearrange("p (j q) -> p j q", j=2),
                                                       1.0, None, ALU.add))
                        st(nc.vector.memset(map_new[:, :, 3], 1.0))
                        st(nc.vector.tensor_reduce(wbar[:, :], wet[:, :, :], AX.X, ALU.add))
                        for k in range(3):
                            st(nc.vector.tensor_scalar(wb[:, k, :], ones[0:DE, :], wbar[:, k:k + 1], 1.0 / D, ALU.mult, ALU.mult))
                        dve.sem_inc(to_pe, 1)
                        cnt[0] += 1
                        dve.wait_ge(turned, cnt[0])
                        st(nc.vector.tensor_copy(wrow[:, :, :].rearrange("p a b -> p (a b)"), bank[3][:, 0:3 * DE]))
                        st(nc.vector.tensor_reduce(be1[:, :], bem[:, :, :], AX.X, ALU.add))
                        st(nc.vector.tensor_scalar(be1[:, :], be1[:, :], 1.0 / D, None, ALU.mult))
                        ch2 = Chain(dve, gather_go, 2)
                        with dve.Fori(0, n_tiles // 8, 1) as i:
                            ch2.begin(Turn(i, 0, 1))
                            dve.wait_ge(ea_in, i * 16 + 16)
                            for k in range(3):
                                ins = nc.vector.tensor_tensor(prod[:, k, :, :], ea[:, :, :],
                                                              wrow[:, k:k + 1, :].to_broadcast([P, 8, DE]), ALU.mult)
                            ch2.step(ins)
                            ch2.step(nc.vector.tensor_reduce(ewc[:, :, :], prod[:, :, :, :], AX.X, ALU.add))
                            nc.vector.tensor_copy(ew[:, :, bass.ds(i * 8, 8)], ewc[:, :, :]).then_inc(ea_used, 1)
                        dve.wait_ge(ea_used, n_tiles // 8 + 1)
                        st(nc.vector.tensor_reduce(ewc[:, :, 0], ew[:, :, :], AX.X, ALU.add))
                        for k in range(3):
                            st(nc.vector.tensor_scalar(ew[:, k, :], ew[:, k, :], be1[:, k:k + 1], None, ALU.add))
                        dve.sem_inc(to_pe, 1)
                        cnt[0] += 1
                        dve.wait_ge(turned, cnt[0])
                        st(nc.vector.scalar_tensor_tensor(ew_mean[:, :], bank[7][:, 0:3], 1.0 / n_edges, be1[:, :],
                                                          ALU.mult, ALU.add))
                got = [s(f"got{k}", [P, 4]) for k in range(GB)]
                put = [s(f"put{k}", [P, 4]) for k in range(GB)]
                back = [s(f"back{k}", [P, 4, D]) for k in range(1)][0]
                ids = s("ids", [P, GB], I32)
                src_i = s("src_i", [P, n_tiles], I32)
                dst_i = s("dst_i", [P, n_tiles], I32)
                ends = s("ends", [P, 2, n_tiles, 4])
                pace, idc, taken, raw_out, in2, d3 = (sem(x) for x in ("pace", "idc", "taken", "raw_out", "in2", "d3"))
                sc_done, lk, raw_ready = (ctx.enter_context(nc.semaphore(x)) for x in ("sc_done", "lk", "raw_ready"))
                deg2 = sem("deg2")
                with nc.Block() as block:
                    @block.sync
                    def _(sp):
                        sp.dma_start(src_i[:, :], io["src_part"]).then_inc(in2, 16)
                        sp.dma_start(dst_i[:, :], io["dst_part"]).then_inc(in2, 16)
                        with sp.Fori(0, nb, 1) as i:
                            sp.wait_ge(raw_ready, i * 64 + 64)
                            sp.dma_start(batch_rows(raw, i), back[:, :, :].rearrange("p g d -> p (g d)")).then_inc(raw_out, 16)
                        sp.wait_ge(raw_out, 16 * nb + 16)

                    @block.gpsimd
                    def _(pool):
                        pool.sem_inc(raw_out, 16)
                        skip = nc.gpsimd.to_reg(n_rows_nodes - 1)
                        with pool.Fori(0, nb, 1) as i:
                            for k in range(GB):
                                nc.gpsimd.tensor_copy(put[k][:, :], map_new[:, bass.ds(i * GB + k, 1), :].rearrange("p a f -> p (a f)"))
                            nc.gpsimd.tensor_copy(ids[:, :], slot_node[:, bass.ds(i * GB, GB)]).then_inc(idc, 1)
                            pool.wait_ge(idc, i + 1)
                            pool.sem_inc(pace, 1)
                            for k in range(GB):
                                nc.gpsimd.indirect_dma_start(
                                    out=row_map, out_offset=bass.IndirectOffsetOnAxis(ap=ids[:, k:k + 1], axis=0),
                                    in_=put[k][:, :], in_offset=None, bounds_check=skip,
                                    oob_is_err=False).then_inc(sc_done, 16)
                            pool.wait_ge(sc_done, i * 64 + 64)
                            pool.sem_inc(pace, 1)
                        pool.wait_ge(in2, 32)
                        for e, idx in enumerate((src_i, dst_i)):
                            with pool.Fori(0, nb, 1) as i:
                                pool.wait_ge(taken, i * GB + (e * GB * nb + 1))
                                pool.sem_inc(pace, 1)
                                nc.gpsimd.tensor_copy(ids[:, :], idx[:, bass.ds(i * GB, GB)]).then_inc(idc, 1)
                                pool.wait_ge(idc, i + (nb * (e + 1) + 1))
                                pool.sem_inc(pace, 1)
                                for k in range(GB):
                                    nc.gpsimd.indirect_dma_start(
                                        out=got[k][:, :], out_offset=None, in_=row_map,
                                        in_offset=bass.IndirectOffsetOnAxis(ap=ids[:, k:k + 1], axis=0)).then_inc(lk, 16)
                        pool.wait_ge(taken, 2 * GB * nb + 1)
                        with pool.Fori(0, nb, 1) as i:
                            pool.wait_ge(raw_out, i * 16 + 16)
                            pool.sem_inc(pace, 1)
                            nc.gpsimd.tensor_copy(ids[:, :], dst_i[:, bass.ds(i * GB, GB)]).then_inc(idc, 1)
                            pool.wait_ge(idc, i + (nb * 3 + 1))
                            pool.sem_inc(pace, 1)
                            for k in range(GB):
                                nc.gpsimd.indirect_dma_start(
                                    out=back[:, k, :], out_offset=None, in_=io["x"],
                                    in_offset=bass.IndirectOffsetOnAxis(ap=ids[:, k:k + 1], axis=0)).then_inc(raw_ready, 16)

                    @block.vector
                    def _(dve):
                        dve.sem_inc(taken, 1)
                        for e in range(2):
                            with dve.Fori(0, nb, 1) as i:
                                dve.wait_ge(lk, i * 64 + (e * 64 * nb + 64))
                                for k in range(GB):
                                    nc.vector.tensor_copy(ends[:, e, bass.ds(i * GB + k, 1), :].rearrange("p a f -> p (a f)"),
                                                          got[k][:, :]).then_inc(taken, 1)
                        ch = Chain(dve, d3)
                        st = ch.step
                        dve.wait_ge(taken, 2 * GB * nb + 1)
                        st(nc.vector.tensor_copy(src_row[:, :], ends[:, 0, :, 0]))
                        st(nc.vector.tensor_copy(dst_row[:, :], ends[:, 1, :, 0]))
                        st(nc.vector.tensor_scalar(ends[:, :, :, 3], ends[:, :, :, 1], 0.0, None, ALU.is_gt))
                        st(nc.vector.tensor_tensor(ends[:, :, :, 1], ends[:, :, :, 1], ends[:, :, :, 3], ALU.mult))
                        st(nc.vector.scalar_tensor_tensor(ends[:, :, :, 1], ends[:, :, :, 1], 1.0, ends[:, :, :, 3], ALU.add, ALU.subtract))
                        st(nc.vector.tensor_scalar(coef[:, 2, :], ends[:, 1, :, 2], 1.0, 1.0, ALU.subtract, ALU.max))
                        st(nc.vector.reciprocal(coef[:, 2, :], coef[:, 2, :]))
                        dve.sem_inc(deg2, 1)
                        dve.wait_ge(deg2, 2)
                        st(nc.vector.reciprocal(ends[:, :, :, 1:3], ends[:, :, :, 1:3]))
                        st(nc.vector.tensor_tensor(ends[:, :, :, 1], ends[:, :, :, 1], ends[:, :, :, 3], ALU.mult))
                        for k in range(2):
                            st(nc.vector.tensor_tensor(coef[:, k, :], ends[:, 0, :, 1 + k], ends[:, 1, :, 1 + k], ALU.mult))
                            st(nc.vector.tensor_tensor(self_coef[:, k, :], ends[:, 1, :, 1 + k], ends[:, 1, :, 1 + k], ALU.mult))
                        st(nc.vector.tensor_tensor(coef[:, 0, :], coef[:, 0, :], wp[:, :], ALU.mult))

                    @block.scalar
                    def _(act):
                        act.wait_ge(deg2, 1)
                        nc.scalar.sqrt(ends[:, :, :, 1:3], ends[:, :, :, 1:3]).then_inc(deg2, 1)

        edge_structure()

        x_in = [sb(f"x_in{u}", [P, GB, D]) for u in range(3)]
        x_res = [sb(f"x_res{u}", [P, GB, D]) for u in range(3)]
        y = [sb(f"y{u}", [P, GB, D]) for u in range(3)]
        x_turned = [sb(f"x_turned{u}", [P, GB, P]) for u in range(3)]
        got = [[sb(f"got_{r}_{k}", [P, D]) for k in range(2 * GB)] for r in range(2)]
        ids = [sb(f"ids_{r}", [P, 2, GB], I32) for r in range(2)]
        pick = [sb(f"pick{k}", [P, HEADS, P]) for k in range(2)]
        own = [sb(f"own{k}", [P, HEADS, P]) for k in range(2)]
        agg = [sb(f"agg{k}", [P, HEADS, P]) for k in range(2)]
        tail = [sb(f"tail{k}", [P, HEADS]) for k in range(2)]
        now = sb("now", [P, 3, GB])
        now_coef = sb("now_coef", [P, 2, GB, HEADS])
        stat6 = [sb(f"stat6_{u}", [P, GB, 6]) for u in range(3)]
        stat = [sb(f"stat_{u}", [P, GB, 2]) for u in range(3)]
        dev = [sb(f"dev_{u}", [P, GB]) for u in range(3)]
        w_slot = sb("w_slot", [P, HEADS, D])
        w_node = sb("w_node", [P, D])
        w_att = sb("w_att", [P, 3 * HEADS])
        att = sb("att", [P, 2, HEADS, D])
        att_p = sb("att_p", [P, 2, HEADS, D])
        affine = sb("affine", [P, 3, D])
        att_s = sb("att_s", [P, n_tiles, HEADS])
        att_d = sb("att_d", [P, n_tiles, 2 * HEADS])

        def load_weights(parts, scale_heads):
            with Semaphores(nc) as sem:
                w_in, w_chain = sem("w_in"), sem("w_chain")
                with nc.Block() as block:
                    @block.sync
                    def _(sp):
                        for dst, src in parts:
                            sp.dma_start(dst, src).then_inc(w_in, 16)
                        sp.wait_ge(w_in, 16 * len(parts))

                    @block.vector
                    def _(dve):
                        st = Chain(dve, w_chain).step
                        dve.wait_ge(w_in, 16 * len(parts))
                        if scale_heads:
                            for k in range(2):
                                st(nc.vector.tensor_tensor(att_p[:, k, :, :], w_slot[:, :, :], att[:, k, :, :], ALU.mult))
                            st(nc.vector.tensor_reduce(w_att[:, HEADS:], att_p[:, :, :, :].rearrange("p k h d -> p (k h) d"),
                                                       AX.X, ALU.add))
                            st(nc.vector.tensor_copy(w_att[:, 0:HEADS], w_att[:, HEADS:2 * HEADS]))
                            st(nc.vector.tensor_scalar(w_slot[:, :, :], w_slot[:, :, :], 1.0 / HEADS, None, ALU.mult))
                            st(nc.vector.tensor_tensor(att_p[:, 0, 0:2, :], w_slot[:, 0:2, :], w_slot[:, 2:4, :], ALU.add))
                            st(nc.vector.tensor_tensor(w_node[:, :], att_p[:, 0, 0, :], att_p[:, 0, 1, :], ALU.add))

        def rows_pass(slots, nodes, scores, inp, out, res, post, mode):
            us = ([1, 2] if nodes else []) + ([0] if slots else [])
            edges = slots and mode != "own"
            blocks = {"gat": HEADS, "sage": 2}[mode] if mode in ("gat", "sage") else 1
            summed = HEADS if mode == "gat" else 1
            with_res = post in ("norm", "gat_end")
            n_stat = {"relu": 0, "norm": 1, "gat": 1, "gat_end": 2}[post]
            gat = post in ("gat", "gat_end")
            with Semaphores(nc) as sem:
                def sems(name):
                    return [sem(f"{name}{u}") for u in range(3)]
                x_loaded, res_loaded, stored = sems("x_loaded"), sems("res_loaded"), sems("stored")
                turned, turned_out, y_ready, y_taken = sems("turned"), sems("turned_out"), sems("y_ready"), sems("y_taken")
                stat_ready, dev_ready, summed_up, done = sems("stat_ready"), sems("dev_ready"), sems("summed_up"), sems("done")
                gathered = [ctx.enter_context(nc.semaphore(f"gathered{r}_{out.tensor.name}_{mode}_{int(slots)}")) for r in range(2)] if edges or scores else None
                picks_ready, agg_ready, agg_out, agg_fixed, agg_used = (sem(x) for x in (
                    "picks_ready", "agg_ready", "agg_out", "agg_fixed", "agg_used"))
                sc_turned, sc_out, sc_ready, sc_taken = (sem(x) for x in ("sc_turned", "sc_out", "sc_ready", "sc_taken"))
                ids_ready, pool_pace, dve_pace, dve_chain, dve_start = (sem(x) for x in (
                    "ids_ready", "pool_pace", "dve_pace", "dve_chain", "dve_start"))
                AHEAD = 6

                def tail_bank(b):
                    return bank[2 + b][:, 0:HEADS] if mode == "gat" else bank[b][:, 2 * P:2 * P + 1]

                def table_batch(t, u, turn):
                    b = turn.batch()
                    return batch_rows(t, b if u == 0 else b * 2 + (nb + u - 1))

                with nc.Block() as block:
                    @block.sync
                    def _(sp):
                        def load(u, turn):
                            sp.dma_start(x_in[u][:, :, :].rearrange("p g d -> p (g d)"),
                                         table_batch(inp, u, turn)).then_inc(x_loaded[u], 16)
                            if with_res:
                                sp.dma_start(x_res[u][:, :, :].rearrange("p g d -> p (g d)"),
                                             table_batch(res, u, turn)).then_inc(res_loaded[u], 16)

                        def store(u, turn):
                            sp.wait_ge(done[u], turn.count(1, 1))
                            sp.dma_start(table_batch(out, u, turn),
                                         y[u][:, :, :].rearrange("p g d -> p (g d)")).then_inc(stored[u], 16)
                        for u in us:
                            load(u, Turn(0, 0))
                        with sp.Fori(0, nb // 2 - 1, 1) as i:
                            for half in range(2):
                                for u in us:
                                    store(u, Turn(i, half))
                                    load(u, Turn(i, half + 1))
                        for u in us:
                            store(u, Turn(nb // 2 - 1, 0))
                            load(u, Turn(nb // 2 - 1, 1))
                        for u in us:
                            store(u, Turn(nb // 2 - 1, 1))
                        for u in us:
                            sp.wait_ge(stored[u], 16 * nb + 16)

                    @block.gpsimd
                    def _(pool):
                        for u in us:
                            pool.sem_inc(stored[u], 16)
                        if not (edges or scores):
                            return
                        with pool.Fori(0, nb // 2, 1) as i:
                            for half in range(2):
                                turn = Turn(i, half)
                                if scores:
                                    pool.wait_ge(sc_turned, turn.count(1, 1))
                                else:
                                    pool.wait_ge(agg_ready, turn.count(GB, AHEAD - GB))
                                pool.sem_inc(pool_pace, 1)
                                nc.gpsimd.tensor_copy(ids[half][:, 0, :], src_row[:, bass.ds(turn.batch() * GB, GB)])
                                nc.gpsimd.tensor_copy(ids[half][:, 1, :], dst_row[:, bass.ds(turn.batch() * GB, GB)]).then_inc(ids_ready, 1)
                                pool.wait_ge(ids_ready, turn.count(1, 1))
                                pool.sem_inc(pool_pace, 1)
                                for e in range(2 if scores else 1):
                                    for k in range(GB):
                                        nc.gpsimd.indirect_dma_start(
                                            out=got[half][e * GB + k][:, :], out_offset=None, in_=inp,
                                            in_offset=bass.IndirectOffsetOnAxis(ap=ids[half][:, e, k:k + 1], axis=0)
                                        ).then_inc(gathered[half], 16)

                    @block.tensor
                    def _(pe):
                        if scores:
                            pe.sem_inc(sc_turned, 2)
                        if edges:
                            pe.sem_inc(agg_ready, AHEAD)

                        def turn_rows(u, turn):
                            pe.wait_ge(x_loaded[u], turn.count(16, 16))
                            pe.wait_ge(y_taken[u], turn.count(1, 1))
                            for g in range(GB):
                                ins = nc.tensor.transpose(bank[2 + u][:, g * P:(g + 1) * P], x_in[u][:, g, :], ident[:, :])
                            ins.then_inc(turned[u], 1)

                        def product(u, turn):
                            pe.wait_ge(turned_out[u], turn.count(1, 1))
                            for g in range(GB):
                                ins = nc.tensor.matmul(bank[5 + u][:, g * D:(g + 1) * D], x_turned[u][:, g, :],
                                                       w_node[:, :], start=True, stop=True)
                            ins.then_inc(y_ready[u], 1)

                        def sum_edges(k, half, turn):
                            pe.wait_ge(gathered[half], turn.i * 64 + 64)
                            if k == 0:
                                pe.wait_ge(x_loaded[0], turn.count(16, 16))
                            pe.wait_ge(picks_ready, turn.count(GB, k + 1))
                            pe.wait_ge(agg_out, turn.count(GB, k + 1))
                            pe.wait_ge(agg_fixed, turn.count(GB, k + 1))
                            g, b = got[half][k], k % 2
                            nc.tensor.matmul(tail_bank(b), g[:, :], pick[b][:, 0:summed, P - 1],
                                             start=True, stop=True)
                            a = bank[b][:, 0:summed * P]
                            last = mode == "sage"
                            ins = nc.tensor.matmul(a, g[:, :], pick[b][:, 0:summed, :].rearrange("p h e -> p (h e)"),
                                                   start=True, stop=last)
                            if mode == "sage":
                                ins = nc.tensor.transpose(bank[b][:, P:2 * P], x_in[0][:, k, :], ident[:, :])
                            else:
                                ins = nc.tensor.matmul(a, x_in[0][:, k, :], own[b][:, 0:summed, :].rearrange("p h e -> p (h e)"),
                                                       start=False, stop=True)
                            ins.then_inc(agg_ready, 1)

                        def slot_product(k, turn):
                            pe.wait_ge(agg_fixed, turn.count(GB, k + 3))
                            if k == 0:
                                pe.wait_ge(y_taken[0], turn.count(1, 1))
                            for h in range(blocks):
                                ins = nc.tensor.matmul(bank[5][:, k * D:(k + 1) * D], agg[k % 2][:, h, :], w_slot[:, h, :],
                                                       start=(h == 0), stop=(h == blocks - 1))
                            if k == GB - 1:
                                ins.then_inc(y_ready[0], 1)
                            else:
                                ins.then_inc(agg_used, 1)

                        def score_rows(half, turn):
                            pe.wait_ge(gathered[half], turn.i * 128 + 128)
                            for e in range(2):
                                for g in range(GB):
                                    ins = nc.tensor.transpose(bank[e][:, g * P:(g + 1) * P], got[half][e * GB + g][:, :], ident[:, :])
                            ins.then_inc(sc_turned, 1)

                        def score_products(turn):
                            pe.wait_ge(sc_out, turn.count(2, 2))
                            pe.wait_ge(sc_taken, turn.count(1, 1))
                            for g in range(GB):
                                nc.tensor.matmul(bank[2][:, g * HEADS:(g + 1) * HEADS], agg[0][:, g, :], w_att[:, 0:HEADS],
                                                 start=True, stop=True)
                                ins = nc.tensor.matmul(bank[2][:, 16 + g * 8:24 + g * 8], agg[1][:, g, :], w_att[:, HEADS:],
                                                       start=True, stop=True)
                            ins.then_inc(sc_ready, 1)

                        with pe.Fori(0, nb // 2, 1) as i:
                            for half in range(2):
                                turn = Turn(i, half)
                                for u in us:
                                    if u or not edges:
                                        turn_rows(u, turn)
                                if scores:
                                    score_rows(half, turn)
                                if edges:
                                    sum_edges(0, half, turn)
                                if nodes:
                                    product(1, turn)
                                if edges:
                                    sum_edges(1, half, turn)
                                    slot_product(0, turn)
                                if nodes:
                                    product(2, turn)
                                if edges:
                                    sum_edges(2, half, turn)
                                    slot_product(1, turn)
                                    sum_edges(3, half, turn)
                                    slot_product(2, turn)
                                    slot_product(3, turn)
                                elif slots:
                                    product(0, turn)
                                if scores:
                                    score_products(turn)

                    @block.scalar
                    def _(act):
                        if edges:
                            act.sem_inc(agg_out, 2)

                        def deviation(u, turn, n):
                            act.wait_ge(stat_ready[u], turn.count(n_stat, n))
                            nc.scalar.activation(dev[u][:, :], stat[u][:, :, 1], ACT.Sqrt,
                                                 bias=eps[:, 0:1]).then_inc(dev_ready[u], 1)
                        with act.Fori(0, nb // 2, 1) as i:
                            for half in range(2):
                                turn = Turn(i, half)
                                for u in us:
                                    if u or not edges:
                                        act.wait_ge(turned[u], turn.count(1, 1))
                                        nc.scalar.copy(x_turned[u][:, :, :].rearrange("p g e -> p (g e)"),
                                                       bank[2 + u][:, :]).then_inc(turned_out[u], 1)
                                if scores:
                                    act.wait_ge(sc_turned, turn.count(1, 3))
                                    for e in range(2):
                                        nc.scalar.copy(agg[e][:, :, :].rearrange("p g e -> p (g e)"),
                                                       bank[e][:, :]).then_inc(sc_out, 1)
                                if edges:
                                    for k in range(GB):
                                        act.wait_ge(agg_ready, turn.count(GB, AHEAD + k + 1))
                                        if k < 2:
                                            act.wait_ge(y_taken[0], turn.count(1, 1))
                                        else:
                                            act.wait_ge(agg_used, turn.count(GB - 1, k - 1))
                                        nc.scalar.copy(agg[k % 2][:, 0:blocks, :].rearrange("p h e -> p (h e)"),
                                                       bank[k % 2][:, 0:blocks * P]).then_inc(agg_out, 1)
                                for u in us:
                                    if post == "relu":
                                        act.wait_ge(y_taken[u], turn.count(1, 2))
                                        nc.scalar.activation(y[u][:, :, :], y[u][:, :, :], ACT.Relu).then_inc(done[u], 1)
                                    else:
                                        deviation(u, turn, 1)
                                if post == "gat":
                                    for u in us:
                                        act.wait_ge(summed_up[u], turn.count(1, 1))
                                        nc.scalar.activation(y[u][:, :, :], y[u][:, :, :], ACT.Relu).then_inc(done[u], 1)
                                if post == "gat_end":
                                    for u in us:
                                        deviation(u, turn, 2)

                    @block.vector
                    def _(dve):
                        for u in us:
                            dve.sem_inc(y_taken[u], 1)
                        if scores:
                            dve.sem_inc(sc_taken, 1)
                        per_u = {"relu": 0, "norm": 3, "gat": 5, "gat_end": 9}[post]
                        ch = Chain(dve, dve_chain, per_u * len(us) + (1 + 2 * GB if edges else 0))
                        if edges:
                            dve.sem_inc(agg_fixed, 2)
                            nc.vector.memset(tail[0][:, :], 0.0).then_inc(dve_start, 1)
                            dve.wait_ge(dve_start, 1)

                        def wide(k):
                            return affine[:, k:k + 1, :].to_broadcast([P, GB, D])

                        def statistics(u):
                            for g in range(GB):
                                ins = nc.vector.bn_stats(stat6[u][:, g, :], y[u][:, g, :])
                            ch.step(ins)
                            dve.sem_inc(dve_pace, 1)
                            for g in range(GB):
                                ins = nc.vector.bn_aggr(stat[u][:, g, :], stat6[u][:, g, :])
                            ins.then_inc(stat_ready[u], 1)

                        def normalise(u, turn, n):
                            dve.wait_ge(dev_ready[u], turn.count(n_stat, n))
                            ch.step(nc.vector.reciprocal(dev[u][:, :], dev[u][:, :]))
                            for g in range(GB):
                                ins = nc.vector.tensor_scalar(y[u][:, g, :], y[u][:, g, :], stat[u][:, g, 0:1],
                                                              dev[u][:, g:g + 1], ALU.subtract, ALU.mult)
                            return ins

                        def take(u, turn):
                            dve.wait_ge(y_ready[u], turn.count(1, 1))
                            dve.wait_ge(stored[u], turn.count(16, 16))
                            nc.vector.tensor_tensor(y[u][:, :, :], bank[5 + u][:, :].rearrange("p (g d) -> p g d", g=GB),
                                                    wide(0), ALU.add).then_inc(y_taken[u], 1)
                            if post == "relu":
                                return
                            dve.wait_ge(y_taken[u], turn.count(1, 2))
                            if post == "norm":
                                dve.wait_ge(res_loaded[u], turn.count(16, 16))
                                ch.step(nc.vector.scalar_tensor_tensor(y[u][:, :, :], y[u][:, :, :], 0.0, x_res[u][:, :, :],
                                                                       ALU.max, ALU.add))
                            statistics(u)

                        def finish(u, turn):
                            if post == "relu":
                                return
                            ins = normalise(u, turn, 1)
                            if post == "norm":
                                ins.then_inc(done[u], 1)
                                return
                            ch.step(ins)
                            ch.step(nc.vector.tensor_tensor(y[u][:, :, :], y[u][:, :, :], wide(1), ALU.mult))
                            ch.step(nc.vector.tensor_tensor(y[u][:, :, :], y[u][:, :, :], wide(2), ALU.add))
                            ins = nc.vector.tensor_tensor(y[u][:, :, :], y[u][:, :, :], x_in[u][:, :, :], ALU.add)
                            if post == "gat":
                                ins.then_inc(summed_up[u], 1)
                                return
                            ch.step(ins)
                            dve.wait_ge(res_loaded[u], turn.count(16, 16))
                            ch.step(nc.vector.scalar_tensor_tensor(y[u][:, :, :], y[u][:, :, :], 0.0, x_res[u][:, :, :],
                                                                   ALU.max, ALU.add))
                            statistics(u)

                        def finish_end(u, turn):
                            normalise(u, turn, 2).then_inc(done[u], 1)

                        def read_now(turn):
                            t = bass.ds(turn.batch() * GB, GB)
                            nc.vector.tensor_copy(now[:, 0, :], key[:, t])
                            nc.vector.tensor_copy(now[:, 1, :], cont[:, t])
                            nc.vector.tensor_copy(now[:, 2, :], single[:, t])
                            if mode == "gat":
                                nc.vector.tensor_copy(now_coef[:, 0, :, :], att_s[:, t, :])
                                ins = nc.vector.tensor_copy(now_coef[:, 1, :, :], att_d[:, t, 0:HEADS])
                            elif mode == "sage":
                                ins = nc.vector.tensor_copy(now_coef[:, 0, :, 0], coef[:, 2, t])
                            else:
                                m = int(mode[3])
                                nc.vector.tensor_copy(now_coef[:, 0, :, 0], coef[:, m, t])
                                ins = nc.vector.tensor_copy(now_coef[:, 1, :, 0], self_coef[:, m, t])
                            ch.step(ins)

                        def build(k, turn):
                            dve.wait_ge(agg_ready, turn.count(GB, AHEAD + k - 1))
                            for h in range(summed):
                                ins = nc.vector.tensor_scalar(pick[k % 2][:, h, :], iota[:, :], now[:, 0, k:k + 1],
                                                              now_coef[:, 0, k, h:h + 1], ALU.is_equal, ALU.mult)
                                if mode != "sage":
                                    ins = nc.vector.tensor_scalar(own[k % 2][:, h, :], ident[:, :],
                                                                  now_coef[:, 1, k, h:h + 1], None, ALU.mult)
                            ins.then_inc(picks_ready, 1)

                        def fix(k, turn):
                            dve.wait_ge(agg_out, turn.count(GB, k + 3))
                            t0, t1 = tail[k % 2], tail[(k + 1) % 2]
                            a = agg[k % 2]
                            ch.step(nc.vector.scalar_tensor_tensor(t1[:, 0:summed], t0[:, 0:summed], now[:, 2, k:k + 1],
                                                                   tail_bank(k % 2), ALU.mult, ALU.add))
                            ch.step(nc.vector.scalar_tensor_tensor(a[:, 0:summed, 0], t0[:, 0:summed], now[:, 1, k:k + 1],
                                                                   a[:, 0:summed, 0], ALU.mult, ALU.add))
                            nc.vector.scalar_tensor_tensor(a[:, 0:summed, P - 1], t0[:, 0:summed], now[:, 2, k:k + 1],
                                                           a[:, 0:summed, P - 1], ALU.mult, ALU.add).then_inc(agg_fixed, 1)
                            dve.wait_ge(agg_fixed, turn.count(GB, k + 3))

                        with dve.Fori(0, nb // 2, 1) as i:
                            for half in range(2):
                                turn = Turn(i, half)
                                ch.begin(turn)
                                if edges:
                                    read_now(turn)
                                    build(0, turn)
                                    build(1, turn)
                                    fix(0, turn)
                                    build(2, turn)
                                    fix(1, turn)
                                    build(3, turn)
                                if nodes:
                                    take(1, turn)
                                if edges:
                                    fix(2, turn)
                                if nodes:
                                    take(2, turn)
                                if edges:
                                    fix(3, turn)
                                if scores:
                                    dve.wait_ge(sc_ready, turn.count(1, 1))
                                    t = bass.ds(turn.batch() * GB, GB)
                                    nc.vector.tensor_copy(att_s[:, t, :], bank[2][:, 0:16].rearrange("p (g h) -> p g h", g=GB))
                                    nc.vector.tensor_copy(att_d[:, t, :], bank[2][:, 16:48].rearrange("p (g h) -> p g h", g=GB)).then_inc(sc_taken, 1)
                                if slots:
                                    take(0, turn)
                                for u in us:
                                    finish(u, turn)
                                if post == "gat_end":
                                    for u in us:
                                        finish_end(u, turn)
                                ch.n += 0

        def softmax(layer):
            with ExitStack() as c, Semaphores(nc) as sem:
                lr = c.enter_context(nc.sbuf_tensor(f"lr_{layer}", [rq, 4, ROW], F32))
                sr = c.enter_context(nc.sbuf_tensor(f"own_r_{layer}", [rq, 4, ROW], F32))
                dr = c.enter_context(nc.sbuf_tensor(f"den_r_{layer}", [rq, 4, ROW], F32))
                tmp = c.enter_context(nc.sbuf_tensor(f"tmp_p_{layer}", [P, n_tiles, HEADS], F32))
                to_pe, turned, chain, exps = (sem(x) for x in ("to_pe", "turned", "chain", "exps"))
                with nc.Block() as block:
                    @block.scalar
                    def _(act):
                        act.wait_ge(exps, 1)
                        nc.scalar.activation(lr[:, :, :], lr[:, :, :], ACT.Exp)
                        nc.scalar.activation(sr[:, :, :], sr[:, :, :], ACT.Exp).then_inc(exps, 1)

                    @block.tensor
                    def _(pe):
                        cnt = [1]
                        pe.wait_ge(to_pe, 1)
                        for e, src in ((0, att_s), (1, tmp)):
                            for h in range(HEADS):
                                for j in range(2):
                                    ins = nc.tensor.transpose(bank[2 + 2 * e + h // 2][0:rq, ((h % 2) * 2 + j) * P:((h % 2) * 2 + j + 1) * P],
                                                              src[:, :, h].rearrange("p (q j) -> p j q", j=2)[:, j, :], ident[:, :])
                        ins.then_inc(turned, 1)
                        segments_pe(pe, to_pe, turned, cnt)
                        segments_pe(pe, to_pe, turned, cnt)
                        cnt[0] += 1
                        pe.wait_ge(to_pe, cnt[0])
                        for e, src in ((0, lr), (1, sr)):
                            for h in range(HEADS):
                                for j in range(2):
                                    ins = nc.tensor.transpose(bank[2 + 2 * e + h // 2][:, ((h % 2) * 2 + j) * rq:((h % 2) * 2 + j + 1) * rq],
                                                              src[:, h, j * P:(j + 1) * P], ident[0:rq, 0:rq])
                        ins.then_inc(turned, 1)

                    @block.vector
                    def _(dve):
                        st = Chain(dve, chain)
                        ch, st = st, st.step
                        cnt = [1]
                        vd = att_d[:, :, HEADS:]
                        st(nc.vector.tensor_tensor(att_s[:, :, :], att_s[:, :, :], vd, ALU.add))
                        st(nc.vector.tensor_tensor(tmp[:, :, :], att_d[:, :, 0:HEADS], vd, ALU.add))
                        for h in range(HEADS):
                            st(nc.vector.tensor_tensor(att_s[:, :, h], att_s[:, :, h], ew[:, layer, :], ALU.add))
                        st(nc.vector.tensor_scalar(tmp[:, :, :], tmp[:, :, :], ew_mean[:, layer:layer + 1], None, ALU.add))
                        st(nc.vector.scalar_tensor_tensor(att_s[:, :, :], att_s[:, :, :], SLOPE, att_s[:, :, :], ALU.mult, ALU.max))
                        nc.vector.scalar_tensor_tensor(tmp[:, :, :], tmp[:, :, :], SLOPE, tmp[:, :, :], ALU.mult, ALU.max).then_inc(to_pe, 1)
                        dve.wait_ge(turned, 1)
                        for e, dst in ((0, lr), (1, sr)):
                            for m in range(2):
                                st(nc.vector.tensor_copy(dst[:, 2 * m:2 * m + 2, :].rearrange("q h e -> q (h e)"),
                                                         bank[2 + 2 * e + m][0:rq, :]))
                        segments(dve, ch, to_pe, turned, cnt, "max", lr, False)
                        st(nc.vector.tensor_tensor(seg_f[:, :, :], seg_f[:, :, :], sr[:, :, :], ALU.max))
                        st(nc.vector.tensor_tensor(lr[:, :, :], lr[:, :, :], seg_f[:, :, :], ALU.subtract))
                        nc.vector.tensor_tensor(sr[:, :, :], sr[:, :, :], seg_f[:, :, :], ALU.subtract).then_inc(exps, 1)
                        dve.wait_ge(exps, 2)
                        segments(dve, ch, to_pe, turned, cnt, "sum", lr, False)
                        st(nc.vector.tensor_tensor(dr[:, :, :], seg_f[:, :, :], sr[:, :, :], ALU.add))
                        st(nc.vector.reciprocal(dr[:, :, :], dr[:, :, :]))
                        st(nc.vector.tensor_tensor(lr[:, :, :], lr[:, :, :], dr[:, :, :], ALU.mult))
                        nc.vector.tensor_tensor(sr[:, :, :], sr[:, :, :], dr[:, :, :], ALU.mult).then_inc(to_pe, 1)
                        cnt[0] += 1
                        dve.wait_ge(turned, cnt[0])
                        for e, dst in ((0, att_s), (1, att_d)):
                            for h in range(HEADS):
                                o = (h % 2) * 2 * rq
                                st(nc.vector.tensor_copy(dst[:, :, h].rearrange("p (q j) -> p j q", j=2),
                                                         bank[2 + 2 * e + h // 2][:, o:o + 2 * rq].rearrange("p (j q) -> p j q", j=2)))

        t = tables
        load_weights([(w_node[:, :], io["L0_gnn_W0"]), (affine[:, 0, :], io["b_L0_b0"])], False)
        rows_pass(True, True, False, raw, t[0], None, "relu", "own")
        for l in range(3):
            load_weights([(w_slot[:, :, :], io["L0_gnn_Wg"][l].rearrange("k (h d) -> k h d", h=HEADS)),
                          (att[:, :, :, :], io["b_att"][l]), (affine[:, :, :], io["b_affine"][l])], True)
            post, res = ("gat_end", raw) if l == 2 else ("gat", None)
            rows_pass(False, True, True, t[l], t[l + 1], res, post, "gat")
            softmax(l)
            rows_pass(True, False, False, t[l], t[l + 1], res, post, "gat")
        rest = [("L1_gnn_W1", "L1_gnn_b1", "gcn0", "relu", None), ("L1_gnn_W2", "L1_gnn_b2", "gcn0", "norm", 3),
                ("L2_gnn_W", "L2_gnn_b", "gcn1", "norm", 5), ("L3_gnn_W1", "L3_gnn_b1", "sage", "relu", None),
                ("L3_gnn_W2", "L3_gnn_b2", "sage", "norm", 6)]
        for n, (w, b, mode, post, res) in enumerate(rest):
            if mode == "sage":
                parts = [(w_slot[:, 0, :], io[w][D:, :]), (w_slot[:, 1, :], io[w][0:D, :]), (w_node[:, :], io[w][0:D, :])]
            else:
                parts = [(w_slot[:, 0, :], io[w]), (w_node[:, :], io[w])]
            load_weights(parts + [(affine[:, 0, :], io["b_" + b])], False)
            rows_pass(True, True, False, t[3 + n], t[4 + n], None if res is None else t[res], post, mode)
        placed = ctx.enter_context(nc.semaphore("placed"))
        with Semaphores(nc) as sem:
            copied, idc, pace, free = (sem(x) for x in ("copied", "idc", "pace", "free"))
            loaded = [sem(f"loaded{r}") for r in range(2)]
            with nc.Block() as block:
                @block.sync
                def _(sp):
                    sp.dma_start(io["out"].rearrange("(p r) d -> p (r d)", p=P),
                                 t[8][n_slots:, :].rearrange("(p r) d -> p (r d)", p=P)).then_inc(copied, 16)
                    with sp.Fori(0, nb // 2, 1) as i:
                        for half in range(2):
                            turn = Turn(i, half)
                            sp.wait_ge(free, turn.count(1, 1))
                            sp.dma_start(x_in[half][:, :, :].rearrange("p g d -> p (g d)"),
                                         batch_rows(t[8], turn.batch())).then_inc(loaded[half], 16)

                @block.gpsimd
                def _(pool):
                    skip = nc.gpsimd.to_reg(n_rows_nodes - 1)
                    pool.sem_inc(free, 2)
                    pool.wait_ge(copied, 16)
                    with pool.Fori(0, nb // 2, 1) as i:
                        for half in range(2):
                            turn = Turn(i, half)
                            nc.gpsimd.tensor_copy(ids[half][:, 0, :], slot_node[:, bass.ds(turn.batch() * GB, GB)]).then_inc(idc, 1)
                            pool.wait_ge(idc, turn.count(1, 1))
                            pool.sem_inc(pace, 1)
                            pool.wait_ge(loaded[half], i * 16 + 16)
                            pool.sem_inc(pace, 1)
                            for k in range(GB):
                                nc.gpsimd.indirect_dma_start(
                                    out=io["out"], out_offset=bass.IndirectOffsetOnAxis(ap=ids[half][:, 0, k:k + 1], axis=0),
                                    in_=x_in[half][:, k, :], in_offset=None, bounds_check=skip,
                                    oob_is_err=False).then_inc(placed, 16)
                        pool.wait_ge(placed, i * 128 + 128)
                        pool.sem_inc(free, 1)
                        pool.sem_inc(free, 1)


def kernel(**inputs):
    import numpy as _np
    import concourse.bacc as _bacc
    from concourse import mybir as _mybir
    from concourse.bass_utils import run_bass_kernel_spmd as _run

    a = {k: _np.asarray(v) for k, v in inputs.items()}
    n_nodes, n_edges = a["x"].shape[0], a["src"].shape[0]
    nb, n_slots, n_rows_nodes = sizes(n_nodes, n_edges)
    assert n_rows_nodes > n_nodes
    rq, n_tiles = n_slots // ROW, n_slots // P

    def padded(v, n, fill=0):
        w = _np.full((n,) + v.shape[1:], fill, v.dtype)
        w[:v.shape[0]] = v
        return w

    def part(v):
        return _np.ascontiguousarray(_np.moveaxis(v.reshape((n_tiles, P) + v.shape[1:]), 0, 1))

    def wide(v):
        return _np.ascontiguousarray(_np.broadcast_to(v, (P,) + v.shape))
    dst = padded(a["dst"], n_slots, n_nodes)
    around = _np.full(n_slots + 2, -1, dst.dtype)
    around[1:-1] = dst
    src = padded(a["src"], n_slots)
    w = padded(a["edge_weight"], n_slots)
    io = {
        "x": padded(a["x"], n_rows_nodes),
        "dst3": _np.stack([around[:-2], around[1:-1], around[2:]]).reshape(3, rq, ROW),
        "w_rows": w.reshape(rq, ROW), "w_part": part(w), "src_part": part(src), "dst_part": part(dst),
        "ea": part(padded(a["edge_attr_64"], n_slots)).reshape(P, n_tiles * DE),
        "ident": _np.eye(P, dtype=_np.float32),
        "iota": wide(_np.arange(P, dtype=_np.float32)),
        "pos": wide(_np.arange(ROW, dtype=_np.float32) % P),
        "L0_gnn_We": a["L0_gnn_We"], "be_all": wide(a["L0_gnn_be"]),
        "L0_gnn_W0": a["L0_gnn_W0"], "b_L0_b0": wide(a["L0_gnn_b0"]), "L0_gnn_Wg": a["L0_gnn_Wg"],
        "b_att": _np.stack([wide(_np.stack([a["L0_gnn_att_src"][l], a["L0_gnn_att_dst"][l]])) for l in range(3)]),
        "b_affine": _np.stack([wide(_np.stack([a["L0_gnn_" + k][l] for k in ("bg", "gamma", "beta")])) for l in range(3)]),
        "L1_gnn_W1": _np.ascontiguousarray(a["L1_gnn_W1"].T), "L1_gnn_W2": _np.ascontiguousarray(a["L1_gnn_W2"].T),
        "L2_gnn_W": a["L2_gnn_W"], "L3_gnn_W1": a["L3_gnn_W1"], "L3_gnn_W2": a["L3_gnn_W2"],
    }
    for k in ("L1_gnn_b1", "L1_gnn_b2", "L2_gnn_b", "L3_gnn_b1", "L3_gnn_b2"):
        io["b_" + k] = wide(a[k])
    nc = _bacc.Bacc("TRN2", target_bir_lowering=False, num_devices=1)
    arrays = {f"in_{k}_dram": _np.ascontiguousarray(v) for k, v in io.items()}
    aps = {k: nc.dram_tensor(f"in_{k}_dram", v.shape, _mybir.dt.from_np(v.dtype), kind="ExternalInput").ap()
           for k, v in io.items()}
    aps["out"] = nc.dram_tensor("out_0_dram", (n_rows_nodes, D), _mybir.dt.float32, kind="ExternalOutput").ap()
    program(nc, aps, n_nodes, n_edges)
    r = _run(nc, [arrays], core_ids=[0])
    return r.results[0]["out_0_dram"][:n_nodes]
```

```python
from contextlib import ExitStack

import numpy as np
import concourse.bass as bass
from concourse import mybir

F32 = mybir.dt.float32
I32 = mybir.dt.int32
ALU = mybir.AluOpType
ACT = mybir.ActivationFunctionType
AX = mybir.AxisListType

P = 128
D = 128
DE = 64
HEADS = 4
GB = 4
BIG = 1.0e6
FAR = 1.0e30
EPS = 1e-5
SLOPE = 0.2
ROW = 256


def sizes(n_nodes, n_edges):
    nb = max(-(-n_edges // (P * GB)), -(-n_nodes // (2 * P * GB)))
    nb += nb % 2
    return nb, nb * GB * P, 2 * nb * GB * P


class Turn:

    def __init__(self, i, half, span=2):
        self.i, self.half, self.span = i, half, span

    def count(self, k, n):
        return self.i * (self.span * k) + (self.half * k + n)

    def batch(self):
        return self.i * self.span + self.half


class Chain:

    def __init__(self, eng, sem, per_turn=0):
        self.eng, self.sem, self.n, self.per_turn, self.turn = eng, sem, 0, per_turn, None

    def begin(self, turn):
        assert self.turn is None or self.n == self.per_turn, (self.n, self.per_turn)
        self.turn, self.n = turn, 0

    def step(self, ins):
        self.n += 1
        ins.then_inc(self.sem, 1)
        self.eng.wait_ge(self.sem, self.turn.count(self.per_turn, self.n) if self.turn else self.n)


class Semaphores:

    phases = 0

    def __init__(self, nc):
        self.nc, self.held = nc, []
        Semaphores.phases += 1

    def __enter__(self):
        return self

    def __call__(self, name):
        self.held.append(self.nc.alloc_semaphore(name=f"{name}_{Semaphores.phases}"))
        return self.held[-1]

    def __exit__(self, *failed):
        if failed[0] is None:
            self.nc.clear_and_free_semaphores(self.held)
            self.nc.all_engine_barrier()


def batch_rows(table, b):
    v = table.rearrange("(b p g) d -> b p (g d)", p=P, g=GB)
    return v[bass.ds(b, 1), :, :].rearrange("a p f -> (a p) f")


def program(nc, io, n_nodes, n_edges):
    nb, n_slots, n_rows_nodes = sizes(n_nodes, n_edges)
    n_tiles = nb * GB
    n_rows = n_slots + n_rows_nodes
    rq = n_tiles // 2
    ctx = ExitStack()
    with ctx:
        def sb(name, shape, dt=F32):
            return ctx.enter_context(nc.sbuf_tensor(name, shape, dt))

        tables = [nc.dram_tensor(f"table{n}", (n_rows, D), F32, kind="Internal").ap() for n in range(9)]
        raw = nc.dram_tensor("raw_rows", (n_rows, D), F32, kind="Internal").ap()
        row_map = nc.dram_tensor("row_map", (n_rows_nodes, 4), F32, kind="Internal").ap()

        ident = sb("ident", [P, P])
        iota = sb("iota", [P, P])
        eps = sb("eps", [P, 1])
        key = sb("key", [P, n_tiles])
        slot_node = sb("slot_node", [P, n_tiles], I32)
        src_row = sb("src_row", [P, n_tiles], I32)
        dst_row = sb("dst_row", [P, n_tiles], I32)
        cont = sb("cont", [P, n_tiles])
        single = sb("single", [P, n_tiles])
        coef = sb("coef", [P, 3, n_tiles])
        self_coef = sb("self_coef", [P, 2, n_tiles])
        ew = sb("ew", [P, 3, n_tiles])
        ew_mean = sb("ew_mean", [P, 3])
        keep = sb("keep", [rq, 2, ROW])
        pen = sb("pen", [rq, 2, ROW])
        keep2 = sb("keep2", [4, 2, rq])
        pen2 = sb("pen2", [4, 2, rq])
        seg_f = sb("seg_f", [rq, 4, ROW])
        seg_b = sb("seg_b", [rq, 4, ROW])
        seg_t = sb("seg_t", [rq, 4])
        seg_s = sb("seg_s", [4, rq])
        seg_c = sb("seg_c", [4, rq])
        bank = [ctx.enter_context(nc.psum_tensor(f"bank{k}", [P, 512], F32)) for k in range(8)]

        def segments(dve, ch, pe_sem, tr_sem, cnt, what, val, first):
            neutral = 0.0 if what == "sum" else -FAR
            ops = (ALU.mult, ALU.add) if what == "sum" else (ALU.add, ALU.max)
            src, src2 = (keep, keep2) if what == "sum" else (pen, pen2)
            for d, out in ((0, seg_f), (1, seg_b)):
                rev = slice(None, None, -1) if d else slice(None)
                for h in range(4):
                    ins = nc.vector.tensor_tensor_scan(out[:, h, rev], src[:, d, rev], val[:, h, rev],
                                                       neutral, *ops)
                ch.step(ins)
                edge = 0 if d else ROW - 1
                nc.vector.tensor_copy(seg_t[:, :], out[:, :, edge]).then_inc(pe_sem, 1)
                cnt[0] += 1
                dve.wait_ge(tr_sem, cnt[0])
                ch.step(nc.vector.tensor_tensor_scan(seg_s[:, rev], src2[:, d, rev],
                                                     bank[0][0:4, 0:rq][:, rev], neutral, *ops))
                ch.step(nc.vector.memset(seg_c[:, :], neutral))
                if d:
                    ins = nc.vector.tensor_copy(seg_c[:, 0:rq - 1], seg_s[:, 1:rq])
                else:
                    ins = nc.vector.tensor_copy(seg_c[:, 1:rq], seg_s[:, 0:rq - 1])
                ins.then_inc(pe_sem, 1)
                cnt[0] += 1
                dve.wait_ge(tr_sem, cnt[0])
                ch.step(nc.vector.tensor_copy(seg_t[:, :], bank[1][0:rq, 0:4]))
                for h in range(4):
                    ins = nc.vector.tensor_tensor_scan(out[:, h, rev], src[:, d, rev], val[:, h, rev],
                                                       seg_t[:, h:h + 1], *ops)
                ch.step(ins)
            if what == "sum":
                ch.step(nc.vector.tensor_tensor(seg_f[:, :, :], seg_f[:, :, :], seg_b[:, :, :], ALU.add))
                ch.step(nc.vector.tensor_tensor(seg_f[:, :, :], seg_f[:, :, :], val[:, :, :], ALU.subtract))
            else:
                ch.step(nc.vector.tensor_tensor(seg_f[:, :, :], seg_f[:, :, :], seg_b[:, :, :], ALU.max))

        def segments_pe(pe, pe_sem, tr_sem, cnt):
            for d in range(2):
                cnt[0] += 1
                pe.wait_ge(pe_sem, cnt[0])
                nc.tensor.transpose(bank[0][0:4, 0:rq], seg_t[:, :], ident[0:rq, 0:rq]).then_inc(tr_sem, 1)
                cnt[0] += 1
                pe.wait_ge(pe_sem, cnt[0])
                nc.tensor.transpose(bank[1][0:rq, 0:4], seg_c[:, :], ident[0:4, 0:4]).then_inc(tr_sem, 1)

        def edge_structure():
            with ExitStack() as c, Semaphores(nc) as sem:
                def s(name, shape, dt=F32):
                    return c.enter_context(nc.sbuf_tensor(name, shape, dt))

                di = s("di", [rq, 3, ROW], I32)
                df = s("df", [rq, 3, ROW])
                val = s("val", [rq, 4, ROW])
                pos = s("pos", [rq, ROW])
                tst = s("tst", [rq, ROW])
                isl = s("isl", [rq, ROW])
                nst = s("nst", [rq, ROW])
                kr = s("kr", [rq, ROW])
                sr = s("sr", [rq, ROW])
                fl = s("fl", [rq, 4])
                wf = s("wf", [rq, 2, 4])
                fb = s("fb", [rq, 4, P])
                ea = s("ea", [P, 8, DE])
                prod = s("prod", [P, 3, 8, DE])
                wet = s("wet", [DE, 3, D])
                wbar = s("wbar", [DE, 3])
                wb = s("wb", [DE, 3, P])
                wrow = s("wrow", [P, 3, DE])
                bem = s("bem", [P, 3, D])
                be1 = s("be1", [P, 3])
                ones = s("ones", [P, P])
                ewc = s("ewc", [P, 3, 8])
                map_new = s("map_new", [P, n_tiles, 4])
                map_def = s("map_def", [P, n_rows_nodes // P, 4])
                wp = s("wp", [P, n_tiles])
                loaded, chain, to_pe, turned, pe_done = (sem(x) for x in (
                    "loaded", "chain", "to_pe", "turned", "pe_done"))
                ea_in, ea_used, map_out, iotas, gather_go, deg_ready = (sem(x) for x in (
                    "ea_in", "ea_used", "map_out", "iotas", "gather_go", "deg_ready"))
                n_load = 10
                with nc.Block() as block:
                    @block.sync
                    def _(sp):
                        v = io["dst3"]
                        for k in range(3):
                            sp.dma_start(di[:, k, :], v[k]).then_inc(loaded, 16)
                        sp.dma_start(val[:, 0, :], io["w_rows"]).then_inc(loaded, 16)
                        sp.dma_start(wp[:, :], io["w_part"]).then_inc(loaded, 16)
                        sp.dma_start(pos[:, :], io["pos"][0:rq, :]).then_inc(loaded, 16)
                        sp.dma_start(ident[:, :], io["ident"]).then_inc(loaded, 16)
                        sp.dma_start(iota[:, :], io["iota"]).then_inc(loaded, 16)
                        sp.dma_start(wet[:, :, :], io["L0_gnn_We"].rearrange("l e h -> e l h")).then_inc(loaded, 16)
                        sp.dma_start(bem[:, :, :], io["be_all"]).then_inc(loaded, 16)
                        sp.dma_start(raw[n_slots:, :].rearrange("(p r) d -> p (r d)", p=P),
                                     io["x"].rearrange("(p r) d -> p (r d)", p=P)).then_inc(map_out, 16)
                        with sp.Fori(0, n_tiles // 8, 1) as i:
                            sp.wait_ge(ea_used, i + 1)
                            sp.dma_start(ea[:, :, :].rearrange("p a b -> p (a b)"),
                                         io["ea"][:, bass.ds(i * (8 * DE), 8 * DE)]).then_inc(ea_in, 16)
                        sp.wait_ge(iotas, 3)
                        sp.dma_start(row_map.rearrange("(p r) f -> p (r f)", p=P),
                                     map_def[:, :, :].rearrange("p r f -> p (r f)")).then_inc(map_out, 16)
                        sp.wait_ge(map_out, 32)

                    @block.gpsimd
                    def _(pool):
                        nr = n_rows_nodes // P
                        nc.gpsimd.memset(map_def[:, :, 1:4], 1.0).then_inc(iotas, 1)
                        nc.gpsimd.iota(map_def[:, :, 0], [[1, nr]], n_slots, nr,
                                       allow_small_or_imprecise_dtypes=True).then_inc(iotas, 1)
                        nc.gpsimd.iota(map_new[:, :, 0].rearrange("p (b g) -> p b g", g=GB),
                                       [[P * GB, nb], [1, GB]], 0, GB,
                                       allow_small_or_imprecise_dtypes=True).then_inc(iotas, 1)

                    @block.tensor
                    def _(pe):
                        cnt = [0]
                        pe.wait_ge(loaded, 16 * n_load)
                        for _i in range(2):
                            cnt[0] += 1
                            pe.wait_ge(to_pe, cnt[0])
                            nc.tensor.transpose(bank[2 + _i][0:4, 0:rq], wf[:, _i, :],
                                                ident[0:rq, 0:rq]).then_inc(turned, 1)
                        cnt[0] += 1
                        pe.wait_ge(to_pe, cnt[0])
                        for j in range(2):
                            nc.tensor.transpose(bank[4][:, j * rq:(j + 1) * rq], kr[:, j * P:(j + 1) * P],
                                                ident[0:rq, 0:rq])
                            nc.tensor.transpose(bank[5][:, j * rq:(j + 1) * rq], sr[:, j * P:(j + 1) * P],
                                                ident[0:rq, 0:rq])
                        for k in range(4):
                            ins = nc.tensor.matmul(bank[6][:, k * rq:(k + 1) * rq], fb[:, k, :],
                                                   ident[0:rq, 0:rq], start=True, stop=True)
                        ins.then_inc(turned, 1)
                        segments_pe(pe, to_pe, turned, cnt)
                        cnt[0] += 1
                        pe.wait_ge(to_pe, cnt[0])
                        for k in range(2):
                            for j in range(2):
                                ins = nc.tensor.transpose(bank[2][:, (2 * k + j) * rq:(2 * k + j + 1) * rq],
                                                          seg_f[:, k, j * P:(j + 1) * P], ident[0:rq, 0:rq])
                        ins.then_inc(turned, 1)
                        cnt[0] += 1
                        pe.wait_ge(to_pe, cnt[0])
                        for k in range(3):
                            ins = nc.tensor.matmul(bank[3][:, k * DE:(k + 1) * DE], wb[:, k, :],
                                                   ident[0:DE, 0:DE], start=True, stop=True)
                        ins.then_inc(turned, 1)
                        cnt[0] += 1
                        pe.wait_ge(to_pe, cnt[0])
                        nc.tensor.matmul(bank[7][:, 0:3], ones[:, :], ewc[:, :, 0], start=True,
                                         stop=True).then_inc(turned, 1)

                    @block.vector
                    def _(dve):
                        ch = Chain(dve, chain)
                        cnt = [0]
                        dve.sem_inc(ea_used, 1)
                        st = ch.step
                        dve.wait_ge(loaded, 16 * n_load)
                        st(nc.vector.tensor_copy(df[:, :, :], di[:, :, :]))
                        st(nc.vector.memset(eps[:, :], EPS))
                        st(nc.vector.memset(ones[:, :], 1.0))
                        st(nc.vector.tensor_tensor(keep[:, 0, :], df[:, 1, :], df[:, 0, :], ALU.is_equal))
                        st(nc.vector.tensor_tensor(keep[:, 1, :], df[:, 1, :], df[:, 2, :], ALU.is_equal))
                        st(nc.vector.tensor_scalar(pen[:, :, :], keep[:, :, :], 1.0, FAR, ALU.subtract, ALU.mult))
                        st(nc.vector.tensor_reduce(fl[:, 0:2], keep[:, :, :], AX.X, ALU.min))
                        for d in range(2):
                            ins = nc.vector.tensor_scalar(wf[:, d, :], ones[0:rq, 0:4], fl[:, d:d + 1], None, ALU.mult)
                            st(ins)
                        dve.sem_inc(to_pe, 1)
                        dve.sem_inc(to_pe, 1)
                        cnt[0] += 2
                        dve.wait_ge(turned, cnt[0])
                        for d in range(2):
                            st(nc.vector.tensor_copy(keep2[:, d, :], bank[2 + d][0:4, 0:rq]))
                        st(nc.vector.tensor_scalar(pen2[:, :, :], keep2[:, :, :], 1.0, FAR, ALU.subtract, ALU.mult))
                        st(nc.vector.tensor_scalar(nst[:, :], keep[:, 0, :], 1.0, None, ALU.mult))
                        st(nc.vector.memset(nst[:, :].rearrange("q (j e) -> q j e", j=2)[:, :, 0], 0.0))
                        st(nc.vector.tensor_scalar(tst[:, :], nst[:, :], -1.0, 1.0, ALU.mult, ALU.add))
                        st(nc.vector.tensor_tensor(kr[:, :], tst[:, :], pos[:, :], ALU.mult))
                        st(nc.vector.tensor_tensor_scan(sr[:, :], nst[:, :], kr[:, :], 0.0, ALU.mult, ALU.add))
                        for j in range(2):
                            a = slice(j * P, (j + 1) * P)
                            st(nc.vector.tensor_scalar(isl[:, a], df[:, 1, a], df[:, 1, (j + 1) * P - 1:(j + 1) * P],
                                                       None, ALU.is_equal))
                        st(nc.vector.tensor_scalar(kr[:, :], sr[:, :], -1.0, P - 1.0, ALU.mult, ALU.add))
                        st(nc.vector.tensor_tensor(kr[:, :], kr[:, :], isl[:, :], ALU.mult))
                        st(nc.vector.tensor_tensor(kr[:, :], kr[:, :], sr[:, :], ALU.add))
                        for j in range(2):
                            st(nc.vector.tensor_copy(fl[:, j:j + 1], keep[:, 0, j * P:j * P + 1]))
                            st(nc.vector.tensor_tensor(fl[:, 2 + j:3 + j], fl[:, j:j + 1], isl[:, j * P:j * P + 1], ALU.mult))
                        for k in range(4):
                            st(nc.vector.tensor_scalar(fb[:, k, :], ones[0:rq, :], fl[:, k:k + 1], None, ALU.mult))
                        st(nc.vector.tensor_scalar(isl[:, :], isl[:, :], -1.0, 1.0, ALU.mult, ALU.add))
                        st(nc.vector.tensor_tensor(tst[:, :], tst[:, :], isl[:, :], ALU.mult))
                        last = tst[:, :].rearrange("q (j e) -> q j e", j=2)[:, :, P - 1]
                        st(nc.vector.tensor_scalar(last, keep[:, 1, :].rearrange("q (j e) -> q j e", j=2)[:, :, P - 1],
                                                   -1.0, 1.0, ALU.mult, ALU.add))
                        st(nc.vector.tensor_scalar(sr[:, :], df[:, 1, :], BIG, None, ALU.subtract))
                        st(nc.vector.tensor_tensor(sr[:, :], sr[:, :], tst[:, :], ALU.mult))
                        st(nc.vector.tensor_scalar(sr[:, :], sr[:, :], BIG, None, ALU.add))
                        dve.sem_inc(to_pe, 1)
                        cnt[0] += 1
                        dve.wait_ge(turned, cnt[0])

                        def parts(t):
                            return t.rearrange("p (q j) -> p j q", j=2)
                        st(nc.vector.tensor_copy(parts(key[:, :]), bank[4][:, 0:2 * rq].rearrange("p (j q) -> p j q", j=2)))
                        st(nc.vector.tensor_copy(parts(slot_node[:, :]), bank[5][:, 0:2 * rq].rearrange("p (j q) -> p j q", j=2)))
                        st(nc.vector.tensor_copy(parts(cont[:, :]), bank[6][:, 0:2 * rq].rearrange("p (j q) -> p j q", j=2)))
                        st(nc.vector.tensor_copy(parts(single[:, :]), bank[6][:, 2 * rq:4 * rq].rearrange("p (j q) -> p j q", j=2)))
                        st(nc.vector.memset(val[:, 1, :], 1.0))
                        st(nc.vector.memset(val[:, 2:4, :], 0.0))
                        segments(dve, ch, to_pe, turned, cnt, "sum", val, True)
                        dve.sem_inc(to_pe, 1)
                        cnt[0] += 1
                        dve.wait_ge(turned, cnt[0])
                        dve.wait_ge(iotas, 3)
                        for k in range(2):
                            st(nc.vector.tensor_scalar(parts(map_new[:, :, 1 + k]),
                                                       bank[2][:, 2 * k * rq:(2 * k + 2) * rq].rearrange("p (j q) -> p j q", j=2),
                                                       1.0, None, ALU.add))
                        st(nc.vector.memset(map_new[:, :, 3], 1.0))
                        st(nc.vector.tensor_reduce(wbar[:, :], wet[:, :, :], AX.X, ALU.add))
                        for k in range(3):
                            st(nc.vector.tensor_scalar(wb[:, k, :], ones[0:DE, :], wbar[:, k:k + 1], 1.0 / D, ALU.mult, ALU.mult))
                        dve.sem_inc(to_pe, 1)
                        cnt[0] += 1
                        dve.wait_ge(turned, cnt[0])
                        st(nc.vector.tensor_copy(wrow[:, :, :].rearrange("p a b -> p (a b)"), bank[3][:, 0:3 * DE]))
                        st(nc.vector.tensor_reduce(be1[:, :], bem[:, :, :], AX.X, ALU.add))
                        st(nc.vector.tensor_scalar(be1[:, :], be1[:, :], 1.0 / D, None, ALU.mult))
                        ch2 = Chain(dve, gather_go, 2)
                        with dve.Fori(0, n_tiles // 8, 1) as i:
                            ch2.begin(Turn(i, 0, 1))
                            dve.wait_ge(ea_in, i * 16 + 16)
                            for k in range(3):
                                ins = nc.vector.tensor_tensor(prod[:, k, :, :], ea[:, :, :],
                                                              wrow[:, k:k + 1, :].to_broadcast([P, 8, DE]), ALU.mult)
                            ch2.step(ins)
                            ch2.step(nc.vector.tensor_reduce(ewc[:, :, :], prod[:, :, :, :], AX.X, ALU.add))
                            nc.vector.tensor_copy(ew[:, :, bass.ds(i * 8, 8)], ewc[:, :, :]).then_inc(ea_used, 1)
                        dve.wait_ge(ea_used, n_tiles // 8 + 1)
                        st(nc.vector.tensor_reduce(ewc[:, :, 0], ew[:, :, :], AX.X, ALU.add))
                        for k in range(3):
                            st(nc.vector.tensor_scalar(ew[:, k, :], ew[:, k, :], be1[:, k:k + 1], None, ALU.add))
                        dve.sem_inc(to_pe, 1)
                        cnt[0] += 1
                        dve.wait_ge(turned, cnt[0])
                        st(nc.vector.scalar_tensor_tensor(ew_mean[:, :], bank[7][:, 0:3], 1.0 / n_edges, be1[:, :],
                                                          ALU.mult, ALU.add))
                got = [s(f"got{k}", [P, 4]) for k in range(GB)]
                put = [s(f"put{k}", [P, 4]) for k in range(GB)]
                back = [s(f"back{k}", [P, 4, D]) for k in range(1)][0]
                ids = s("ids", [P, GB], I32)
                src_i = s("src_i", [P, n_tiles], I32)
                dst_i = s("dst_i", [P, n_tiles], I32)
                ends = s("ends", [P, 2, n_tiles, 4])
                pace, idc, taken, raw_out, in2, d3 = (sem(x) for x in ("pace", "idc", "taken", "raw_out", "in2", "d3"))
                sc_done, lk, raw_ready = (ctx.enter_context(nc.semaphore(x)) for x in ("sc_done", "lk", "raw_ready"))
                deg2 = sem("deg2")
                with nc.Block() as block:
                    @block.sync
                    def _(sp):
                        sp.dma_start(src_i[:, :], io["src_part"]).then_inc(in2, 16)
                        sp.dma_start(dst_i[:, :], io["dst_part"]).then_inc(in2, 16)
                        with sp.Fori(0, nb, 1) as i:
                            sp.wait_ge(raw_ready, i * 64 + 64)
                            sp.dma_start(batch_rows(raw, i), back[:, :, :].rearrange("p g d -> p (g d)")).then_inc(raw_out, 16)
                        sp.wait_ge(raw_out, 16 * nb + 16)

                    @block.gpsimd
                    def _(pool):
                        pool.sem_inc(raw_out, 16)
                        skip = nc.gpsimd.to_reg(n_rows_nodes - 1)
                        with pool.Fori(0, nb, 1) as i:
                            for k in range(GB):
                                nc.gpsimd.tensor_copy(put[k][:, :], map_new[:, bass.ds(i * GB + k, 1), :].rearrange("p a f -> p (a f)"))
                            nc.gpsimd.tensor_copy(ids[:, :], slot_node[:, bass.ds(i * GB, GB)]).then_inc(idc, 1)
                            pool.wait_ge(idc, i + 1)
                            pool.sem_inc(pace, 1)
                            for k in range(GB):
                                nc.gpsimd.indirect_dma_start(
                                    out=row_map, out_offset=bass.IndirectOffsetOnAxis(ap=ids[:, k:k + 1], axis=0),
                                    in_=put[k][:, :], in_offset=None, bounds_check=skip,
                                    oob_is_err=False).then_inc(sc_done, 16)
                            pool.wait_ge(sc_done, i * 64 + 64)
                            pool.sem_inc(pace, 1)
                        pool.wait_ge(in2, 32)
                        for e, idx in enumerate((src_i, dst_i)):
                            with pool.Fori(0, nb, 1) as i:
                                pool.wait_ge(taken, i * GB + (e * GB * nb + 1))
                                pool.sem_inc(pace, 1)
                                nc.gpsimd.tensor_copy(ids[:, :], idx[:, bass.ds(i * GB, GB)]).then_inc(idc, 1)
                                pool.wait_ge(idc, i + (nb * (e + 1) + 1))
                                pool.sem_inc(pace, 1)
                                for k in range(GB):
                                    nc.gpsimd.indirect_dma_start(
                                        out=got[k][:, :], out_offset=None, in_=row_map,
                                        in_offset=bass.IndirectOffsetOnAxis(ap=ids[:, k:k + 1], axis=0)).then_inc(lk, 16)
                        pool.wait_ge(taken, 2 * GB * nb + 1)
                        with pool.Fori(0, nb, 1) as i:
                            pool.wait_ge(raw_out, i * 16 + 16)
                            pool.sem_inc(pace, 1)
                            nc.gpsimd.tensor_copy(ids[:, :], dst_i[:, bass.ds(i * GB, GB)]).then_inc(idc, 1)
                            pool.wait_ge(idc, i + (nb * 3 + 1))
                            pool.sem_inc(pace, 1)
                            for k in range(GB):
                                nc.gpsimd.indirect_dma_start(
                                    out=back[:, k, :], out_offset=None, in_=io["x"],
                                    in_offset=bass.IndirectOffsetOnAxis(ap=ids[:, k:k + 1], axis=0)).then_inc(raw_ready, 16)

                    @block.vector
                    def _(dve):
                        dve.sem_inc(taken, 1)
                        for e in range(2):
                            with dve.Fori(0, nb, 1) as i:
                                dve.wait_ge(lk, i * 64 + (e * 64 * nb + 64))
                                for k in range(GB):
                                    nc.vector.tensor_copy(ends[:, e, bass.ds(i * GB + k, 1), :].rearrange("p a f -> p (a f)"),
                                                          got[k][:, :]).then_inc(taken, 1)
                        ch = Chain(dve, d3)
                        st = ch.step
                        dve.wait_ge(taken, 2 * GB * nb + 1)
                        st(nc.vector.tensor_copy(src_row[:, :], ends[:, 0, :, 0]))
                        st(nc.vector.tensor_copy(dst_row[:, :], ends[:, 1, :, 0]))
                        st(nc.vector.tensor_scalar(ends[:, :, :, 3], ends[:, :, :, 1], 0.0, None, ALU.is_gt))
                        st(nc.vector.tensor_tensor(ends[:, :, :, 1], ends[:, :, :, 1], ends[:, :, :, 3], ALU.mult))
                        st(nc.vector.scalar_tensor_tensor(ends[:, :, :, 1], ends[:, :, :, 1], 1.0, ends[:, :, :, 3], ALU.add, ALU.subtract))
                        st(nc.vector.tensor_scalar(coef[:, 2, :], ends[:, 1, :, 2], 1.0, 1.0, ALU.subtract, ALU.max))
                        st(nc.vector.reciprocal(coef[:, 2, :], coef[:, 2, :]))
                        dve.sem_inc(deg2, 1)
                        dve.wait_ge(deg2, 2)
                        st(nc.vector.reciprocal(ends[:, :, :, 1:3], ends[:, :, :, 1:3]))
                        st(nc.vector.tensor_tensor(ends[:, :, :, 1], ends[:, :, :, 1], ends[:, :, :, 3], ALU.mult))
                        for k in range(2):
                            st(nc.vector.tensor_tensor(coef[:, k, :], ends[:, 0, :, 1 + k], ends[:, 1, :, 1 + k], ALU.mult))
                            st(nc.vector.tensor_tensor(self_coef[:, k, :], ends[:, 1, :, 1 + k], ends[:, 1, :, 1 + k], ALU.mult))
                        st(nc.vector.tensor_tensor(coef[:, 0, :], coef[:, 0, :], wp[:, :], ALU.mult))

                    @block.scalar
                    def _(act):
                        act.wait_ge(deg2, 1)
                        nc.scalar.sqrt(ends[:, :, :, 1:3], ends[:, :, :, 1:3]).then_inc(deg2, 1)

        edge_structure()

        x_in = [[sb(f"x_in{u}_{r}", [P, GB, D]) for r in range(2)] for u in range(3)]
        x_res = [[sb(f"x_res{u}_{r}", [P, GB, D]) for r in range(2)] for u in range(3)]
        y = [[sb(f"y{u}_{r}", [P, GB, D]) for r in range(2)] for u in range(3)]
        x_turned = [sb(f"x_turned{u}", [P, GB, P]) for u in range(3)]
        got = [[sb(f"got_{r}_{k}", [P, D]) for k in range(2 * GB)] for r in range(2)]
        ids = [sb(f"ids_{r}", [P, 2, GB], I32) for r in range(2)]
        pick = [sb(f"pick{k}", [P, HEADS, P]) for k in range(2)]
        own = [sb(f"own{k}", [P, HEADS, P]) for k in range(2)]
        agg = [sb(f"agg{k}", [P, HEADS, P]) for k in range(2)]
        tail = [sb(f"tail{k}", [P, HEADS]) for k in range(2)]
        now = sb("now", [P, 3, GB])
        now_coef = sb("now_coef", [P, GB, HEADS])
        stat6 = [[sb(f"stat6_{u}_{r}", [P, GB, 6]) for r in range(2)] for u in range(3)]
        stat = [[sb(f"stat_{u}_{r}", [P, GB, 2]) for r in range(2)] for u in range(3)]
        dev = [[sb(f"dev_{u}_{r}", [P, GB]) for r in range(2)] for u in range(3)]
        shift = [[sb(f"shift_{u}_{r}", [P, GB]) for r in range(2)] for u in range(3)]
        own_coef = [sb(f"own_coef{r}", [P, GB, HEADS]) for r in range(2)]
        w_slot = sb("w_slot", [P, HEADS, D])
        w_node = sb("w_node", [P, D])
        w_att = sb("w_att", [P, 3 * HEADS])
        att = sb("att", [P, 2, HEADS, D])
        att_p = sb("att_p", [P, 2, HEADS, D])
        affine = sb("affine", [P, 3, D])
        att_s = sb("att_s", [P, n_tiles, HEADS])
        att_d = sb("att_d", [P, n_tiles, 2 * HEADS])

        def load_weights(parts, scale_heads):
            with Semaphores(nc) as sem:
                w_in, w_chain = sem("w_in"), sem("w_chain")
                with nc.Block() as block:
                    @block.sync
                    def _(sp):
                        for dst, src in parts:
                            sp.dma_start(dst, src).then_inc(w_in, 16)
                        sp.wait_ge(w_in, 16 * len(parts))

                    @block.vector
                    def _(dve):
                        st = Chain(dve, w_chain).step
                        dve.wait_ge(w_in, 16 * len(parts))
                        if scale_heads:
                            for k in range(2):
                                st(nc.vector.tensor_tensor(att_p[:, k, :, :], w_slot[:, :, :], att[:, k, :, :], ALU.mult))
                            st(nc.vector.tensor_reduce(w_att[:, HEADS:], att_p[:, :, :, :].rearrange("p k h d -> p (k h) d"),
                                                       AX.X, ALU.add))
                            st(nc.vector.tensor_copy(w_att[:, 0:HEADS], w_att[:, HEADS:2 * HEADS]))
                            st(nc.vector.tensor_scalar(w_slot[:, :, :], w_slot[:, :, :], 1.0 / HEADS, None, ALU.mult))
                            st(nc.vector.tensor_tensor(att_p[:, 0, 0:2, :], w_slot[:, 0:2, :], w_slot[:, 2:4, :], ALU.add))
                            st(nc.vector.tensor_tensor(w_node[:, :], att_p[:, 0, 0, :], att_p[:, 0, 1, :], ALU.add))

        def rows_pass(slots, nodes, scores, inp, out, res, post, mode):
            us = ([1, 2] if nodes else []) + ([0] if slots else [])
            edges = slots and mode != "own"
            blocks = {"gat": HEADS, "sage": 2}[mode] if mode in ("gat", "sage") else 1
            summed = HEADS if mode == "gat" else 1
            with_res = post in ("norm", "gat_end")
            n_stat = {"relu": 0, "norm": 1, "gat": 1, "gat_end": 2}[post]
            gat = post in ("gat", "gat_end")
            with Semaphores(nc) as sem:
                def sems(name):
                    return [sem(f"{name}{u}") for u in range(3)]
                def rings(name):
                    return [[sem(f"{name}{u}_{r}") for r in range(2)] for u in range(3)]
                x_loaded, res_loaded, stored = rings("x_loaded"), rings("res_loaded"), rings("stored")
                turned, turned_out, y_ready, y_taken = sems("turned"), sems("turned_out"), sems("y_ready"), sems("y_taken")
                stat_ready, dev_ready, scale_ready = sems("stat_ready"), sems("dev_ready"), sems("scale_ready")
                normed, summed_up, done = sems("normed"), sems("summed_up"), sems("done")
                gathered = [ctx.enter_context(nc.semaphore(f"gathered{r}_{out.tensor.name}_{mode}_{int(slots)}")) for r in range(2)] if edges or scores else None
                picks_ready, own_ready, agg_ready, agg_out, agg_fixed, agg_used = (sem(x) for x in (
                    "picks_ready", "own_ready", "agg_ready", "agg_out", "agg_fixed", "agg_used"))
                sc_turned, sc_out, sc_ready, sc_taken = (sem(x) for x in ("sc_turned", "sc_out", "sc_ready", "sc_taken"))
                ids_ready, pool_pace, dve_pace, dve_chain, dve_start, act_chain = (sem(x) for x in (
                    "ids_ready", "pool_pace", "dve_pace", "dve_chain", "dve_start", "act_chain"))
                AHEAD = 6

                def tail_bank(b):
                    return bank[2 + b][:, 0:HEADS] if mode == "gat" else bank[b][:, 2 * P:2 * P + 1]

                def table_batch(t, u, turn):
                    b = turn.batch()
                    return batch_rows(t, b if u == 0 else b * 2 + (nb + u - 1))

                with nc.Block() as block:
                    @block.sync
                    def _(sp):
                        def load(u, turn):
                            r = turn.half
                            sp.dma_start(x_in[u][r][:, :, :].rearrange("p g d -> p (g d)"),
                                         table_batch(inp, u, turn)).then_inc(x_loaded[u][r], 16)
                            if with_res:
                                sp.dma_start(x_res[u][r][:, :, :].rearrange("p g d -> p (g d)"),
                                             table_batch(res, u, turn)).then_inc(res_loaded[u][r], 16)

                        def store(u, turn):
                            sp.wait_ge(done[u], turn.count(1, 1))
                            sp.dma_start(table_batch(out, u, turn),
                                         y[u][turn.half][:, :, :].rearrange("p g d -> p (g d)")).then_inc(stored[u][turn.half], 16)
                        for half in range(2):
                            for u in us:
                                load(u, Turn(0, half))
                        with sp.Fori(0, nb // 2 - 1, 1) as i:
                            for half in range(2):
                                for u in us:
                                    store(u, Turn(i, half))
                                    load(u, Turn(i + 1, half))
                        for half in range(2):
                            for u in us:
                                store(u, Turn(nb // 2 - 1, half))
                        for u in us:
                            for half in range(2):
                                sp.wait_ge(stored[u][half], 8 * nb + 16)

                    @block.gpsimd
                    def _(pool):
                        for u in us:
                            for half in range(2):
                                pool.sem_inc(stored[u][half], 16)
                        if not (edges or scores):
                            return
                        with pool.Fori(0, nb // 2, 1) as i:
                            for half in range(2):
                                turn = Turn(i, half)
                                if scores:
                                    pool.wait_ge(sc_turned, turn.count(1, 1))
                                else:
                                    pool.wait_ge(agg_ready, turn.count(GB, AHEAD - GB))
                                pool.sem_inc(pool_pace, 1)
                                nc.gpsimd.tensor_copy(ids[half][:, 0, :], src_row[:, bass.ds(turn.batch() * GB, GB)])
                                nc.gpsimd.tensor_copy(ids[half][:, 1, :], dst_row[:, bass.ds(turn.batch() * GB, GB)]).then_inc(ids_ready, 1)
                                pool.wait_ge(ids_ready, turn.count(1, 1))
                                pool.sem_inc(pool_pace, 1)
                                for e in range(2 if scores else 1):
                                    for k in range(GB):
                                        nc.gpsimd.indirect_dma_start(
                                            out=got[half][e * GB + k][:, :], out_offset=None, in_=inp,
                                            in_offset=bass.IndirectOffsetOnAxis(ap=ids[half][:, e, k:k + 1], axis=0)
                                        ).then_inc(gathered[half], 16)

                    @block.tensor
                    def _(pe):
                        if scores:
                            pe.sem_inc(sc_turned, 2)
                        if edges:
                            pe.sem_inc(agg_ready, AHEAD)
                            pe.sem_inc(y_ready[0], 1)

                        def turn_rows(u, turn):
                            pe.wait_ge(x_loaded[u][turn.half], turn.i * 16 + 16)
                            for g in range(GB):
                                ins = nc.tensor.transpose(bank[2 + u][:, g * P:(g + 1) * P], x_in[u][turn.half][:, g, :], ident[:, :])
                            ins.then_inc(turned[u], 1)

                        def product(u, turn):
                            pe.wait_ge(turned_out[u], turn.count(1, 1))
                            pe.wait_ge(y_taken[u], turn.count(1, 1))
                            for g in range(GB):
                                ins = nc.tensor.matmul(bank[5 + u][:, g * D:(g + 1) * D], x_turned[u][:, g, :],
                                                       w_node[:, :], start=True, stop=True)
                            ins.then_inc(y_ready[u], 1)

                        def sum_edges(k, half, turn):
                            pe.wait_ge(gathered[half], turn.i * 64 + 64)
                            if k == 0:
                                pe.wait_ge(x_loaded[0][half], turn.i * 16 + 16)
                            pe.wait_ge(picks_ready, turn.count(GB, k + 1))
                            pe.wait_ge(agg_out, turn.count(GB, k + 1))
                            pe.wait_ge(agg_fixed, turn.count(GB, k + 1))
                            g, b = got[half][k], k % 2
                            nc.tensor.matmul(tail_bank(b), g[:, :], pick[b][:, 0:summed, P - 1],
                                             start=True, stop=True)
                            a = bank[b][:, 0:summed * P]
                            last = mode == "sage"
                            ins = nc.tensor.matmul(a, g[:, :], pick[b][:, 0:summed, :].rearrange("p h e -> p (h e)"),
                                                   start=True, stop=last)
                            if mode == "sage":
                                ins = nc.tensor.transpose(bank[b][:, P:2 * P], x_in[0][half][:, k, :], ident[:, :])
                            else:
                                pe.wait_ge(own_ready, turn.count(GB, k + 1))
                                ins = nc.tensor.matmul(a, x_in[0][half][:, k, :], own[b][:, 0:summed, :].rearrange("p h e -> p (h e)"),
                                                       start=False, stop=True)
                            ins.then_inc(agg_ready, 1)

                        def slot_product(k, turn):
                            pe.wait_ge(agg_fixed, turn.count(GB, k + 3))
                            if k == 0:
                                pe.wait_ge(y_taken[0], turn.count(1, 1))
                            for h in range(blocks):
                                ins = nc.tensor.matmul(bank[5][:, k * D:(k + 1) * D], agg[k % 2][:, h, :], w_slot[:, h, :],
                                                       start=(h == 0), stop=(h == blocks - 1))
                            if k == GB - 1:
                                ins.then_inc(y_ready[0], 1)
                            else:
                                ins.then_inc(agg_used, 1)

                        def score_rows(half, turn):
                            pe.wait_ge(gathered[half], turn.i * 128 + 128)
                            for e in range(2):
                                for g in range(GB):
                                    ins = nc.tensor.transpose(bank[e][:, g * P:(g + 1) * P], got[half][e * GB + g][:, :], ident[:, :])
                            ins.then_inc(sc_turned, 1)

                        def score_products(turn):
                            pe.wait_ge(sc_out, turn.count(2, 2))
                            pe.wait_ge(sc_taken, turn.count(1, 1))
                            for g in range(GB):
                                nc.tensor.matmul(bank[2][:, g * HEADS:(g + 1) * HEADS], agg[0][:, g, :], w_att[:, 0:HEADS],
                                                 start=True, stop=True)
                                ins = nc.tensor.matmul(bank[2][:, 16 + g * 8:24 + g * 8], agg[1][:, g, :], w_att[:, HEADS:],
                                                       start=True, stop=True)
                            ins.then_inc(sc_ready, 1)

                        with pe.Fori(0, nb // 2, 1) as i:
                            for half in range(2):
                                turn = Turn(i, half)
                                for u in us:
                                    if u or not edges:
                                        turn_rows(u, turn)
                                if nodes:
                                    product(1, turn)
                                    product(2, turn)
                                if scores:
                                    score_rows(half, turn)
                                    score_products(turn)
                                if edges:
                                    sum_edges(0, half, turn)
                                    sum_edges(1, half, turn)
                                    slot_product(0, turn)
                                    sum_edges(2, half, turn)
                                    slot_product(1, turn)
                                    sum_edges(3, half, turn)
                                    slot_product(2, turn)
                                    slot_product(3, turn)
                                elif slots:
                                    product(0, turn)

                    @block.scalar
                    def _(act):
                        if edges:
                            act.sem_inc(agg_out, 2)

                        def deviation(u, turn, n):
                            r = turn.half
                            act.wait_ge(stat_ready[u], turn.count(n_stat, n))
                            nc.scalar.activation(dev[u][r][:, :], stat[u][r][:, :, 1], ACT.Sqrt,
                                                 bias=eps[:, 0:1]).then_inc(dev_ready[u], 1)

                        def normalise(u, turn, n):
                            r = turn.half
                            act.wait_ge(scale_ready[u], turn.count(n_stat, n))
                            for g in range(GB):
                                ins = nc.scalar.activation(y[u][r][:, g, :], y[u][r][:, g, :], ACT.Identity,
                                                           bias=shift[u][r][:, g:g + 1], scale=dev[u][r][:, g:g + 1])
                            ins.then_inc(normed[u] if gat and n == 1 else done[u], 1)

                        def relu(u, turn, after, n):
                            act.wait_ge(after[u], turn.count(1, n))
                            yu = y[u][turn.half]
                            nc.scalar.activation(yu[:, :, :], yu[:, :, :], ACT.Relu).then_inc(done[u], 1)

                        def copy_rows(u, turn):
                            act.wait_ge(turned[u], turn.count(1, 1))
                            nc.scalar.copy(x_turned[u][:, :, :].rearrange("p g e -> p (g e)"),
                                           bank[2 + u][:, :]).then_inc(turned_out[u], 1)

                        def read_own(turn):
                            t = bass.ds(turn.batch() * GB, GB)
                            if mode == "gat":
                                ins = nc.scalar.copy(own_coef[turn.half][:, :, :], att_d[:, t, 0:HEADS])
                            else:
                                ins = nc.scalar.copy(own_coef[turn.half][:, :, 0], self_coef[:, int(mode[3]), t])
                            ins.then_inc(act_chain, 1)
                            act.wait_ge(act_chain, turn.count(1, 1))

                        def build_own(k, turn):
                            if mode == "sage":
                                return
                            act.wait_ge(agg_ready, turn.count(GB, AHEAD + k - 1))
                            for h in range(summed):
                                ins = nc.scalar.activation(own[k % 2][:, h, :], ident[:, :], ACT.Copy,
                                                           scale=own_coef[turn.half][:, k, h:h + 1])
                            ins.then_inc(own_ready, 1)

                        def copy_sums(k, turn):
                            act.wait_ge(agg_ready, turn.count(GB, AHEAD + k + 1))
                            if k < 2:
                                act.wait_ge(y_ready[0], turn.count(1, 1))
                            else:
                                act.wait_ge(agg_used, turn.count(GB - 1, k - 1))
                            nc.scalar.copy(agg[k % 2][:, 0:blocks, :].rearrange("p h e -> p (h e)"),
                                           bank[k % 2][:, 0:blocks * P]).then_inc(agg_out, 1)

                        def first(u, turn):
                            if post == "relu":
                                relu(u, turn, y_taken, 2)
                            else:
                                deviation(u, turn, 1)

                        def second(u, turn):
                            if n_stat:
                                normalise(u, turn, 1)

                        with act.Fori(0, nb // 2, 1) as i:
                            for half in range(2):
                                turn = Turn(i, half)
                                if edges:
                                    if mode != "sage":
                                        read_own(turn)
                                    build_own(0, turn)
                                    build_own(1, turn)
                                for u in us:
                                    if u or not edges:
                                        copy_rows(u, turn)
                                if scores:
                                    act.wait_ge(sc_turned, turn.count(1, 3))
                                    for e in range(2):
                                        nc.scalar.copy(agg[e][:, :, :].rearrange("p g e -> p (g e)"),
                                                       bank[e][:, :]).then_inc(sc_out, 1)
                                if edges:
                                    copy_sums(0, turn)
                                    build_own(2, turn)
                                if nodes:
                                    first(1, turn)
                                if edges:
                                    copy_sums(1, turn)
                                    build_own(3, turn)
                                if nodes:
                                    first(2, turn)
                                    second(1, turn)
                                if edges:
                                    copy_sums(2, turn)
                                if nodes:
                                    second(2, turn)
                                if edges:
                                    copy_sums(3, turn)
                                if slots:
                                    first(0, turn)
                                    second(0, turn)
                                if post == "gat":
                                    for u in us:
                                        relu(u, turn, summed_up, 1)
                                if post == "gat_end":
                                    for u in us:
                                        deviation(u, turn, 2)
                                    for u in us:
                                        normalise(u, turn, 2)

                    @block.vector
                    def _(dve):
                        for u in us:
                            dve.sem_inc(y_taken[u], 1)
                        if scores:
                            dve.sem_inc(sc_taken, 1)
                        per_u = {"relu": 0, "norm": 3, "gat": 4, "gat_end": 8}[post]
                        ch = Chain(dve, dve_chain, per_u * len(us) + (1 + 2 * GB if edges else 0))
                        if edges:
                            dve.sem_inc(agg_fixed, 2)
                            nc.vector.memset(tail[0][:, :], 0.0).then_inc(dve_start, 1)
                            dve.wait_ge(dve_start, 1)

                        def wide(k):
                            return affine[:, k:k + 1, :].to_broadcast([P, GB, D])

                        def statistics(u, r):
                            for g in range(GB):
                                ins = nc.vector.bn_stats(stat6[u][r][:, g, :], y[u][r][:, g, :])
                            ch.step(ins)
                            dve.sem_inc(dve_pace, 1)
                            for g in range(GB):
                                ins = nc.vector.bn_aggr(stat[u][r][:, g, :], stat6[u][r][:, g, :])
                            ins.then_inc(stat_ready[u], 1)

                        def residual(u, turn):
                            r = turn.half
                            dve.wait_ge(res_loaded[u][r], turn.i * 16 + 16)
                            ch.step(nc.vector.scalar_tensor_tensor(y[u][r][:, :, :], y[u][r][:, :, :], 0.0, x_res[u][r][:, :, :],
                                                                   ALU.max, ALU.add))
                            statistics(u, r)

                        def scale(u, turn, n):
                            r = turn.half
                            dve.wait_ge(dev_ready[u], turn.count(n_stat, n))
                            ch.step(nc.vector.reciprocal(dev[u][r][:, :], dev[u][r][:, :]))
                            nc.vector.scalar_tensor_tensor(shift[u][r][:, :], stat[u][r][:, :, 0], -1.0, dev[u][r][:, :],
                                                           ALU.mult, ALU.mult).then_inc(scale_ready[u], 1)

                        def take(u, turn):
                            r = turn.half
                            dve.wait_ge(y_ready[u], turn.count(1, 1 + (u == 0 and edges)))
                            dve.wait_ge(stored[u][r], turn.i * 16 + 16)
                            nc.vector.tensor_tensor(y[u][r][:, :, :], bank[5 + u][:, :].rearrange("p (g d) -> p g d", g=GB),
                                                    wide(0), ALU.add).then_inc(y_taken[u], 1)
                            if post == "relu":
                                return
                            dve.wait_ge(y_taken[u], turn.count(1, 2))
                            if post == "norm":
                                residual(u, turn)
                            else:
                                statistics(u, r)

                        def finish(u, turn):
                            yu = y[u][turn.half]
                            dve.wait_ge(normed[u], turn.count(1, 1))
                            ch.step(nc.vector.tensor_tensor(yu[:, :, :], yu[:, :, :], wide(1), ALU.mult))
                            ch.step(nc.vector.tensor_tensor(yu[:, :, :], yu[:, :, :], wide(2), ALU.add))
                            ins = nc.vector.tensor_tensor(yu[:, :, :], yu[:, :, :], x_in[u][turn.half][:, :, :], ALU.add)
                            if post == "gat":
                                ins.then_inc(summed_up[u], 1)
                                return
                            ch.step(ins)
                            residual(u, turn)

                        def read_now(turn):
                            t = bass.ds(turn.batch() * GB, GB)
                            nc.vector.tensor_copy(now[:, 0, :], key[:, t])
                            nc.vector.tensor_copy(now[:, 1, :], cont[:, t])
                            nc.vector.tensor_copy(now[:, 2, :], single[:, t])
                            if mode == "gat":
                                ins = nc.vector.tensor_copy(now_coef[:, :, :], att_s[:, t, :])
                            else:
                                m = 2 if mode == "sage" else int(mode[3])
                                ins = nc.vector.tensor_copy(now_coef[:, :, 0], coef[:, m, t])
                            ch.step(ins)

                        def build(k, turn):
                            dve.wait_ge(agg_ready, turn.count(GB, AHEAD + k - 1))
                            for h in range(summed):
                                ins = nc.vector.tensor_scalar(pick[k % 2][:, h, :], iota[:, :], now[:, 0, k:k + 1],
                                                              now_coef[:, k, h:h + 1], ALU.is_equal, ALU.mult)
                            ins.then_inc(picks_ready, 1)

                        def fix(k, turn):
                            dve.wait_ge(agg_out, turn.count(GB, k + 3))
                            t0, t1 = tail[k % 2], tail[(k + 1) % 2]
                            a = agg[k % 2]
                            ch.step(nc.vector.scalar_tensor_tensor(t1[:, 0:summed], t0[:, 0:summed], now[:, 2, k:k + 1],
                                                                   tail_bank(k % 2), ALU.mult, ALU.add))
                            ch.step(nc.vector.scalar_tensor_tensor(a[:, 0:summed, 0], t0[:, 0:summed], now[:, 1, k:k + 1],
                                                                   a[:, 0:summed, 0], ALU.mult, ALU.add))
                            nc.vector.scalar_tensor_tensor(a[:, 0:summed, P - 1], t0[:, 0:summed], now[:, 2, k:k + 1],
                                                           a[:, 0:summed, P - 1], ALU.mult, ALU.add).then_inc(agg_fixed, 1)
                            dve.wait_ge(agg_fixed, turn.count(GB, k + 3))

                        with dve.Fori(0, nb // 2, 1) as i:
                            for half in range(2):
                                turn = Turn(i, half)
                                ch.begin(turn)
                                if edges:
                                    read_now(turn)
                                    build(0, turn)
                                    build(1, turn)
                                if nodes:
                                    take(1, turn)
                                if edges:
                                    fix(0, turn)
                                    build(2, turn)
                                if nodes:
                                    if n_stat:
                                        scale(1, turn, 1)
                                    take(2, turn)
                                if edges:
                                    fix(1, turn)
                                    build(3, turn)
                                if nodes and n_stat:
                                    scale(2, turn, 1)
                                if edges:
                                    fix(2, turn)
                                if edges:
                                    fix(3, turn)
                                if scores:
                                    dve.wait_ge(sc_ready, turn.count(1, 1))
                                    t = bass.ds(turn.batch() * GB, GB)
                                    nc.vector.tensor_copy(att_s[:, t, :], bank[2][:, 0:16].rearrange("p (g h) -> p g h", g=GB))
                                    nc.vector.tensor_copy(att_d[:, t, :], bank[2][:, 16:48].rearrange("p (g h) -> p g h", g=GB)).then_inc(sc_taken, 1)
                                if slots:
                                    take(0, turn)
                                    if n_stat:
                                        scale(0, turn, 1)
                                if gat:
                                    for u in us:
                                        finish(u, turn)
                                if post == "gat_end":
                                    for u in us:
                                        scale(u, turn, 2)

        def softmax(layer):
            with ExitStack() as c, Semaphores(nc) as sem:
                lr = c.enter_context(nc.sbuf_tensor(f"lr_{layer}", [rq, 4, ROW], F32))
                sr = c.enter_context(nc.sbuf_tensor(f"own_r_{layer}", [rq, 4, ROW], F32))
                dr = c.enter_context(nc.sbuf_tensor(f"den_r_{layer}", [rq, 4, ROW], F32))
                tmp = c.enter_context(nc.sbuf_tensor(f"tmp_p_{layer}", [P, n_tiles, HEADS], F32))
                to_pe, turned, chain, exps = (sem(x) for x in ("to_pe", "turned", "chain", "exps"))
                with nc.Block() as block:
                    @block.scalar
                    def _(act):
                        act.wait_ge(exps, 1)
                        nc.scalar.activation(lr[:, :, :], lr[:, :, :], ACT.Exp)
                        nc.scalar.activation(sr[:, :, :], sr[:, :, :], ACT.Exp).then_inc(exps, 1)

                    @block.tensor
                    def _(pe):
                        cnt = [1]
                        pe.wait_ge(to_pe, 1)
                        for e, src in ((0, att_s), (1, tmp)):
                            for h in range(HEADS):
                                for j in range(2):
                                    ins = nc.tensor.transpose(bank[2 + 2 * e + h // 2][0:rq, ((h % 2) * 2 + j) * P:((h % 2) * 2 + j + 1) * P],
                                                              src[:, :, h].rearrange("p (q j) -> p j q", j=2)[:, j, :], ident[:, :])
                        ins.then_inc(turned, 1)
                        segments_pe(pe, to_pe, turned, cnt)
                        segments_pe(pe, to_pe, turned, cnt)
                        cnt[0] += 1
                        pe.wait_ge(to_pe, cnt[0])
                        for e, src in ((0, lr), (1, sr)):
                            for h in range(HEADS):
                                for j in range(2):
                                    ins = nc.tensor.transpose(bank[2 + 2 * e + h // 2][:, ((h % 2) * 2 + j) * rq:((h % 2) * 2 + j + 1) * rq],
                                                              src[:, h, j * P:(j + 1) * P], ident[0:rq, 0:rq])
                        ins.then_inc(turned, 1)

                    @block.vector
                    def _(dve):
                        st = Chain(dve, chain)
                        ch, st = st, st.step
                        cnt = [1]
                        vd = att_d[:, :, HEADS:]
                        st(nc.vector.tensor_tensor(att_s[:, :, :], att_s[:, :, :], vd, ALU.add))
                        st(nc.vector.tensor_tensor(tmp[:, :, :], att_d[:, :, 0:HEADS], vd, ALU.add))
                        for h in range(HEADS):
                            st(nc.vector.tensor_tensor(att_s[:, :, h], att_s[:, :, h], ew[:, layer, :], ALU.add))
                        st(nc.vector.tensor_scalar(tmp[:, :, :], tmp[:, :, :], ew_mean[:, layer:layer + 1], None, ALU.add))
                        st(nc.vector.scalar_tensor_tensor(att_s[:, :, :], att_s[:, :, :], SLOPE, att_s[:, :, :], ALU.mult, ALU.max))
                        nc.vector.scalar_tensor_tensor(tmp[:, :, :], tmp[:, :, :], SLOPE, tmp[:, :, :], ALU.mult, ALU.max).then_inc(to_pe, 1)
                        dve.wait_ge(turned, 1)
                        for e, dst in ((0, lr), (1, sr)):
                            for m in range(2):
                                st(nc.vector.tensor_copy(dst[:, 2 * m:2 * m + 2, :].rearrange("q h e -> q (h e)"),
                                                         bank[2 + 2 * e + m][0:rq, :]))
                        segments(dve, ch, to_pe, turned, cnt, "max", lr, False)
                        st(nc.vector.tensor_tensor(seg_f[:, :, :], seg_f[:, :, :], sr[:, :, :], ALU.max))
                        st(nc.vector.tensor_tensor(lr[:, :, :], lr[:, :, :], seg_f[:, :, :], ALU.subtract))
                        nc.vector.tensor_tensor(sr[:, :, :], sr[:, :, :], seg_f[:, :, :], ALU.subtract).then_inc(exps, 1)
                        dve.wait_ge(exps, 2)
                        segments(dve, ch, to_pe, turned, cnt, "sum", lr, False)
                        st(nc.vector.tensor_tensor(dr[:, :, :], seg_f[:, :, :], sr[:, :, :], ALU.add))
                        st(nc.vector.reciprocal(dr[:, :, :], dr[:, :, :]))
                        st(nc.vector.tensor_tensor(lr[:, :, :], lr[:, :, :], dr[:, :, :], ALU.mult))
                        nc.vector.tensor_tensor(sr[:, :, :], sr[:, :, :], dr[:, :, :], ALU.mult).then_inc(to_pe, 1)
                        cnt[0] += 1
                        dve.wait_ge(turned, cnt[0])
                        for e, dst in ((0, att_s), (1, att_d)):
                            for h in range(HEADS):
                                o = (h % 2) * 2 * rq
                                st(nc.vector.tensor_copy(dst[:, :, h].rearrange("p (q j) -> p j q", j=2),
                                                         bank[2 + 2 * e + h // 2][:, o:o + 2 * rq].rearrange("p (j q) -> p j q", j=2)))

        t = tables
        load_weights([(w_node[:, :], io["L0_gnn_W0"]), (affine[:, 0, :], io["b_L0_b0"])], False)
        rows_pass(True, True, False, raw, t[0], None, "relu", "own")
        for l in range(3):
            load_weights([(w_slot[:, :, :], io["L0_gnn_Wg"][l].rearrange("k (h d) -> k h d", h=HEADS)),
                          (att[:, :, :, :], io["b_att"][l]), (affine[:, :, :], io["b_affine"][l])], True)
            post, res = ("gat_end", raw) if l == 2 else ("gat", None)
            rows_pass(False, True, True, t[l], t[l + 1], res, post, "gat")
            softmax(l)
            rows_pass(True, False, False, t[l], t[l + 1], res, post, "gat")
        rest = [("L1_gnn_W1", "L1_gnn_b1", "gcn0", "relu", None), ("L1_gnn_W2", "L1_gnn_b2", "gcn0", "norm", 3),
                ("L2_gnn_W", "L2_gnn_b", "gcn1", "norm", 5), ("L3_gnn_W1", "L3_gnn_b1", "sage", "relu", None),
                ("L3_gnn_W2", "L3_gnn_b2", "sage", "norm", 6)]
        for n, (w, b, mode, post, res) in enumerate(rest):
            if mode == "sage":
                parts = [(w_slot[:, 0, :], io[w][D:, :]), (w_slot[:, 1, :], io[w][0:D, :]), (w_node[:, :], io[w][0:D, :])]
            else:
                parts = [(w_slot[:, 0, :], io[w]), (w_node[:, :], io[w])]
            load_weights(parts + [(affine[:, 0, :], io["b_" + b])], False)
            rows_pass(True, True, False, t[3 + n], t[4 + n], None if res is None else t[res], post, mode)
        placed = ctx.enter_context(nc.semaphore("placed"))
        with Semaphores(nc) as sem:
            copied, idc, pace, free = (sem(x) for x in ("copied", "idc", "pace", "free"))
            loaded = [sem(f"loaded{r}") for r in range(2)]
            with nc.Block() as block:
                @block.sync
                def _(sp):
                    sp.dma_start(io["out"].rearrange("(p r) d -> p (r d)", p=P),
                                 t[8][n_slots:, :].rearrange("(p r) d -> p (r d)", p=P)).then_inc(copied, 16)
                    with sp.Fori(0, nb // 2, 1) as i:
                        for half in range(2):
                            turn = Turn(i, half)
                            sp.wait_ge(free, turn.count(1, 1))
                            sp.dma_start(x_in[0][half][:, :, :].rearrange("p g d -> p (g d)"),
                                         batch_rows(t[8], turn.batch())).then_inc(loaded[half], 16)

                @block.gpsimd
                def _(pool):
                    skip = nc.gpsimd.to_reg(n_rows_nodes - 1)
                    pool.sem_inc(free, 2)
                    pool.wait_ge(copied, 16)
                    with pool.Fori(0, nb // 2, 1) as i:
                        for half in range(2):
                            turn = Turn(i, half)
                            nc.gpsimd.tensor_copy(ids[half][:, 0, :], slot_node[:, bass.ds(turn.batch() * GB, GB)]).then_inc(idc, 1)
                            pool.wait_ge(idc, turn.count(1, 1))
                            pool.sem_inc(pace, 1)
                            pool.wait_ge(loaded[half], i * 16 + 16)
                            pool.sem_inc(pace, 1)
                            for k in range(GB):
                                nc.gpsimd.indirect_dma_start(
                                    out=io["out"], out_offset=bass.IndirectOffsetOnAxis(ap=ids[half][:, 0, k:k + 1], axis=0),
                                    in_=x_in[0][half][:, k, :], in_offset=None, bounds_check=skip,
                                    oob_is_err=False).then_inc(placed, 16)
                        pool.wait_ge(placed, i * 128 + 128)
                        pool.sem_inc(free, 1)
                        pool.sem_inc(free, 1)


def kernel(**inputs):
    import numpy as _np
    import concourse.bacc as _bacc
    from concourse import mybir as _mybir
    from concourse.bass_utils import run_bass_kernel_spmd as _run

    a = {k: _np.asarray(v) for k, v in inputs.items()}
    n_nodes, n_edges = a["x"].shape[0], a["src"].shape[0]
    nb, n_slots, n_rows_nodes = sizes(n_nodes, n_edges)
    assert n_rows_nodes > n_nodes
    rq, n_tiles = n_slots // ROW, n_slots // P

    def padded(v, n, fill=0):
        w = _np.full((n,) + v.shape[1:], fill, v.dtype)
        w[:v.shape[0]] = v
        return w

    def part(v):
        return _np.ascontiguousarray(_np.moveaxis(v.reshape((n_tiles, P) + v.shape[1:]), 0, 1))

    def wide(v):
        return _np.ascontiguousarray(_np.broadcast_to(v, (P,) + v.shape))
    dst = padded(a["dst"], n_slots, n_nodes)
    around = _np.full(n_slots + 2, -1, dst.dtype)
    around[1:-1] = dst
    src = padded(a["src"], n_slots)
    w = padded(a["edge_weight"], n_slots)
    io = {
        "x": padded(a["x"], n_rows_nodes),
        "dst3": _np.stack([around[:-2], around[1:-1], around[2:]]).reshape(3, rq, ROW),
        "w_rows": w.reshape(rq, ROW), "w_part": part(w), "src_part": part(src), "dst_part": part(dst),
        "ea": part(padded(a["edge_attr_64"], n_slots)).reshape(P, n_tiles * DE),
        "ident": _np.eye(P, dtype=_np.float32),
        "iota": wide(_np.arange(P, dtype=_np.float32)),
        "pos": wide(_np.arange(ROW, dtype=_np.float32) % P),
        "L0_gnn_We": a["L0_gnn_We"], "be_all": wide(a["L0_gnn_be"]),
        "L0_gnn_W0": a["L0_gnn_W0"], "b_L0_b0": wide(a["L0_gnn_b0"]), "L0_gnn_Wg": a["L0_gnn_Wg"],
        "b_att": _np.stack([wide(_np.stack([a["L0_gnn_att_src"][l], a["L0_gnn_att_dst"][l]])) for l in range(3)]),
        "b_affine": _np.stack([wide(_np.stack([a["L0_gnn_" + k][l] for k in ("bg", "gamma", "beta")])) for l in range(3)]),
        "L1_gnn_W1": _np.ascontiguousarray(a["L1_gnn_W1"].T), "L1_gnn_W2": _np.ascontiguousarray(a["L1_gnn_W2"].T),
        "L2_gnn_W": a["L2_gnn_W"], "L3_gnn_W1": a["L3_gnn_W1"], "L3_gnn_W2": a["L3_gnn_W2"],
    }
    for k in ("L1_gnn_b1", "L1_gnn_b2", "L2_gnn_b", "L3_gnn_b1", "L3_gnn_b2"):
        io["b_" + k] = wide(a[k])
    nc = _bacc.Bacc("TRN2", target_bir_lowering=False, num_devices=1)
    arrays = {f"in_{k}_dram": _np.ascontiguousarray(v) for k, v in io.items()}
    aps = {k: nc.dram_tensor(f"in_{k}_dram", v.shape, _mybir.dt.from_np(v.dtype), kind="ExternalInput").ap()
           for k, v in io.items()}
    aps["out"] = nc.dram_tensor("out_0_dram", (n_rows_nodes, D), _mybir.dt.float32, kind="ExternalOutput").ap()
    program(nc, aps, n_nodes, n_edges)
    r = _run(nc, [arrays], core_ids=[0])
    return r.results[0]["out_0_dram"][:n_nodes]
```

```python
from contextlib import ExitStack

import concourse.bass as bass
from concourse import mybir

F32 = mybir.dt.float32
I32 = mybir.dt.int32
ALU = mybir.AluOpType
ACT = mybir.ActivationFunctionType
AX = mybir.AxisListType

P = 128
D = 128
DE = 64
HEADS = 4
GB = 4
BIG = 1.0e6
FAR = 1.0e30
EPS = 1e-5
SLOPE = 0.2
ROW = 256


def sizes(n_nodes, n_edges):
    nb = max(-(-n_edges // (P * GB)), -(-n_nodes // (2 * P * GB)))
    nb += nb % 2
    return nb, nb * GB * P, 2 * nb * GB * P


class Turn:

    def __init__(self, i, half, span=2):
        self.i, self.half, self.span = i, half, span

    def count(self, k, n):
        return self.i * (self.span * k) + (self.half * k + n)

    def batch(self):
        return self.i * self.span + self.half


class Chain:

    def __init__(self, eng, sem, per_turn=0):
        self.eng, self.sem, self.n, self.per_turn, self.turn = eng, sem, 0, per_turn, None

    def begin(self, turn):
        assert self.turn is None or self.n == self.per_turn, (self.n, self.per_turn)
        self.turn, self.n = turn, 0

    def step(self, ins):
        self.n += 1
        ins.then_inc(self.sem, 1)
        self.eng.wait_ge(self.sem, self.turn.count(self.per_turn, self.n) if self.turn else self.n)


class Semaphores:

    phases = 0

    def __init__(self, nc):
        self.nc, self.held = nc, []
        Semaphores.phases += 1

    def __enter__(self):
        return self

    def __call__(self, name):
        self.held.append(self.nc.alloc_semaphore(name=f"{name}_{Semaphores.phases}"))
        return self.held[-1]

    def __exit__(self, *failed):
        if failed[0] is None:
            self.nc.clear_and_free_semaphores(self.held)
            self.nc.all_engine_barrier()


def batch_rows(table, b):
    v = table.rearrange("(b p g) d -> b p (g d)", p=P, g=GB)
    return v[bass.ds(b, 1), :, :].rearrange("a p f -> (a p) f")


def program(nc, io, n_nodes, n_edges):
    nb, n_slots, n_rows_nodes = sizes(n_nodes, n_edges)
    n_tiles = nb * GB
    n_rows = n_slots + n_rows_nodes
    rq = n_tiles // 2
    ctx = ExitStack()
    with ctx:
        def sb(name, shape, dt=F32):
            return ctx.enter_context(nc.sbuf_tensor(name, shape, dt))

        tables = [nc.dram_tensor(f"table{n}", (n_rows, D), F32, kind="Internal").ap() for n in range(9)]
        raw = nc.dram_tensor("raw_rows", (n_rows, D), F32, kind="Internal").ap()
        row_map = nc.dram_tensor("row_map", (n_rows_nodes, 4), F32, kind="Internal").ap()

        ident = sb("ident", [P, P])
        iota = sb("iota", [P, P])
        eps = sb("eps", [P, 1])
        key = sb("key", [P, n_tiles])
        slot_node = sb("slot_node", [P, n_tiles], I32)
        src_row = sb("src_row", [P, n_tiles], I32)
        dst_row = sb("dst_row", [P, n_tiles], I32)
        cont = sb("cont", [P, n_tiles])
        single = sb("single", [P, n_tiles])
        coef = sb("coef", [P, 3, n_tiles])
        self_coef = sb("self_coef", [P, 2, n_tiles])
        ew = sb("ew", [P, 3, n_tiles])
        ew_mean = sb("ew_mean", [P, 3])
        keep = sb("keep", [rq, 2, ROW])
        pen = sb("pen", [rq, 2, ROW])
        keep2 = sb("keep2", [4, 2, rq])
        pen2 = sb("pen2", [4, 2, rq])
        seg_f = sb("seg_f", [rq, 4, ROW])
        seg_b = sb("seg_b", [rq, 4, ROW])
        seg_t = sb("seg_t", [rq, 4])
        seg_s = sb("seg_s", [4, rq])
        seg_c = sb("seg_c", [4, rq])
        bank = [ctx.enter_context(nc.psum_tensor(f"bank{k}", [P, 512], F32)) for k in range(8)]

        def segments(dve, ch, pe_sem, tr_sem, cnt, what, val):
            neutral = 0.0 if what == "sum" else -FAR
            ops = (ALU.mult, ALU.add) if what == "sum" else (ALU.add, ALU.max)
            src, src2 = (keep, keep2) if what == "sum" else (pen, pen2)
            for d, out in ((0, seg_f), (1, seg_b)):
                rev = slice(None, None, -1) if d else slice(None)
                for h in range(4):
                    ins = nc.vector.tensor_tensor_scan(out[:, h, rev], src[:, d, rev], val[:, h, rev],
                                                       neutral, *ops)
                ch.step(ins)
                edge = 0 if d else ROW - 1
                nc.vector.tensor_copy(seg_t[:, :], out[:, :, edge]).then_inc(pe_sem, 1)
                cnt[0] += 1
                dve.wait_ge(tr_sem, cnt[0])
                ch.step(nc.vector.tensor_tensor_scan(seg_s[:, rev], src2[:, d, rev],
                                                     bank[0][0:4, 0:rq][:, rev], neutral, *ops))
                ch.step(nc.vector.memset(seg_c[:, :], neutral))
                if d:
                    ins = nc.vector.tensor_copy(seg_c[:, 0:rq - 1], seg_s[:, 1:rq])
                else:
                    ins = nc.vector.tensor_copy(seg_c[:, 1:rq], seg_s[:, 0:rq - 1])
                ins.then_inc(pe_sem, 1)
                cnt[0] += 1
                dve.wait_ge(tr_sem, cnt[0])
                ch.step(nc.vector.tensor_copy(seg_t[:, :], bank[1][0:rq, 0:4]))
                for h in range(4):
                    ins = nc.vector.tensor_tensor_scan(out[:, h, rev], src[:, d, rev], val[:, h, rev],
                                                       seg_t[:, h:h + 1], *ops)
                ch.step(ins)
            if what == "sum":
                ch.step(nc.vector.tensor_tensor(seg_f[:, :, :], seg_f[:, :, :], seg_b[:, :, :], ALU.add))
                ch.step(nc.vector.tensor_tensor(seg_f[:, :, :], seg_f[:, :, :], val[:, :, :], ALU.subtract))
            else:
                ch.step(nc.vector.tensor_tensor(seg_f[:, :, :], seg_f[:, :, :], seg_b[:, :, :], ALU.max))

        def segments_pe(pe, pe_sem, tr_sem, cnt):
            for d in range(2):
                cnt[0] += 1
                pe.wait_ge(pe_sem, cnt[0])
                nc.tensor.transpose(bank[0][0:4, 0:rq], seg_t[:, :], ident[0:rq, 0:rq]).then_inc(tr_sem, 1)
                cnt[0] += 1
                pe.wait_ge(pe_sem, cnt[0])
                nc.tensor.transpose(bank[1][0:rq, 0:4], seg_c[:, :], ident[0:4, 0:4]).then_inc(tr_sem, 1)

        def edge_structure():
            with ExitStack() as c, Semaphores(nc) as sem:
                def s(name, shape, dt=F32):
                    return c.enter_context(nc.sbuf_tensor(name, shape, dt))

                di = s("di", [rq, 3, ROW], I32)
                df = s("df", [rq, 3, ROW])
                val = s("val", [rq, 4, ROW])
                pos = s("pos", [rq, ROW])
                tst = s("tst", [rq, ROW])
                isl = s("isl", [rq, ROW])
                nst = s("nst", [rq, ROW])
                kr = s("kr", [rq, ROW])
                sr = s("sr", [rq, ROW])
                fl = s("fl", [rq, 4])
                wf = s("wf", [rq, 2, 4])
                fb = s("fb", [rq, 4, P])
                ea = s("ea", [P, 8, DE])
                prod = s("prod", [P, 3, 8, DE])
                wet = s("wet", [DE, 3, D])
                wbar = s("wbar", [DE, 3])
                wb = s("wb", [DE, 3, P])
                wrow = s("wrow", [P, 3, DE])
                bem = s("bem", [P, 3, D])
                be1 = s("be1", [P, 3])
                ones = s("ones", [P, P])
                ewc = s("ewc", [P, 3, 8])
                map_new = s("map_new", [P, n_tiles, 4])
                map_def = s("map_def", [P, n_rows_nodes // P, 4])
                wp = s("wp", [P, n_tiles])
                loaded, chain, to_pe, turned, pe_done = (sem(x) for x in (
                    "loaded", "chain", "to_pe", "turned", "pe_done"))
                ea_in, ea_used, map_out, iotas, gather_go, deg_ready = (sem(x) for x in (
                    "ea_in", "ea_used", "map_out", "iotas", "gather_go", "deg_ready"))
                n_load = 10
                with nc.Block() as block:
                    @block.sync
                    def _(sp):
                        v = io["dst3"]
                        for k in range(3):
                            sp.dma_start(di[:, k, :], v[k]).then_inc(loaded, 16)
                        sp.dma_start(val[:, 0, :], io["w_rows"]).then_inc(loaded, 16)
                        sp.dma_start(wp[:, :], io["w_part"]).then_inc(loaded, 16)
                        sp.dma_start(pos[:, :], io["pos"][0:rq, :]).then_inc(loaded, 16)
                        sp.dma_start(ident[:, :], io["ident"]).then_inc(loaded, 16)
                        sp.dma_start(iota[:, :], io["iota"]).then_inc(loaded, 16)
                        sp.dma_start(wet[:, :, :], io["L0_gnn_We"].rearrange("l e h -> e l h")).then_inc(loaded, 16)
                        sp.dma_start(bem[:, :, :], io["be_all"]).then_inc(loaded, 16)
                        sp.dma_start(raw[n_slots:, :].rearrange("(p r) d -> p (r d)", p=P),
                                     io["x"].rearrange("(p r) d -> p (r d)", p=P)).then_inc(map_out, 16)
                        with sp.Fori(0, n_tiles // 8, 1) as i:
                            sp.wait_ge(ea_used, i + 1)
                            sp.dma_start(ea[:, :, :].rearrange("p a b -> p (a b)"),
                                         io["ea"][:, bass.ds(i * (8 * DE), 8 * DE)]).then_inc(ea_in, 16)
                        sp.wait_ge(iotas, 3)
                        sp.dma_start(row_map.rearrange("(p r) f -> p (r f)", p=P),
                                     map_def[:, :, :].rearrange("p r f -> p (r f)")).then_inc(map_out, 16)
                        sp.wait_ge(map_out, 32)

                    @block.gpsimd
                    def _(pool):
                        nr = n_rows_nodes // P
                        nc.gpsimd.memset(map_def[:, :, 1:4], 1.0).then_inc(iotas, 1)
                        nc.gpsimd.iota(map_def[:, :, 0], [[1, nr]], n_slots, nr,
                                       allow_small_or_imprecise_dtypes=True).then_inc(iotas, 1)
                        nc.gpsimd.iota(map_new[:, :, 0].rearrange("p (b g) -> p b g", g=GB),
                                       [[P * GB, nb], [1, GB]], 0, GB,
                                       allow_small_or_imprecise_dtypes=True).then_inc(iotas, 1)

                    @block.tensor
                    def _(pe):
                        cnt = [0]
                        pe.wait_ge(loaded, 16 * n_load)
                        for _i in range(2):
                            cnt[0] += 1
                            pe.wait_ge(to_pe, cnt[0])
                            nc.tensor.transpose(bank[2 + _i][0:4, 0:rq], wf[:, _i, :],
                                                ident[0:rq, 0:rq]).then_inc(turned, 1)
                        cnt[0] += 1
                        pe.wait_ge(to_pe, cnt[0])
                        for j in range(2):
                            nc.tensor.transpose(bank[4][:, j * rq:(j + 1) * rq], kr[:, j * P:(j + 1) * P],
                                                ident[0:rq, 0:rq])
                            nc.tensor.transpose(bank[5][:, j * rq:(j + 1) * rq], sr[:, j * P:(j + 1) * P],
                                                ident[0:rq, 0:rq])
                        for k in range(4):
                            ins = nc.tensor.matmul(bank[6][:, k * rq:(k + 1) * rq], fb[:, k, :],
                                                   ident[0:rq, 0:rq], start=True, stop=True)
                        ins.then_inc(turned, 1)
                        segments_pe(pe, to_pe, turned, cnt)
                        cnt[0] += 1
                        pe.wait_ge(to_pe, cnt[0])
                        for k in range(2):
                            for j in range(2):
                                ins = nc.tensor.transpose(bank[2][:, (2 * k + j) * rq:(2 * k + j + 1) * rq],
                                                          seg_f[:, k, j * P:(j + 1) * P], ident[0:rq, 0:rq])
                        ins.then_inc(turned, 1)
                        cnt[0] += 1
                        pe.wait_ge(to_pe, cnt[0])
                        for k in range(3):
                            ins = nc.tensor.matmul(bank[3][:, k * DE:(k + 1) * DE], wb[:, k, :],
                                                   ident[0:DE, 0:DE], start=True, stop=True)
                        ins.then_inc(turned, 1)
                        cnt[0] += 1
                        pe.wait_ge(to_pe, cnt[0])
                        nc.tensor.matmul(bank[7][:, 0:3], ones[:, :], ewc[:, :, 0], start=True,
                                         stop=True).then_inc(turned, 1)

                    @block.vector
                    def _(dve):
                        ch = Chain(dve, chain)
                        cnt = [0]
                        dve.sem_inc(ea_used, 1)
                        st = ch.step
                        dve.wait_ge(loaded, 16 * n_load)
                        st(nc.vector.tensor_copy(df[:, :, :], di[:, :, :]))
                        st(nc.vector.memset(eps[:, :], EPS))
                        st(nc.vector.memset(ones[:, :], 1.0))
                        st(nc.vector.tensor_tensor(keep[:, 0, :], df[:, 1, :], df[:, 0, :], ALU.is_equal))
                        st(nc.vector.tensor_tensor(keep[:, 1, :], df[:, 1, :], df[:, 2, :], ALU.is_equal))
                        st(nc.vector.tensor_scalar(pen[:, :, :], keep[:, :, :], 1.0, FAR, ALU.subtract, ALU.mult))
                        st(nc.vector.tensor_reduce(fl[:, 0:2], keep[:, :, :], AX.X, ALU.min))
                        for d in range(2):
                            ins = nc.vector.tensor_scalar(wf[:, d, :], ones[0:rq, 0:4], fl[:, d:d + 1], None, ALU.mult)
                            st(ins)
                        dve.sem_inc(to_pe, 1)
                        dve.sem_inc(to_pe, 1)
                        cnt[0] += 2
                        dve.wait_ge(turned, cnt[0])
                        for d in range(2):
                            st(nc.vector.tensor_copy(keep2[:, d, :], bank[2 + d][0:4, 0:rq]))
                        st(nc.vector.tensor_scalar(pen2[:, :, :], keep2[:, :, :], 1.0, FAR, ALU.subtract, ALU.mult))
                        st(nc.vector.tensor_scalar(nst[:, :], keep[:, 0, :], 1.0, None, ALU.mult))
                        st(nc.vector.memset(nst[:, :].rearrange("q (j e) -> q j e", j=2)[:, :, 0], 0.0))
                        st(nc.vector.tensor_scalar(tst[:, :], nst[:, :], -1.0, 1.0, ALU.mult, ALU.add))
                        st(nc.vector.tensor_tensor(kr[:, :], tst[:, :], pos[:, :], ALU.mult))
                        st(nc.vector.tensor_tensor_scan(sr[:, :], nst[:, :], kr[:, :], 0.0, ALU.mult, ALU.add))
                        for j in range(2):
                            a = slice(j * P, (j + 1) * P)
                            st(nc.vector.tensor_scalar(isl[:, a], df[:, 1, a], df[:, 1, (j + 1) * P - 1:(j + 1) * P],
                                                       None, ALU.is_equal))
                        st(nc.vector.tensor_scalar(kr[:, :], sr[:, :], -1.0, P - 1.0, ALU.mult, ALU.add))
                        st(nc.vector.tensor_tensor(kr[:, :], kr[:, :], isl[:, :], ALU.mult))
                        st(nc.vector.tensor_tensor(kr[:, :], kr[:, :], sr[:, :], ALU.add))
                        for j in range(2):
                            st(nc.vector.tensor_copy(fl[:, j:j + 1], keep[:, 0, j * P:j * P + 1]))
                            st(nc.vector.tensor_tensor(fl[:, 2 + j:3 + j], fl[:, j:j + 1], isl[:, j * P:j * P + 1], ALU.mult))
                        for k in range(4):
                            st(nc.vector.tensor_scalar(fb[:, k, :], ones[0:rq, :], fl[:, k:k + 1], None, ALU.mult))
                        st(nc.vector.tensor_scalar(isl[:, :], isl[:, :], -1.0, 1.0, ALU.mult, ALU.add))
                        st(nc.vector.tensor_tensor(tst[:, :], tst[:, :], isl[:, :], ALU.mult))
                        last = tst[:, :].rearrange("q (j e) -> q j e", j=2)[:, :, P - 1]
                        st(nc.vector.tensor_scalar(last, keep[:, 1, :].rearrange("q (j e) -> q j e", j=2)[:, :, P - 1],
                                                   -1.0, 1.0, ALU.mult, ALU.add))
                        st(nc.vector.tensor_scalar(sr[:, :], df[:, 1, :], BIG, None, ALU.subtract))
                        st(nc.vector.tensor_tensor(sr[:, :], sr[:, :], tst[:, :], ALU.mult))
                        st(nc.vector.tensor_scalar(sr[:, :], sr[:, :], BIG, None, ALU.add))
                        dve.sem_inc(to_pe, 1)
                        cnt[0] += 1
                        dve.wait_ge(turned, cnt[0])

                        def parts(t):
                            return t.rearrange("p (q j) -> p j q", j=2)
                        st(nc.vector.tensor_copy(parts(key[:, :]), bank[4][:, 0:2 * rq].rearrange("p (j q) -> p j q", j=2)))
                        st(nc.vector.tensor_copy(parts(slot_node[:, :]), bank[5][:, 0:2 * rq].rearrange("p (j q) -> p j q", j=2)))
                        st(nc.vector.tensor_copy(parts(cont[:, :]), bank[6][:, 0:2 * rq].rearrange("p (j q) -> p j q", j=2)))
                        st(nc.vector.tensor_copy(parts(single[:, :]), bank[6][:, 2 * rq:4 * rq].rearrange("p (j q) -> p j q", j=2)))
                        st(nc.vector.memset(val[:, 1, :], 1.0))
                        st(nc.vector.memset(val[:, 2:4, :], 0.0))
                        segments(dve, ch, to_pe, turned, cnt, "sum", val)
                        dve.sem_inc(to_pe, 1)
                        cnt[0] += 1
                        dve.wait_ge(turned, cnt[0])
                        dve.wait_ge(iotas, 3)
                        for k in range(2):
                            st(nc.vector.tensor_scalar(parts(map_new[:, :, 1 + k]),
                                                       bank[2][:, 2 * k * rq:(2 * k + 2) * rq].rearrange("p (j q) -> p j q", j=2),
                                                       1.0, None, ALU.add))
                        st(nc.vector.memset(map_new[:, :, 3], 1.0))
                        st(nc.vector.tensor_reduce(wbar[:, :], wet[:, :, :], AX.X, ALU.add))
                        for k in range(3):
                            st(nc.vector.tensor_scalar(wb[:, k, :], ones[0:DE, :], wbar[:, k:k + 1], 1.0 / D, ALU.mult, ALU.mult))
                        dve.sem_inc(to_pe, 1)
                        cnt[0] += 1
                        dve.wait_ge(turned, cnt[0])
                        st(nc.vector.tensor_copy(wrow[:, :, :].rearrange("p a b -> p (a b)"), bank[3][:, 0:3 * DE]))
                        st(nc.vector.tensor_reduce(be1[:, :], bem[:, :, :], AX.X, ALU.add))
                        st(nc.vector.tensor_scalar(be1[:, :], be1[:, :], 1.0 / D, None, ALU.mult))
                        ch2 = Chain(dve, gather_go, 2)
                        with dve.Fori(0, n_tiles // 8, 1) as i:
                            ch2.begin(Turn(i, 0, 1))
                            dve.wait_ge(ea_in, i * 16 + 16)
                            for k in range(3):
                                ins = nc.vector.tensor_tensor(prod[:, k, :, :], ea[:, :, :],
                                                              wrow[:, k:k + 1, :].to_broadcast([P, 8, DE]), ALU.mult)
                            ch2.step(ins)
                            ch2.step(nc.vector.tensor_reduce(ewc[:, :, :], prod[:, :, :, :], AX.X, ALU.add))
                            nc.vector.tensor_copy(ew[:, :, bass.ds(i * 8, 8)], ewc[:, :, :]).then_inc(ea_used, 1)
                        dve.wait_ge(ea_used, n_tiles // 8 + 1)
                        st(nc.vector.tensor_reduce(ewc[:, :, 0], ew[:, :, :], AX.X, ALU.add))
                        for k in range(3):
                            st(nc.vector.tensor_scalar(ew[:, k, :], ew[:, k, :], be1[:, k:k + 1], None, ALU.add))
                        dve.sem_inc(to_pe, 1)
                        cnt[0] += 1
                        dve.wait_ge(turned, cnt[0])
                        st(nc.vector.scalar_tensor_tensor(ew_mean[:, :], bank[7][:, 0:3], 1.0 / n_edges, be1[:, :],
                                                          ALU.mult, ALU.add))
                got = [s(f"got{k}", [P, 4]) for k in range(GB)]
                put = [s(f"put{k}", [P, 4]) for k in range(GB)]
                back = [s(f"back{k}", [P, 4, D]) for k in range(1)][0]
                ids = s("ids", [P, GB], I32)
                src_i = s("src_i", [P, n_tiles], I32)
                dst_i = s("dst_i", [P, n_tiles], I32)
                ends = s("ends", [P, 2, n_tiles, 4])
                pace, idc, taken, raw_out, in2, d3 = (sem(x) for x in ("pace", "idc", "taken", "raw_out", "in2", "d3"))
                sc_done, lk, raw_ready = (ctx.enter_context(nc.semaphore(x)) for x in ("sc_done", "lk", "raw_ready"))
                deg2 = sem("deg2")
                with nc.Block() as block:
                    @block.sync
                    def _(sp):
                        sp.dma_start(src_i[:, :], io["src_part"]).then_inc(in2, 16)
                        sp.dma_start(dst_i[:, :], io["dst_part"]).then_inc(in2, 16)
                        with sp.Fori(0, nb, 1) as i:
                            sp.wait_ge(raw_ready, i * 64 + 64)
                            sp.dma_start(batch_rows(raw, i), back[:, :, :].rearrange("p g d -> p (g d)")).then_inc(raw_out, 16)
                        sp.wait_ge(raw_out, 16 * nb + 16)

                    @block.gpsimd
                    def _(pool):
                        pool.sem_inc(raw_out, 16)
                        skip = nc.gpsimd.to_reg(n_rows_nodes - 1)
                        with pool.Fori(0, nb, 1) as i:
                            for k in range(GB):
                                nc.gpsimd.tensor_copy(put[k][:, :], map_new[:, bass.ds(i * GB + k, 1), :].rearrange("p a f -> p (a f)"))
                            nc.gpsimd.tensor_copy(ids[:, :], slot_node[:, bass.ds(i * GB, GB)]).then_inc(idc, 1)
                            pool.wait_ge(idc, i + 1)
                            pool.sem_inc(pace, 1)
                            for k in range(GB):
                                nc.gpsimd.indirect_dma_start(
                                    out=row_map, out_offset=bass.IndirectOffsetOnAxis(ap=ids[:, k:k + 1], axis=0),
                                    in_=put[k][:, :], in_offset=None, bounds_check=skip,
                                    oob_is_err=False).then_inc(sc_done, 16)
                            pool.wait_ge(sc_done, i * 64 + 64)
                            pool.sem_inc(pace, 1)
                        pool.wait_ge(in2, 32)
                        for e, idx in enumerate((src_i, dst_i)):
                            with pool.Fori(0, nb, 1) as i:
                                pool.wait_ge(taken, i * GB + (e * GB * nb + 1))
                                pool.sem_inc(pace, 1)
                                nc.gpsimd.tensor_copy(ids[:, :], idx[:, bass.ds(i * GB, GB)]).then_inc(idc, 1)
                                pool.wait_ge(idc, i + (nb * (e + 1) + 1))
                                pool.sem_inc(pace, 1)
                                for k in range(GB):
                                    nc.gpsimd.indirect_dma_start(
                                        out=got[k][:, :], out_offset=None, in_=row_map,
                                        in_offset=bass.IndirectOffsetOnAxis(ap=ids[:, k:k + 1], axis=0)).then_inc(lk, 16)
                        pool.wait_ge(taken, 2 * GB * nb + 1)
                        with pool.Fori(0, nb, 1) as i:
                            pool.wait_ge(raw_out, i * 16 + 16)
                            pool.sem_inc(pace, 1)
                            nc.gpsimd.tensor_copy(ids[:, :], dst_i[:, bass.ds(i * GB, GB)]).then_inc(idc, 1)
                            pool.wait_ge(idc, i + (nb * 3 + 1))
                            pool.sem_inc(pace, 1)
                            for k in range(GB):
                                nc.gpsimd.indirect_dma_start(
                                    out=back[:, k, :], out_offset=None, in_=io["x"],
                                    in_offset=bass.IndirectOffsetOnAxis(ap=ids[:, k:k + 1], axis=0)).then_inc(raw_ready, 16)

                    @block.vector
                    def _(dve):
                        dve.sem_inc(taken, 1)
                        for e in range(2):
                            with dve.Fori(0, nb, 1) as i:
                                dve.wait_ge(lk, i * 64 + (e * 64 * nb + 64))
                                for k in range(GB):
                                    nc.vector.tensor_copy(ends[:, e, bass.ds(i * GB + k, 1), :].rearrange("p a f -> p (a f)"),
                                                          got[k][:, :]).then_inc(taken, 1)
                        ch = Chain(dve, d3)
                        st = ch.step
                        dve.wait_ge(taken, 2 * GB * nb + 1)
                        st(nc.vector.tensor_copy(src_row[:, :], ends[:, 0, :, 0]))
                        st(nc.vector.tensor_copy(dst_row[:, :], ends[:, 1, :, 0]))
                        st(nc.vector.tensor_scalar(ends[:, :, :, 3], ends[:, :, :, 1], 0.0, None, ALU.is_gt))
                        st(nc.vector.tensor_tensor(ends[:, :, :, 1], ends[:, :, :, 1], ends[:, :, :, 3], ALU.mult))
                        st(nc.vector.scalar_tensor_tensor(ends[:, :, :, 1], ends[:, :, :, 1], 1.0, ends[:, :, :, 3], ALU.add, ALU.subtract))
                        st(nc.vector.tensor_scalar(coef[:, 2, :], ends[:, 1, :, 2], 1.0, 1.0, ALU.subtract, ALU.max))
                        st(nc.vector.reciprocal(coef[:, 2, :], coef[:, 2, :]))
                        dve.sem_inc(deg2, 1)
                        dve.wait_ge(deg2, 2)
                        st(nc.vector.reciprocal(ends[:, :, :, 1:3], ends[:, :, :, 1:3]))
                        st(nc.vector.tensor_tensor(ends[:, :, :, 1], ends[:, :, :, 1], ends[:, :, :, 3], ALU.mult))
                        for k in range(2):
                            st(nc.vector.tensor_tensor(coef[:, k, :], ends[:, 0, :, 1 + k], ends[:, 1, :, 1 + k], ALU.mult))
                            st(nc.vector.tensor_tensor(self_coef[:, k, :], ends[:, 1, :, 1 + k], ends[:, 1, :, 1 + k], ALU.mult))
                        st(nc.vector.tensor_tensor(coef[:, 0, :], coef[:, 0, :], wp[:, :], ALU.mult))

                    @block.scalar
                    def _(act):
                        act.wait_ge(deg2, 1)
                        nc.scalar.sqrt(ends[:, :, :, 1:3], ends[:, :, :, 1:3]).then_inc(deg2, 1)

        edge_structure()

        x_in = [[sb(f"x_in{u}_{r}", [P, GB, D]) for r in range(2)] for u in range(3)]
        x_res = [[sb(f"x_res{u}_{r}", [P, GB, D]) for r in range(2)] for u in range(3)]
        y = [[sb(f"y{u}_{r}", [P, GB, D]) for r in range(2)] for u in range(3)]
        x_turned = [[sb(f"x_turned{u}_{r}", [P, GB, P]) for r in range(2)] for u in range(3)]
        got = [[sb(f"got_{r}_{k}", [P, D]) for k in range(2 * GB)] for r in range(2)]
        ids = [sb(f"ids_{r}", [P, 2, GB], I32) for r in range(2)]
        pick = [sb(f"pick{r}", [P, GB, HEADS, P]) for r in range(2)]
        own = [sb(f"own{r}", [P, GB, HEADS, P]) for r in range(2)]
        agg = [sb(f"agg{r}", [P, GB, HEADS, P]) for r in range(2)]
        tails = [sb(f"tails{r}", [P, HEADS, GB + 1]) for r in range(2)]
        carried = sb("carried", [P, HEADS, GB, 2])
        now_key = [sb(f"now_key{r}", [P, GB]) for r in range(2)]
        now_flag = [sb(f"now_flag{r}", [P, GB, 2]) for r in range(2)]
        now_coef = [sb(f"now_coef{r}", [P, GB, HEADS]) for r in range(2)]
        stat6 = [[sb(f"stat6_{u}_{r}", [P, GB, 6]) for r in range(2)] for u in range(3)]
        stat = [[sb(f"stat_{u}_{r}", [P, GB, 2]) for r in range(2)] for u in range(3)]
        dev = [[sb(f"dev_{u}_{r}", [P, GB]) for r in range(2)] for u in range(3)]
        shift = [[sb(f"shift_{u}_{r}", [P, GB]) for r in range(2)] for u in range(3)]
        own_coef = [sb(f"own_coef{r}", [P, GB, HEADS]) for r in range(2)]
        w_slot = sb("w_slot", [P, HEADS, D])
        w_node = sb("w_node", [P, D])
        w_att = sb("w_att", [P, 3 * HEADS])
        att = sb("att", [P, 2, HEADS, D])
        att_p = sb("att_p", [P, 2, HEADS, D])
        affine = sb("affine", [P, 3, D])
        att_s = sb("att_s", [P, n_tiles, HEADS])
        att_d = sb("att_d", [P, n_tiles, 2 * HEADS])

        def load_weights(parts, scale_heads):
            with Semaphores(nc) as sem:
                w_in, w_chain = sem("w_in"), sem("w_chain")
                with nc.Block() as block:
                    @block.sync
                    def _(sp):
                        for dst, src in parts:
                            sp.dma_start(dst, src).then_inc(w_in, 16)
                        sp.wait_ge(w_in, 16 * len(parts))

                    @block.vector
                    def _(dve):
                        st = Chain(dve, w_chain).step
                        dve.wait_ge(w_in, 16 * len(parts))
                        if scale_heads:
                            for k in range(2):
                                st(nc.vector.tensor_tensor(att_p[:, k, :, :], w_slot[:, :, :], att[:, k, :, :], ALU.mult))
                            st(nc.vector.tensor_reduce(w_att[:, HEADS:], att_p[:, :, :, :].rearrange("p k h d -> p (k h) d"),
                                                       AX.X, ALU.add))
                            st(nc.vector.tensor_copy(w_att[:, 0:HEADS], w_att[:, HEADS:2 * HEADS]))
                            st(nc.vector.tensor_scalar(w_slot[:, :, :], w_slot[:, :, :], 1.0 / HEADS, None, ALU.mult))
                            st(nc.vector.tensor_tensor(att_p[:, 0, 0:2, :], w_slot[:, 0:2, :], w_slot[:, 2:4, :], ALU.add))
                            st(nc.vector.tensor_tensor(w_node[:, :], att_p[:, 0, 0, :], att_p[:, 0, 1, :], ALU.add))

        def rows_pass(slots, nodes, scores, inp, out, res, post, mode, result=None):
            us = ([1, 2] if nodes else []) + ([0] if slots else [])
            edges = slots and mode != "own"
            blocks = {"gat": HEADS, "sage": 2}[mode] if mode in ("gat", "sage") else 1
            summed = HEADS if mode == "gat" else 1
            with_res = post in ("norm", "gat_end")
            n_stat = {"relu": 0, "norm": 1, "gat": 1, "gat_end": 2}[post]
            gat = post in ("gat", "gat_end")
            with Semaphores(nc) as sem:
                def sems(name):
                    return [sem(f"{name}{u}") for u in range(3)]
                def rings(name):
                    return [[sem(f"{name}{u}_{r}") for r in range(2)] for u in range(3)]
                x_loaded, res_loaded, stored = rings("x_loaded"), rings("res_loaded"), rings("stored")
                turned, turned_out, y_ready, y_taken = sems("turned"), sems("turned_out"), sems("y_ready"), sems("y_taken")
                stat_ready, dev_ready, scale_ready = sems("stat_ready"), sems("dev_ready"), sems("scale_ready")
                normed, summed_up, done = sems("normed"), sems("summed_up"), sems("done")
                gathered = [ctx.enter_context(nc.semaphore(f"gathered{r}_{out.tensor.name}_{mode}_{int(slots)}")) for r in range(2)] if edges or scores else None
                now_read, picks_ready, own_ready, agg_ready, agg_out, fixed = (sem(x) for x in (
                    "now_read", "picks_ready", "own_ready", "agg_ready", "agg_out", "fixed"))
                sc_turned, sc_out, sc_ready, sc_taken = (sem(x) for x in ("sc_turned", "sc_out", "sc_ready", "sc_taken"))
                ids_ready, pool_pace, dve_pace, dve_chain, fix_chain, dve_start, act_chain = (sem(x) for x in (
                    "ids_ready", "pool_pace", "dve_pace", "dve_chain", "fix_chain", "dve_start", "act_chain"))
                last = nb // 2 - 1

                def pipeline(eng, start, body):
                    start(Turn(0, 0), Turn(0, 1))
                    with eng.Fori(0, last, 1) as i:
                        body(Turn(i, 0), Turn(i, 1), Turn(i + 1, 0))
                        body(Turn(i, 1), Turn(i + 1, 0), Turn(i + 1, 1))
                    body(Turn(last, 0), Turn(last, 1), None)
                    body(Turn(last, 1), None, None)

                def sums(k, r):
                    return bank[k][:, :] if mode == "gat" else bank[r][:, k * P:(k + 1) * P]

                tail_bank = bank[4 if mode == "gat" else 2]

                def table_batch(t, u, turn):
                    b = turn.batch()
                    return batch_rows(t, b if u == 0 else b * 2 + (nb + u - 1))

                with nc.Block() as block:
                    @block.sync
                    def _(sp):
                        def load(u, turn):
                            sp.dma_start(x_in[u][turn.half][:, :, :].rearrange("p g d -> p (g d)"),
                                         table_batch(inp, u, turn)).then_inc(x_loaded[u][turn.half], 16)

                        def load_res(u, turn):
                            sp.dma_start(x_res[u][turn.half][:, :, :].rearrange("p g d -> p (g d)"),
                                         table_batch(res, u, turn)).then_inc(res_loaded[u][turn.half], 16)

                        def store(u, turn):
                            sp.wait_ge(done[u], turn.count(1, 1))
                            b = turn.batch()
                            sp.dma_start(batch_rows(result, b * 2 + (u - 1)) if result is not None and u else table_batch(out, u, turn),
                                         y[u][turn.half][:, :, :].rearrange("p g d -> p (g d)")).then_inc(stored[u][turn.half], 16)

                        def wait_used(u, turn):
                            if post == "gat":
                                sp.wait_ge(summed_up[u], turn.count(1, 1))
                            elif post == "gat_end":
                                sp.wait_ge(stat_ready[u], turn.count(2, 2))
                            elif u == 0 and edges:
                                sp.wait_ge(agg_ready, turn.count(GB, 3 * GB))
                            else:
                                sp.wait_ge(turned[u], turn.count(1, 1))
                        for half in range(2):
                            for u in us:
                                load(u, Turn(0, half))
                                if with_res:
                                    load_res(u, Turn(0, half))
                        with sp.Fori(0, last, 1) as i:
                            for half in range(2):
                                for u in us:
                                    wait_used(u, Turn(i, half))
                                    load(u, Turn(i + 1, half))
                                if with_res:
                                    for u in us:
                                        sp.wait_ge(stat_ready[u], Turn(i, half).count(n_stat, n_stat))
                                        load_res(u, Turn(i + 1, half))
                                for u in us:
                                    store(u, Turn(i, half))
                        for half in range(2):
                            for u in us:
                                store(u, Turn(last, half))
                        for u in us:
                            for half in range(2):
                                sp.wait_ge(stored[u][half], 8 * nb + 16)

                    @block.gpsimd
                    def _(pool):
                        for u in us:
                            for half in range(2):
                                pool.sem_inc(stored[u][half], 16)
                        if not (edges or scores):
                            return
                        with pool.Fori(0, nb // 2, 1) as i:
                            for half in range(2):
                                turn = Turn(i, half)
                                if scores:
                                    pool.wait_ge(sc_turned, turn.count(1, 1))
                                else:
                                    pool.wait_ge(agg_ready, turn.count(GB, GB))
                                pool.sem_inc(pool_pace, 1)
                                nc.gpsimd.tensor_copy(ids[half][:, 0, :], src_row[:, bass.ds(turn.batch() * GB, GB)])
                                nc.gpsimd.tensor_copy(ids[half][:, 1, :], dst_row[:, bass.ds(turn.batch() * GB, GB)]).then_inc(ids_ready, 1)
                                pool.wait_ge(ids_ready, turn.count(1, 1))
                                pool.sem_inc(pool_pace, 1)
                                for e in range(2 if scores else 1):
                                    for k in range(GB):
                                        nc.gpsimd.indirect_dma_start(
                                            out=got[half][e * GB + k][:, :], out_offset=None, in_=inp,
                                            in_offset=bass.IndirectOffsetOnAxis(ap=ids[half][:, e, k:k + 1], axis=0)
                                        ).then_inc(gathered[half], 16)

                    @block.tensor
                    def _(pe):
                        if scores:
                            pe.sem_inc(sc_turned, 2)
                            pe.sem_inc(sc_ready, 2)
                        if edges:
                            pe.sem_inc(agg_ready, 2 * GB)
                        for u in us:
                            pe.sem_inc(y_ready[u], 2)

                        def turn_rows(u, turn):
                            pe.wait_ge(x_loaded[u][turn.half], turn.i * 16 + 16)
                            pe.wait_ge(turned_out[u], turn.count(1, 1))
                            for g in range(GB):
                                ins = nc.tensor.transpose(bank[2 + u][:, g * P:(g + 1) * P], x_in[u][turn.half][:, g, :], ident[:, :])
                            ins.then_inc(turned[u], 1)

                        def product(u, turn):
                            pe.wait_ge(turned_out[u], turn.count(1, 2))
                            pe.wait_ge(y_taken[u], turn.count(1, 1))
                            for g in range(GB):
                                ins = nc.tensor.matmul(bank[5 + u][:, g * D:(g + 1) * D], x_turned[u][turn.half][:, g, :],
                                                       w_node[:, :], start=True, stop=True)
                            ins.then_inc(y_ready[u], 1)

                        def sum_edges(k, turn):
                            r = turn.half
                            if k == 0:
                                pe.wait_ge(gathered[r], turn.i * 64 + 64)
                                pe.wait_ge(x_loaded[0][r], turn.i * 16 + 16)
                                pe.wait_ge(fixed, turn.count(1, 2))
                                if mode != "gat":
                                    pe.wait_ge(agg_out, turn.count(1, 2))
                            if mode == "gat":
                                pe.wait_ge(agg_out, turn.count(GB, k + 1))
                            pe.wait_ge(picks_ready, turn.count(GB, k + 1))
                            g = got[r][k]
                            if mode != "sage":
                                t = tail_bank[:, 0:HEADS * GB].rearrange("p (h k) -> p h k", k=GB)[:, 0:summed, k]
                                nc.tensor.matmul(t, g[:, :], pick[r][:, k, 0:summed, P - 1], start=True, stop=True)
                            ins = nc.tensor.matmul(sums(k, r), g[:, :], pick[r][:, k, 0:summed, :].rearrange("p h e -> p (h e)"),
                                                   start=True, stop=mode == "sage")
                            if mode == "sage":
                                ins = nc.tensor.transpose(tail_bank[:, k * P:(k + 1) * P], x_in[0][r][:, k, :], ident[:, :])
                            else:
                                pe.wait_ge(own_ready, turn.count(GB, k + 1))
                                ins = nc.tensor.matmul(sums(k, r), x_in[0][r][:, k, :],
                                                       own[r][:, k, 0:summed, :].rearrange("p h e -> p (h e)"),
                                                       start=False, stop=True)
                            ins.then_inc(agg_ready, 1)

                        def slot_products(turn):
                            pe.wait_ge(fixed, turn.count(1, 3))
                            pe.wait_ge(y_taken[0], turn.count(1, 1))
                            for k in range(GB):
                                for h in range(blocks):
                                    ins = nc.tensor.matmul(bank[5][:, k * D:(k + 1) * D], agg[turn.half][:, k, h, :], w_slot[:, h, :],
                                                           start=(h == 0), stop=(h == blocks - 1))
                            ins.then_inc(y_ready[0], 1)

                        def score_rows(turn):
                            pe.wait_ge(gathered[turn.half], turn.i * 128 + 128)
                            pe.wait_ge(sc_out, turn.count(2, 2))
                            for e in range(2):
                                for g in range(GB):
                                    ins = nc.tensor.transpose(bank[e][:, g * P:(g + 1) * P], got[turn.half][e * GB + g][:, :], ident[:, :])
                            ins.then_inc(sc_turned, 1)

                        def score_products(turn):
                            pe.wait_ge(sc_out, turn.count(2, 4))
                            pe.wait_ge(sc_taken, turn.count(1, 1))
                            for g in range(GB):
                                nc.tensor.matmul(bank[2][:, g * HEADS:(g + 1) * HEADS], agg[turn.half][:, 0, g, :], w_att[:, 0:HEADS],
                                                 start=True, stop=True)
                                ins = nc.tensor.matmul(bank[2][:, 16 + g * 8:24 + g * 8], agg[turn.half][:, 1, g, :], w_att[:, HEADS:],
                                                       start=True, stop=True)
                            ins.then_inc(sc_ready, 1)

                        def fill(turn):
                            if nodes:
                                turn_rows(1, turn)
                            if edges:
                                for k in range(GB):
                                    sum_edges(k, turn)
                            elif slots:
                                turn_rows(0, turn)
                            if scores:
                                score_rows(turn)
                            if nodes:
                                turn_rows(2, turn)

                        def body(turn, ahead, _ahead2):
                            if nodes:
                                product(1, turn)
                                product(2, turn)
                            if edges:
                                slot_products(turn)
                            elif slots:
                                product(0, turn)
                            if scores:
                                score_products(turn)
                            if ahead:
                                fill(ahead)
                        pipeline(pe, lambda first, _second: fill(first), body)

                    @block.scalar
                    def _(act):
                        if edges:
                            act.sem_inc(agg_out, GB if mode == "gat" else 2)
                        if scores:
                            act.sem_inc(sc_out, 2)
                        for u in us:
                            act.sem_inc(turned_out[u], 1)

                        def deviation(u, turn, n):
                            r = turn.half
                            act.wait_ge(stat_ready[u], turn.count(n_stat, n))
                            nc.scalar.activation(dev[u][r][:, :], stat[u][r][:, :, 1], ACT.Sqrt,
                                                 bias=eps[:, 0:1]).then_inc(dev_ready[u], 1)

                        def normalise(u, turn, n):
                            r = turn.half
                            act.wait_ge(scale_ready[u], turn.count(n_stat, n))
                            for g in range(GB):
                                ins = nc.scalar.activation(y[u][r][:, g, :], y[u][r][:, g, :], ACT.Identity,
                                                           bias=shift[u][r][:, g:g + 1], scale=dev[u][r][:, g:g + 1])
                            ins.then_inc(normed[u] if gat and n == 1 else done[u], 1)

                        def relu(u, turn, after, n):
                            act.wait_ge(after[u], turn.count(1, n))
                            yu = y[u][turn.half]
                            nc.scalar.activation(yu[:, :, :], yu[:, :, :], ACT.Relu).then_inc(done[u], 1)

                        def copy_rows(u, turn):
                            act.wait_ge(turned[u], turn.count(1, 1))
                            act.wait_ge(y_ready[u], turn.count(1, 1))
                            nc.scalar.copy(x_turned[u][turn.half][:, :, :].rearrange("p g e -> p (g e)"),
                                           bank[2 + u][:, :]).then_inc(turned_out[u], 1)

                        def build_own(turn):
                            r = turn.half
                            act.wait_ge(agg_ready, turn.count(GB, GB))
                            t = bass.ds(turn.batch() * GB, GB)
                            if mode == "gat":
                                ins = nc.scalar.copy(own_coef[r][:, :, :], att_d[:, t, 0:HEADS])
                            else:
                                ins = nc.scalar.copy(own_coef[r][:, :, 0], self_coef[:, int(mode[3]), t])
                            ins.then_inc(act_chain, 1)
                            act.wait_ge(act_chain, turn.count(1, 1))
                            for k in range(GB):
                                for h in range(summed):
                                    ins = nc.scalar.activation(own[r][:, k, h, :], ident[:, :], ACT.Copy,
                                                               scale=own_coef[r][:, k, h:h + 1])
                                ins.then_inc(own_ready, 1)

                        def copy_sums(turn):
                            r = turn.half
                            if mode == "gat":
                                for k in range(GB):
                                    act.wait_ge(agg_ready, turn.count(GB, 2 * GB + k + 1))
                                    if k == 0:
                                        act.wait_ge(y_ready[0], turn.count(1, 1))
                                    nc.scalar.copy(agg[r][:, k, :, :].rearrange("p h e -> p (h e)"), bank[k][:, :]).then_inc(agg_out, 1)
                                return
                            act.wait_ge(agg_ready, turn.count(GB, 3 * GB))
                            act.wait_ge(y_ready[0], turn.count(1, 1))
                            ins = nc.scalar.copy(agg[r][:, :, 0, :], bank[r][:, :].rearrange("p (k e) -> p k e", k=GB))
                            if mode == "sage":
                                ins = nc.scalar.copy(agg[r][:, :, 1, :], tail_bank[:, :].rearrange("p (k e) -> p k e", k=GB))
                            ins.then_inc(agg_out, 1)

                        def copies(turn):
                            if nodes:
                                copy_rows(1, turn)
                            if scores:
                                act.wait_ge(sc_turned, turn.count(1, 3))
                                act.wait_ge(sc_ready, turn.count(1, 1))
                                for e in range(2):
                                    nc.scalar.copy(agg[turn.half][:, e, :, :].rearrange("p g e -> p (g e)"),
                                                   bank[e][:, :]).then_inc(sc_out, 1)
                            if edges:
                                copy_sums(turn)
                            elif slots:
                                copy_rows(0, turn)
                            if nodes:
                                copy_rows(2, turn)

                        def start(first, second):
                            if edges and mode != "sage":
                                build_own(first)
                                build_own(second)
                            copies(first)

                        def body(turn, ahead, ahead2):
                            if edges and mode != "sage" and ahead2:
                                build_own(ahead2)
                            if ahead and not gat:
                                copies(ahead)
                            if post == "relu":
                                for u in us:
                                    relu(u, turn, y_taken, 2)
                            else:
                                for u in us:
                                    deviation(u, turn, 1)
                                for u in us:
                                    normalise(u, turn, 1)
                            if ahead and gat:
                                copies(ahead)
                            if post == "gat":
                                for u in us:
                                    relu(u, turn, summed_up, 1)
                            if post == "gat_end":
                                for u in us:
                                    deviation(u, turn, 2)
                                for u in us:
                                    normalise(u, turn, 2)
                        pipeline(act, start, body)

                    @block.vector
                    def _(dve):
                        for u in us:
                            dve.sem_inc(y_taken[u], 1)
                        if scores:
                            dve.sem_inc(sc_taken, 1)
                        per_u = {"relu": 0, "norm": 3, "gat": 4, "gat_end": 8}[post]
                        ch = Chain(dve, dve_chain, per_u * len(us))
                        fixing = Chain(dve, fix_chain, 2)
                        if edges:
                            dve.sem_inc(fixed, 2)
                            nc.vector.memset(tails[1][:, :, :], 0.0).then_inc(dve_start, 1)
                            dve.wait_ge(dve_start, 1)

                        def wide(k):
                            return affine[:, k:k + 1, :].to_broadcast([P, GB, D])

                        def statistics(u, r):
                            for g in range(GB):
                                ins = nc.vector.bn_stats(stat6[u][r][:, g, :], y[u][r][:, g, :])
                            ch.step(ins)
                            dve.sem_inc(dve_pace, 1)
                            for g in range(GB):
                                ins = nc.vector.bn_aggr(stat[u][r][:, g, :], stat6[u][r][:, g, :])
                            ins.then_inc(stat_ready[u], 1)

                        def residual(u, turn):
                            r = turn.half
                            dve.wait_ge(res_loaded[u][r], turn.i * 16 + 16)
                            ch.step(nc.vector.scalar_tensor_tensor(y[u][r][:, :, :], y[u][r][:, :, :], 0.0, x_res[u][r][:, :, :],
                                                                   ALU.max, ALU.add))
                            statistics(u, r)

                        def scale(u, turn, n):
                            r = turn.half
                            dve.wait_ge(dev_ready[u], turn.count(n_stat, n))
                            ch.step(nc.vector.reciprocal(dev[u][r][:, :], dev[u][r][:, :]))
                            nc.vector.scalar_tensor_tensor(shift[u][r][:, :], stat[u][r][:, :, 0], -1.0, dev[u][r][:, :],
                                                           ALU.mult, ALU.mult).then_inc(scale_ready[u], 1)

                        def take(u, turn):
                            r = turn.half
                            dve.wait_ge(y_ready[u], turn.count(1, 3))
                            dve.wait_ge(stored[u][r], turn.i * 16 + 16)
                            nc.vector.tensor_tensor(y[u][r][:, :, :], bank[5 + u][:, :].rearrange("p (g d) -> p g d", g=GB),
                                                    wide(0), ALU.add).then_inc(y_taken[u], 1)
                            if post == "relu":
                                return
                            dve.wait_ge(y_taken[u], turn.count(1, 2))
                            if post == "norm":
                                residual(u, turn)
                            else:
                                statistics(u, r)

                        def finish(u, turn):
                            yu = y[u][turn.half]
                            dve.wait_ge(normed[u], turn.count(1, 1))
                            ch.step(nc.vector.tensor_tensor(yu[:, :, :], yu[:, :, :], wide(1), ALU.mult))
                            ch.step(nc.vector.tensor_tensor(yu[:, :, :], yu[:, :, :], wide(2), ALU.add))
                            ins = nc.vector.tensor_tensor(yu[:, :, :], yu[:, :, :], x_in[u][turn.half][:, :, :], ALU.add)
                            if post == "gat":
                                ins.then_inc(summed_up[u], 1)
                                return
                            ch.step(ins)
                            residual(u, turn)

                        def build(turn):
                            r = turn.half
                            t = bass.ds(turn.batch() * GB, GB)
                            dve.wait_ge(agg_ready, turn.count(GB, GB))
                            nc.vector.tensor_copy(now_key[r][:, :], key[:, t])
                            nc.vector.tensor_copy(now_flag[r][:, :, 0], cont[:, t])
                            nc.vector.tensor_copy(now_flag[r][:, :, 1], single[:, t])
                            if mode == "gat":
                                ins = nc.vector.tensor_copy(now_coef[r][:, :, :], att_s[:, t, :])
                            else:
                                m = 2 if mode == "sage" else int(mode[3])
                                ins = nc.vector.tensor_copy(now_coef[r][:, :, 0], coef[:, m, t])
                            ins.then_inc(now_read, 1)
                            dve.wait_ge(now_read, turn.count(1, 1))
                            for k in range(GB):
                                for h in range(summed):
                                    ins = nc.vector.tensor_scalar(pick[r][:, k, h, :], iota[:, :], now_key[r][:, k:k + 1],
                                                                  now_coef[r][:, k, h:h + 1], ALU.is_equal, ALU.mult)
                                ins.then_inc(picks_ready, 1)

                        def fix(turn):
                            r = turn.half
                            t = tails[r]
                            if mode == "sage":
                                raw = bank[r][:, P - 1::P].rearrange("p (h k) -> p h k", h=1)
                            else:
                                raw = tail_bank[:, 0:HEADS * GB].rearrange("p (h k) -> p h k", k=GB)
                            fixing.begin(turn)
                            dve.wait_ge(agg_out, turn.count(GB, 2 * GB) if mode == "gat" else turn.count(1, 3))
                            nc.vector.tensor_copy(t[:, 0:summed, 0], tails[1 - r][:, 0:summed, GB])
                            for h in range(summed):
                                ins = nc.vector.tensor_tensor_scan(t[:, h, 1:], now_flag[r][:, :, 1], raw[:, h, :],
                                                                   tails[1 - r][:, h, GB:GB + 1], ALU.mult, ALU.add)
                            fixing.step(ins)
                            for h in range(summed):
                                ins = nc.vector.tensor_tensor(carried[:, h, :, :], now_flag[r][:, :, :],
                                                              t[:, h, 0:GB].unsqueeze(2).to_broadcast([P, GB, 2]), ALU.mult)
                            fixing.step(ins)
                            for h in range(summed):
                                ends = agg[r][:, :, h, 0::P - 1]
                                ins = nc.vector.tensor_tensor(ends, ends, carried[:, h, :, :], ALU.add)
                            ins.then_inc(fixed, 1)
                            dve.wait_ge(fixed, turn.count(1, 3))

                        def start(first, second):
                            if edges:
                                build(first)
                                build(second)
                                fix(first)

                        def body(turn, ahead, ahead2):
                            ch.begin(turn)
                            if edges and ahead2:
                                build(ahead2)
                            for u in us:
                                take(u, turn)
                            if edges and ahead and not gat:
                                fix(ahead)
                            if n_stat:
                                for u in us:
                                    scale(u, turn, 1)
                            if scores:
                                dve.wait_ge(sc_ready, turn.count(1, 3))
                                t = bass.ds(turn.batch() * GB, GB)
                                nc.vector.tensor_copy(att_s[:, t, :], bank[2][:, 0:16].rearrange("p (g h) -> p g h", g=GB))
                                nc.vector.tensor_copy(att_d[:, t, :], bank[2][:, 16:48].rearrange("p (g h) -> p g h", g=GB)).then_inc(sc_taken, 1)
                            if gat:
                                for u in us:
                                    finish(u, turn)
                            if edges and ahead and gat:
                                fix(ahead)
                            if post == "gat_end":
                                for u in us:
                                    scale(u, turn, 2)
                        pipeline(dve, start, body)

        def softmax(layer):
            with ExitStack() as c, Semaphores(nc) as sem:
                lr = c.enter_context(nc.sbuf_tensor(f"lr_{layer}", [rq, 4, ROW], F32))
                sr = c.enter_context(nc.sbuf_tensor(f"own_r_{layer}", [rq, 4, ROW], F32))
                dr = c.enter_context(nc.sbuf_tensor(f"den_r_{layer}", [rq, 4, ROW], F32))
                tmp = c.enter_context(nc.sbuf_tensor(f"tmp_p_{layer}", [P, n_tiles, HEADS], F32))
                to_pe, turned, chain, exps = (sem(x) for x in ("to_pe", "turned", "chain", "exps"))
                with nc.Block() as block:
                    @block.scalar
                    def _(act):
                        act.wait_ge(exps, 1)
                        nc.scalar.activation(lr[:, :, :], lr[:, :, :], ACT.Exp)
                        nc.scalar.activation(sr[:, :, :], sr[:, :, :], ACT.Exp).then_inc(exps, 1)

                    @block.tensor
                    def _(pe):
                        cnt = [1]
                        pe.wait_ge(to_pe, 1)
                        for e, src in ((0, att_s), (1, tmp)):
                            for h in range(HEADS):
                                for j in range(2):
                                    ins = nc.tensor.transpose(bank[2 + 2 * e + h // 2][0:rq, ((h % 2) * 2 + j) * P:((h % 2) * 2 + j + 1) * P],
                                                              src[:, :, h].rearrange("p (q j) -> p j q", j=2)[:, j, :], ident[:, :])
                        ins.then_inc(turned, 1)
                        segments_pe(pe, to_pe, turned, cnt)
                        segments_pe(pe, to_pe, turned, cnt)
                        cnt[0] += 1
                        pe.wait_ge(to_pe, cnt[0])
                        for e, src in ((0, lr), (1, sr)):
                            for h in range(HEADS):
                                for j in range(2):
                                    ins = nc.tensor.transpose(bank[2 + 2 * e + h // 2][:, ((h % 2) * 2 + j) * rq:((h % 2) * 2 + j + 1) * rq],
                                                              src[:, h, j * P:(j + 1) * P], ident[0:rq, 0:rq])
                        ins.then_inc(turned, 1)

                    @block.vector
                    def _(dve):
                        st = Chain(dve, chain)
                        ch, st = st, st.step
                        cnt = [1]
                        vd = att_d[:, :, HEADS:]
                        st(nc.vector.tensor_tensor(att_s[:, :, :], att_s[:, :, :], vd, ALU.add))
                        st(nc.vector.tensor_tensor(tmp[:, :, :], att_d[:, :, 0:HEADS], vd, ALU.add))
                        for h in range(HEADS):
                            st(nc.vector.tensor_tensor(att_s[:, :, h], att_s[:, :, h], ew[:, layer, :], ALU.add))
                        st(nc.vector.tensor_scalar(tmp[:, :, :], tmp[:, :, :], ew_mean[:, layer:layer + 1], None, ALU.add))
                        st(nc.vector.scalar_tensor_tensor(att_s[:, :, :], att_s[:, :, :], SLOPE, att_s[:, :, :], ALU.mult, ALU.max))
                        nc.vector.scalar_tensor_tensor(tmp[:, :, :], tmp[:, :, :], SLOPE, tmp[:, :, :], ALU.mult, ALU.max).then_inc(to_pe, 1)
                        dve.wait_ge(turned, 1)
                        for e, dst in ((0, lr), (1, sr)):
                            for m in range(2):
                                st(nc.vector.tensor_copy(dst[:, 2 * m:2 * m + 2, :].rearrange("q h e -> q (h e)"),
                                                         bank[2 + 2 * e + m][0:rq, :]))
                        segments(dve, ch, to_pe, turned, cnt, "max", lr)
                        st(nc.vector.tensor_tensor(seg_f[:, :, :], seg_f[:, :, :], sr[:, :, :], ALU.max))
                        st(nc.vector.tensor_tensor(lr[:, :, :], lr[:, :, :], seg_f[:, :, :], ALU.subtract))
                        nc.vector.tensor_tensor(sr[:, :, :], sr[:, :, :], seg_f[:, :, :], ALU.subtract).then_inc(exps, 1)
                        dve.wait_ge(exps, 2)
                        segments(dve, ch, to_pe, turned, cnt, "sum", lr)
                        st(nc.vector.tensor_tensor(dr[:, :, :], seg_f[:, :, :], sr[:, :, :], ALU.add))
                        st(nc.vector.reciprocal(dr[:, :, :], dr[:, :, :]))
                        st(nc.vector.tensor_tensor(lr[:, :, :], lr[:, :, :], dr[:, :, :], ALU.mult))
                        nc.vector.tensor_tensor(sr[:, :, :], sr[:, :, :], dr[:, :, :], ALU.mult).then_inc(to_pe, 1)
                        cnt[0] += 1
                        dve.wait_ge(turned, cnt[0])
                        for e, dst in ((0, att_s), (1, att_d)):
                            for h in range(HEADS):
                                o = (h % 2) * 2 * rq
                                st(nc.vector.tensor_copy(dst[:, :, h].rearrange("p (q j) -> p j q", j=2),
                                                         bank[2 + 2 * e + h // 2][:, o:o + 2 * rq].rearrange("p (j q) -> p j q", j=2)))

        t = tables
        load_weights([(w_node[:, :], io["L0_gnn_W0"]), (affine[:, 0, :], io["b_L0_b0"])], False)
        rows_pass(True, True, False, raw, t[0], None, "relu", "own")
        for l in range(3):
            load_weights([(w_slot[:, :, :], io["L0_gnn_Wg"][l].rearrange("k (h d) -> k h d", h=HEADS)),
                          (att[:, :, :, :], io["b_att"][l]), (affine[:, :, :], io["b_affine"][l])], True)
            post, res = ("gat_end", raw) if l == 2 else ("gat", None)
            rows_pass(False, True, True, t[l], t[l + 1], res, post, "gat")
            softmax(l)
            rows_pass(True, False, False, t[l], t[l + 1], res, post, "gat")
        rest = [("L1_gnn_W1", "L1_gnn_b1", "gcn0", "relu", None), ("L1_gnn_W2", "L1_gnn_b2", "gcn0", "norm", 3),
                ("L2_gnn_W", "L2_gnn_b", "gcn1", "norm", 5), ("L3_gnn_W1", "L3_gnn_b1", "sage", "relu", None),
                ("L3_gnn_W2", "L3_gnn_b2", "sage", "norm", 6)]
        for n, (w, b, mode, post, res) in enumerate(rest):
            if mode == "sage":
                parts = [(w_slot[:, 0, :], io[w][D:, :]), (w_slot[:, 1, :], io[w][0:D, :]), (w_node[:, :], io[w][0:D, :])]
            else:
                parts = [(w_slot[:, 0, :], io[w]), (w_node[:, :], io[w])]
            load_weights(parts + [(affine[:, 0, :], io["b_" + b])], False)
            rows_pass(True, True, False, t[3 + n], t[4 + n], None if res is None else t[res], post, mode,
                      io["out"] if n == len(rest) - 1 else None)
        placed = ctx.enter_context(nc.semaphore("placed"))
        with Semaphores(nc) as sem:
            idc, pace, free = (sem(x) for x in ("idc", "pace", "free"))
            loaded = [sem(f"loaded{r}") for r in range(2)]
            with nc.Block() as block:
                @block.sync
                def _(sp):
                    with sp.Fori(0, nb // 2, 1) as i:
                        for half in range(2):
                            turn = Turn(i, half)
                            sp.wait_ge(free, turn.count(1, 1))
                            sp.dma_start(x_in[0][half][:, :, :].rearrange("p g d -> p (g d)"),
                                         batch_rows(t[8], turn.batch())).then_inc(loaded[half], 16)

                @block.gpsimd
                def _(pool):
                    skip = nc.gpsimd.to_reg(n_rows_nodes - 1)
                    pool.sem_inc(free, 2)
                    with pool.Fori(0, nb // 2, 1) as i:
                        for half in range(2):
                            turn = Turn(i, half)
                            nc.gpsimd.tensor_copy(ids[half][:, 0, :], slot_node[:, bass.ds(turn.batch() * GB, GB)]).then_inc(idc, 1)
                            pool.wait_ge(idc, turn.count(1, 1))
                            pool.sem_inc(pace, 1)
                            pool.wait_ge(loaded[half], i * 16 + 16)
                            pool.sem_inc(pace, 1)
                            for k in range(GB):
                                nc.gpsimd.indirect_dma_start(
                                    out=io["out"], out_offset=bass.IndirectOffsetOnAxis(ap=ids[half][:, 0, k:k + 1], axis=0),
                                    in_=x_in[0][half][:, k, :], in_offset=None, bounds_check=skip,
                                    oob_is_err=False).then_inc(placed, 16)
                        pool.wait_ge(placed, i * 128 + 128)
                        pool.sem_inc(free, 1)
                        pool.sem_inc(free, 1)


def kernel(**inputs):
    import numpy as _np
    import concourse.bacc as _bacc
    from concourse import mybir as _mybir
    from concourse.bass_utils import run_bass_kernel_spmd as _run

    a = {k: _np.asarray(v) for k, v in inputs.items()}
    n_nodes, n_edges = a["x"].shape[0], a["src"].shape[0]
    nb, n_slots, n_rows_nodes = sizes(n_nodes, n_edges)
    assert n_rows_nodes > n_nodes
    rq, n_tiles = n_slots // ROW, n_slots // P

    def padded(v, n, fill=0):
        w = _np.full((n,) + v.shape[1:], fill, v.dtype)
        w[:v.shape[0]] = v
        return w

    def part(v):
        return _np.ascontiguousarray(_np.moveaxis(v.reshape((n_tiles, P) + v.shape[1:]), 0, 1))

    def wide(v):
        return _np.ascontiguousarray(_np.broadcast_to(v, (P,) + v.shape))
    dst = padded(a["dst"], n_slots, n_nodes)
    around = _np.full(n_slots + 2, -1, dst.dtype)
    around[1:-1] = dst
    src = padded(a["src"], n_slots)
    w = padded(a["edge_weight"], n_slots)
    io = {
        "x": padded(a["x"], n_rows_nodes),
        "dst3": _np.stack([around[:-2], around[1:-1], around[2:]]).reshape(3, rq, ROW),
        "w_rows": w.reshape(rq, ROW), "w_part": part(w), "src_part": part(src), "dst_part": part(dst),
        "ea": part(padded(a["edge_attr_64"], n_slots)).reshape(P, n_tiles * DE),
        "ident": _np.eye(P, dtype=_np.float32),
        "iota": wide(_np.arange(P, dtype=_np.float32)),
        "pos": wide(_np.arange(ROW, dtype=_np.float32) % P),
        "L0_gnn_We": a["L0_gnn_We"], "be_all": wide(a["L0_gnn_be"]),
        "L0_gnn_W0": a["L0_gnn_W0"], "b_L0_b0": wide(a["L0_gnn_b0"]), "L0_gnn_Wg": a["L0_gnn_Wg"],
        "b_att": _np.stack([wide(_np.stack([a["L0_gnn_att_src"][l], a["L0_gnn_att_dst"][l]])) for l in range(3)]),
        "b_affine": _np.stack([wide(_np.stack([a["L0_gnn_" + k][l] for k in ("bg", "gamma", "beta")])) for l in range(3)]),
        "L1_gnn_W1": _np.ascontiguousarray(a["L1_gnn_W1"].T), "L1_gnn_W2": _np.ascontiguousarray(a["L1_gnn_W2"].T),
        "L2_gnn_W": a["L2_gnn_W"], "L3_gnn_W1": a["L3_gnn_W1"], "L3_gnn_W2": a["L3_gnn_W2"],
    }
    for k in ("L1_gnn_b1", "L1_gnn_b2", "L2_gnn_b", "L3_gnn_b1", "L3_gnn_b2"):
        io["b_" + k] = wide(a[k])
    nc = _bacc.Bacc("TRN2", target_bir_lowering=False, num_devices=1)
    arrays = {f"in_{k}_dram": _np.ascontiguousarray(v) for k, v in io.items()}
    aps = {k: nc.dram_tensor(f"in_{k}_dram", v.shape, _mybir.dt.from_np(v.dtype), kind="ExternalInput").ap()
           for k, v in io.items()}
    aps["out"] = nc.dram_tensor("out_0_dram", (n_rows_nodes, D), _mybir.dt.float32, kind="ExternalOutput").ap()
    program(nc, aps, n_nodes, n_edges)
    r = _run(nc, [arrays], core_ids=[0])
    return r.results[0]["out_0_dram"][:n_nodes]
```
